# Optimizing a Trainium2 kernel written in Bass

```python
import numpy as np
import jax
import jax.numpy as jnp

def _softmax(x, axis=-1):
    return jax.nn.softmax(x, axis=axis)

def _gelu(x):
    return jax.nn.gelu(x, approximate=True)

def _silu(x):
    return jax.nn.silu(x)

def _sigmoid(x):
    return jax.nn.sigmoid(x)

def _layernorm(x, axis=-1, eps=1e-05):
    m = jnp.mean(x, axis=axis, keepdims=True)
    v = jnp.var(x, axis=axis, keepdims=True)
    return (x - m) / jnp.sqrt(v + eps)

def _scatter_add(tgt, idx, src, axis=0):
    return tgt.at[idx].add(src)

def _segment_sum(src, seg, n):
    return jax.ops.segment_sum(src, seg, n)
kernel_name = 'mk_adaln_ffn_d2_seqx_r4_9c569e'

def setup_inputs(seed: int=0):
    np.random.seed(seed)
    _w = jnp.asarray

    def _rec_inputs():
        import jax
        import jax.numpy as jnp
        _rk = jax.random.key(seed)
        x = -7.109e-05 + 0.9999 * jax.random.normal(jax.random.fold_in(_rk, 1), (8, 256, 256), jnp.float32)
        _lenS = 256 - jax.random.randint(jax.random.fold_in(_rk, 7), (8,), 0, max(1, 256 // 4) + 1, jnp.int32)
        _lenS2 = 256 - jax.random.randint(jax.random.fold_in(_rk, 8), (8,), 0, max(1, 256 // 4) + 1, jnp.int32)
        itok_B_0_8 = jax.random.randint(jax.random.fold_in(_rk, 11), (8,), 0, 9, jnp.int32)
        itok_B_0_6 = jax.random.randint(jax.random.fold_in(_rk, 12), (8,), 0, 7, jnp.int32)
        return (x, itok_B_0_8, itok_B_0_6)
    x, itok_B_0_8, itok_B_0_6 = _rec_inputs()

    def _L0_cond_setup():
        import jax, jax.numpy as jnp
        import numpy as np
        LN_EPS = 1e-05
        key = jax.random.key(seed)
        ks = jax.random.split(key, 8)
        B, S, H, A, L = (32, 512, 256, 64, 10)
        return {'hidden_states': jax.random.normal(ks[0], (B, S, H), dtype=jnp.float32), 'language_ids': jax.random.randint(ks[1], (B,), 0, L, dtype=jnp.int64), 'W1': jax.random.normal(ks[2], (L, H, A), dtype=jnp.float32) * (1.0 / np.sqrt(H)), 'b1': jnp.zeros((L, A), dtype=jnp.float32), 'W2': jax.random.normal(ks[3], (L, A, H), dtype=jnp.float32) * (1.0 / np.sqrt(A)), 'b2': jnp.zeros((L, H), dtype=jnp.float32), 'gamma': jnp.ones((L, H), dtype=jnp.float32), 'beta': jnp.zeros((L, H), dtype=jnp.float32)}
    _L0_cond_all = _L0_cond_setup()
    _L0_cond_in = {k: v for k, v in _L0_cond_all.items() if k in ('W1', 'b1', 'W2', 'b2', 'gamma', 'beta')}
    del _L0_cond_all

    def _L0_ffn_setup():
        import jax, jax.numpy as jnp
        import numpy as np
        B, S, D_MODEL, D_HIDDEN = (4, 512, 256, 1024)

        def act_quant(x):
            scale = 127.0 / jnp.clip(jnp.max(jnp.abs(x), axis=-1, keepdims=True), 1e-05)
            return jnp.clip(jnp.round(x * scale), -128, 127) / scale

        def weight_quant(w):
            scale = 1.0 / jnp.clip(jnp.mean(jnp.abs(w)), 1e-05)
            return jnp.clip(jnp.round(w * scale), -1, 1) / scale

        def bit_linear(x, w):
            xq = x + jax.lax.stop_gradient(act_quant(x) - x)
            wq = w + jax.lax.stop_gradient(weight_quant(w) - w)
            return jnp.einsum('bsd,hd->bsh', xq, wq)

        def depthwise_conv1d(x_bcl, w, b):
            y = jax.lax.conv_general_dilated(x_bcl, w, window_strides=(1,), padding=[(1, 1)], dimension_numbers=('NCH', 'OIH', 'NCH'), feature_group_count=x_bcl.shape[1])
            return y + b[None, :, None]
        key = jax.random.key(seed)
        ks = jax.random.split(key, 5)
        lim1 = 1.0 / np.sqrt(D_MODEL)
        lim2 = 1.0 / np.sqrt(D_HIDDEN)
        limc = 1.0 / np.sqrt(3.0)
        return {'x': jax.random.normal(ks[0], (B, S, D_MODEL), dtype=jnp.float32), 'w1': jax.random.uniform(ks[1], (D_HIDDEN, D_MODEL), jnp.float32, -lim1, lim1), 'conv_w': jax.random.uniform(ks[2], (D_HIDDEN, 1, 3), jnp.float32, -limc, limc), 'conv_b': jax.random.uniform(ks[3], (D_HIDDEN,), jnp.float32, -limc, limc), 'w2': jax.random.uniform(ks[4], (D_MODEL, D_HIDDEN), jnp.float32, -lim2, lim2)}
    _L0_ffn_all = _L0_ffn_setup()
    _L0_ffn_in = {k: v for k, v in _L0_ffn_all.items() if k in ('w1', 'conv_w', 'conv_b', 'w2')}
    del _L0_ffn_all

    def _L1_cond_setup():
        import jax, jax.numpy as jnp
        import numpy as np
        N_PROFILES = 8
        HIDDEN = 256
        BOTTLENECK = 128
        EPS = 1e-05
        key = jax.random.key(seed)
        ks = jax.random.split(key, 8)
        B, S, H, K, P = (16, 512, HIDDEN, BOTTLENECK, N_PROFILES)
        down_w = jax.random.normal(ks[0], (P, H, K), dtype=jnp.float32) * (1.0 / np.sqrt(H))
        down_b = jax.random.normal(ks[1], (P, K), dtype=jnp.float32) * 0.01
        up_w = jax.random.normal(ks[2], (P, K, H), dtype=jnp.float32) * (1.0 / np.sqrt(K))
        up_b = jax.random.normal(ks[3], (P, H), dtype=jnp.float32) * 0.01
        ln_g = jnp.ones((P, H), dtype=jnp.float32)
        ln_b = jnp.zeros((P, H), dtype=jnp.float32)
        hidden = jax.random.normal(ks[4], (B, S, H), dtype=jnp.float32)
        profile_ids = jax.random.randint(ks[5], (B,), 0, P)
        return {'hidden': hidden, 'profile_ids': profile_ids, 'down_w': down_w, 'down_b': down_b, 'up_w': up_w, 'up_b': up_b, 'ln_g': ln_g, 'ln_b': ln_b}
    _L1_cond_all = _L1_cond_setup()
    _L1_cond_in = {k: v for k, v in _L1_cond_all.items() if k in ('down_w', 'down_b', 'up_w', 'up_b', 'ln_g', 'ln_b')}
    del _L1_cond_all

    def _L1_ffn_setup():
        import jax, jax.numpy as jnp
        import numpy as np
        from jax import lax
        TOP_K = 4
        N_GROUP = 4
        TOPK_GROUP = 2
        ROUTED_SCALE = 2.5
        NEG_INF = -1000000000.0

        def _route(xf, router_weight, router_bias):
            T = xf.shape[0]
            E = router_weight.shape[0]
            logits = xf @ router_weight.T
            scores = jax.nn.sigmoid(logits)
            s_choice = scores + router_bias
            per_group = E // N_GROUP
            sg = s_choice.reshape(T, N_GROUP, per_group)
            group_scores = lax.top_k(sg, 2)[0].sum(-1)
            _, gidx = lax.top_k(group_scores, TOPK_GROUP)
            gmask = jnp.zeros((T, N_GROUP), dtype=bool).at[jnp.arange(T)[:, None], gidx].set(True)
            masked = jnp.where(gmask[:, :, None], sg, NEG_INF).reshape(T, E)
            _, topk_idx = lax.top_k(masked, TOP_K)
            w = jnp.take_along_axis(scores, topk_idx, axis=1)
            w = w / (w.sum(-1, keepdims=True) + 1e-20) * ROUTED_SCALE
            combine = jnp.zeros((T, E), dtype=xf.dtype).at[jnp.arange(T)[:, None], topk_idx].add(w)
            return combine
        key = jax.random.key(seed)
        ks = jax.random.split(key, 6)
        B, S, H, I, E = (2, 512, 256, 128, 16)
        x = jax.random.normal(ks[0], (B, S, H), dtype=jnp.float32)
        router_weight = jax.random.normal(ks[1], (E, H), dtype=jnp.float32) * 0.02
        router_bias = jnp.zeros((E,), dtype=jnp.float32)
        w_gate = jax.random.normal(ks[2], (E, I, H), dtype=jnp.float32) * 0.02
        w_up = jax.random.normal(ks[3], (E, I, H), dtype=jnp.float32) * 0.02
        w_down = jax.random.normal(ks[4], (E, H, I), dtype=jnp.float32) * 0.02
        return {'x': x, 'router_weight': router_weight, 'router_bias': router_bias, 'w_gate': w_gate, 'w_up': w_up, 'w_down': w_down}
    _L1_ffn_all = _L1_ffn_setup()
    _L1_ffn_in = {k: v for k, v in _L1_ffn_all.items() if k in ('router_weight', 'router_bias', 'w_gate', 'w_up', 'w_down')}
    del _L1_ffn_all
    return {'x': x, 'itok_B_0_8': itok_B_0_8, 'itok_B_0_6': itok_B_0_6, 'L0_cond_W1': _L0_cond_in['W1'], 'L0_cond_b1': _L0_cond_in['b1'], 'L0_cond_W2': _L0_cond_in['W2'], 'L0_cond_b2': _L0_cond_in['b2'], 'L0_cond_gamma': _L0_cond_in['gamma'], 'L0_cond_beta': _L0_cond_in['beta'], 'L0_ffn_w1': _L0_ffn_in['w1'], 'L0_ffn_conv_w': _L0_ffn_in['conv_w'], 'L0_ffn_conv_b': _L0_ffn_in['conv_b'], 'L0_ffn_w2': _L0_ffn_in['w2'], 'L1_cond_down_w': _L1_cond_in['down_w'], 'L1_cond_down_b': _L1_cond_in['down_b'], 'L1_cond_up_w': _L1_cond_in['up_w'], 'L1_cond_up_b': _L1_cond_in['up_b'], 'L1_cond_ln_g': _L1_cond_in['ln_g'], 'L1_cond_ln_b': _L1_cond_in['ln_b'], 'L1_ffn_router_weight': _L1_ffn_in['router_weight'], 'L1_ffn_router_bias': _L1_ffn_in['router_bias'], 'L1_ffn_w_gate': _L1_ffn_in['w_gate'], 'L1_ffn_w_up': _L1_ffn_in['w_up'], 'L1_ffn_w_down': _L1_ffn_in['w_down']}

def reference(x, itok_B_0_8, itok_B_0_6, L0_cond_W1, L0_cond_b1, L0_cond_W2, L0_cond_b2, L0_cond_gamma, L0_cond_beta, L0_ffn_w1, L0_ffn_conv_w, L0_ffn_conv_b, L0_ffn_w2, L1_cond_down_w, L1_cond_down_b, L1_cond_up_w, L1_cond_up_b, L1_cond_ln_g, L1_cond_ln_b, L1_ffn_router_weight, L1_ffn_router_bias, L1_ffn_w_gate, L1_ffn_w_up, L1_ffn_w_down):
    import jax
    import jax.numpy as jnp

    def _L0_cond_ref(hidden_states, language_ids, W1, b1, W2, b2, gamma, beta):
        import jax, jax.numpy as jnp
        import numpy as np
        LN_EPS = 1e-05
        w1 = W1[language_ids]
        w2 = W2[language_ids]
        h = jnp.einsum('bsh,bha->bsa', hidden_states, w1) + b1[language_ids][:, None, :]
        h = jax.nn.relu(h)
        adapted = jnp.einsum('bsa,bah->bsh', h, w2) + b2[language_ids][:, None, :]
        x = hidden_states + adapted
        mean = jnp.mean(x, axis=-1, keepdims=True)
        var = jnp.mean(jnp.square(x - mean), axis=-1, keepdims=True)
        normed = (x - mean) * jax.lax.rsqrt(var + LN_EPS)
        return normed * gamma[language_ids][:, None, :] + beta[language_ids][:, None, :]

    def _L0_ffn_ref(x, w1, conv_w, conv_b, w2):
        import jax, jax.numpy as jnp
        import numpy as np
        B, S, D_MODEL, D_HIDDEN = (4, 512, 256, 1024)

        def act_quant(x):
            scale = 127.0 / jnp.clip(jnp.max(jnp.abs(x), axis=-1, keepdims=True), 1e-05)
            return jnp.clip(jnp.round(x * scale), -128, 127) / scale

        def weight_quant(w):
            scale = 1.0 / jnp.clip(jnp.mean(jnp.abs(w)), 1e-05)
            return jnp.clip(jnp.round(w * scale), -1, 1) / scale

        def bit_linear(x, w):
            xq = x + jax.lax.stop_gradient(act_quant(x) - x)
            wq = w + jax.lax.stop_gradient(weight_quant(w) - w)
            return jnp.einsum('bsd,hd->bsh', xq, wq)

        def depthwise_conv1d(x_bcl, w, b):
            y = jax.lax.conv_general_dilated(x_bcl, w, window_strides=(1,), padding=[(1, 1)], dimension_numbers=('NCH', 'OIH', 'NCH'), feature_group_count=x_bcl.shape[1])
            return y + b[None, :, None]
        h = bit_linear(x, w1)
        h = depthwise_conv1d(h.transpose(0, 2, 1), conv_w, conv_b)
        h = h.transpose(0, 2, 1)
        h = jax.nn.silu(h)
        return bit_linear(h, w2)

    def _L1_cond_ref(hidden, profile_ids, down_w, down_b, up_w, up_b, ln_g, ln_b):
        import jax, jax.numpy as jnp
        import numpy as np
        N_PROFILES = 8
        HIDDEN = 256
        BOTTLENECK = 128
        EPS = 1e-05
        Wd = down_w[profile_ids]
        bd = down_b[profile_ids][:, None]
        Wu = up_w[profile_ids]
        bu = up_b[profile_ids][:, None]
        g = ln_g[profile_ids][:, None]
        b = ln_b[profile_ids][:, None]
        z = jax.nn.relu(jnp.einsum('bsh,bhk->bsk', hidden, Wd) + bd)
        y = hidden + jnp.einsum('bsk,bkh->bsh', z, Wu) + bu
        mu = jnp.mean(y, axis=-1, keepdims=True)
        var = jnp.mean(jnp.square(y - mu), axis=-1, keepdims=True)
        return (y - mu) * jax.lax.rsqrt(var + EPS) * g + b

    def _L1_ffn_ref(x, router_weight, router_bias, w_gate, w_up, w_down):
        import jax, jax.numpy as jnp
        import numpy as np
        from jax import lax
        TOP_K = 4
        N_GROUP = 4
        TOPK_GROUP = 2
        ROUTED_SCALE = 2.5
        NEG_INF = -1000000000.0

        def _route(xf, router_weight, router_bias):
            T = xf.shape[0]
            E = router_weight.shape[0]
            logits = xf @ router_weight.T
            scores = jax.nn.sigmoid(logits)
            s_choice = scores + router_bias
            per_group = E // N_GROUP
            sg = s_choice.reshape(T, N_GROUP, per_group)
            group_scores = lax.top_k(sg, 2)[0].sum(-1)
            _, gidx = lax.top_k(group_scores, TOPK_GROUP)
            gmask = jnp.zeros((T, N_GROUP), dtype=bool).at[jnp.arange(T)[:, None], gidx].set(True)
            masked = jnp.where(gmask[:, :, None], sg, NEG_INF).reshape(T, E)
            _, topk_idx = lax.top_k(masked, TOP_K)
            w = jnp.take_along_axis(scores, topk_idx, axis=1)
            w = w / (w.sum(-1, keepdims=True) + 1e-20) * ROUTED_SCALE
            combine = jnp.zeros((T, E), dtype=xf.dtype).at[jnp.arange(T)[:, None], topk_idx].add(w)
            return combine
        B, S, H = x.shape
        E = w_gate.shape[0]
        xf = x.reshape(-1, H)
        combine = _route(xf, router_weight, router_bias)
        out = jnp.zeros_like(xf)
        for e in range(E):
            g = xf @ w_gate[e].T
            u = xf @ w_up[e].T
            y_e = jax.nn.silu(g) * u @ w_down[e].T
            out = out + combine[:, e:e + 1] * y_e
        return out.reshape(B, S, H)
    x = x + _L0_ffn_ref(_L0_cond_ref(x, itok_B_0_8, L0_cond_W1, L0_cond_b1, L0_cond_W2, L0_cond_b2, L0_cond_gamma, L0_cond_beta), L0_ffn_w1, L0_ffn_conv_w, L0_ffn_conv_b, L0_ffn_w2)
    x = x + _L1_ffn_ref(_L1_cond_ref(x, itok_B_0_6, L1_cond_down_w, L1_cond_down_b, L1_cond_up_w, L1_cond_up_b, L1_cond_ln_g, L1_cond_ln_b), L1_ffn_router_weight, L1_ffn_router_bias, L1_ffn_w_gate, L1_ffn_w_up, L1_ffn_w_down)
    return x

_drawn_inputs = setup_inputs


def setup_inputs(seed=0):
    import zlib

    import numpy as np

    out = dict(_drawn_inputs(seed))
    spreads = {'L0_cond_b1': (0.0, 0.8),
     'L0_cond_b2': (0.0, 0.8),
     'L0_cond_gamma': (1.0, 0.6),
     'L0_cond_beta': (0.0, 0.8),
     'L1_cond_ln_g': (1.0, 0.6),
     'L1_cond_ln_b': (0.0, 0.8),
     'L1_ffn_router_bias': (0.0, 0.511)}
    factors = {'L1_cond_down_w': 4.37,
     'L1_cond_down_b': 8.0,
     'L1_cond_up_w': 4.048,
     'L1_cond_up_b': 8.0,
     'L1_ffn_router_weight': 4.59,
     'L1_ffn_w_gate': 3.385,
     'L1_ffn_w_up': 3.302,
     'L1_ffn_w_down': 3.289}
    for name, (base, spread) in spreads.items():
        noise = np.random.default_rng([zlib.crc32(name.encode()), seed]).standard_normal(out[name].shape)
        drawn = base * np.exp(spread * noise) if base else spread * noise
        out[name] = jnp.asarray(drawn.astype(out[name].dtype))
    for name, factor in factors.items():
        out[name] = (out[name] * factor).astype(out[name].dtype)
    return out
```

```python
from contextlib import ExitStack

import concourse.bass as bass
from concourse import mybir

ALU = mybir.AluOpType
ACT = mybir.ActivationFunctionType
AX_X = mybir.AxisListType.X
F32 = mybir.dt.float32
BF16 = mybir.dt.bfloat16
I32 = mybir.dt.int32
U32 = mybir.dt.uint32

P = 128
MAGIC = 1.5 * 2.0 ** 23
LN_EPS = 1e-5
QUANT_MIN = 1e-5
QMAX = 127.0
INV_E = 0.36787944117144233
GROUPS, GROUPS_KEPT, TOP_K = 4, 2, 4
NEG_INF = -1e9
ROUTED_SCALE = 2.5


def build(nc, x, xT, id0, id1, l0_w1, l0_b1, l0_w2b2, l0_gamma, l0_beta, w1T, conv, w2T,
          l1_down, l1_down_b, l1_up, l1_up_b, l1_gamma, l1_beta, routerT, router_bias,
          gate_upT, downT, out, sent, done):
    NB, S, D = x.shape
    TOK = NB * S
    NT = TOK // P
    TB = S // P
    DK = D // P
    A0 = l0_w1.shape[2]
    A1 = l1_down.shape[2]
    F = w1T.shape[1]
    FC = F // P
    NP = FC // 2
    E = routerT.shape[1]
    HI = downT.shape[0]
    ROW = sent.shape[1]
    REGION = TOK + P
    HT = NT // 2
    HB = NB // 2
    assert A1 == P and HI == P and TB == 2 and DK == 2
    LIVE = (TOP_K * TOK + E * (P - 1)) // P
    RING = 8
    TILES = (LIVE + RING - 1) // RING * RING

    with ExitStack() as ctx:
        def sb(name, shape, dt=F32):
            return ctx.enter_context(nc.sbuf_tensor(name, shape, dt))

        def ps(name, cols):
            return ctx.enter_context(nc.psum_tensor(name, [P, cols], F32))

        def sem(name):
            return ctx.enter_context(nc.semaphore(name))

        p_pair = [ps(f"p_pair{n}", 512) for n in range(2)]
        p_tok = ps("p_tok", 2048)
        p_a = ps("p_a", 512)
        p_c = ps("p_c", 512)

        ident = sb("ident", [P, P])
        ones = sb("ones", [P, P])
        ones_b = sb("ones_b", [P, P], BF16)
        before = sb("before", [P, P], BF16)
        ternary1 = sb("ternary1", [P, DK, F], BF16)
        ternary2 = sb("ternary2", [P, FC, D], BF16)
        convs = sb("convs", [P, FC, 4])
        wstat = sb("wstat", [P, 2])
        wmean = sb("wmean", [P, 2])
        wscale = sb("wscale", [P, 2])
        wdeq = sb("wdeq", [P, 2])
        gate_up = sb("gate_up", [P, E, DK, 2 * HI])
        down = sb("down", [P, E, D])
        router = sb("router", [P, DK, E])
        rbias = sb("rbias", [P, E])

        xs = sb("xs", [P, NT, D])
        xTb = [sb(f"xTb{n}", [P, DK, S]) for n in range(2)]
        w1b = [sb(f"w1b{n}", [P, DK, A0]) for n in range(2)]
        w2b = [sb(f"w2b{n}", [A0 + 1, D]) for n in range(2)]
        b1b = [sb(f"b1b{n}", [A0, 1]) for n in range(2)]
        ga0 = [sb(f"ga0_{n}", [P, D]) for n in range(2)]
        be0 = [sb(f"be0_{n}", [P, D]) for n in range(2)]
        hT = sb("hT", [A0 + 1, S])
        ya = sb("ya", [P, TB, D])
        bn_a = sb("bn_a", [P, TB, 6])
        mv_a = sb("mv_a", [P, TB, 2])
        rstd_a = sb("rstd_a", [P, TB])
        q1 = sb("q1", [P, 4, TB])
        za = sb("za", [P, TB, D])
        rb = sb("rb", [P, TB, P])
        qT = [sb(f"qT{n}", [P, DK, S], BF16) for n in range(2)]
        deq_bc = [sb(f"deq_bc{n}", [P, S]) for n in range(2)]
        gb = [sb(f"gb{n}", [P, 2, S + 2]) for n in range(2)]
        cb = [sb(f"cb{n}", [P, 2, S]) for n in range(2)]
        sbuf_s = [sb(f"act{n}", [P, FC, S]) for n in range(2)]
        q2 = sb("q2", [P, 4, TB])
        zb = sb("zb", [P, TB, F])
        q2T = sb("q2T", [P, FC, S], BF16)

        wdn = [sb(f"wdn{n}", [P, DK, A1]) for n in range(2)]
        wup = [sb(f"wup{n}", [P, D]) for n in range(2)]
        bdn = [sb(f"bdn{n}", [P, 1]) for n in range(2)]
        bup = [sb(f"bup{n}", [P, D]) for n in range(2)]
        ga1 = [sb(f"ga1_{n}", [P, D]) for n in range(2)]
        be1 = [sb(f"be1_{n}", [P, D]) for n in range(2)]
        x1b = sb("x1b", [P, TB, D])
        x1T = sb("x1T", [P, DK, S])
        zk = sb("zk", [P, S])
        yk = sb("yk", [P, TB, D])
        bn_c = sb("bn_c", [P, TB, 6])
        mv_c = sb("mv_c", [P, TB, 2])
        rstd_c = sb("rstd_c", [P, TB])
        xf = sb("xf", [P, TB, D])
        xfT = sb("xfT", [P, DK, S])
        half = sb("half", [P, NT])
        inv_e = sb("inv_e", [P, HT * E])

        lg = sb("lg", [P, NT, E])
        ex = sb("ex", [P, HT, E])
        score = sb("score", [P, HT, E])
        choice = sb("choice", [P, HT, E])
        g_hi = sb("g_hi", [P, HT * GROUPS, 2])
        g_lo = sb("g_lo", [P, HT * GROUPS, 2])
        g_t = sb("g_t", [P, 3, HT * GROUPS])
        g_sum = sb("g_sum", [P, HT, GROUPS])
        g_gt = sb("g_gt", [P, HT, GROUPS, GROUPS])
        g_ge = sb("g_ge", [P, HT, GROUPS, GROUPS])
        g_first = sb("g_first", [P, HT, GROUPS, GROUPS])
        g_rank = sb("g_rank", [P, HT, GROUPS])
        g_mask = sb("g_mask", [P, HT, GROUPS])
        g_pen = sb("g_pen", [P, HT, GROUPS])
        masked = sb("masked", [P, HT, E])
        top8 = sb("top8", [P, HT, 8])
        idx8 = sb("idx8", [P, HT, 8], U32)
        idxf = sb("idxf", [P, HT, TOP_K])
        iota_e = sb("iota_e", [P, E])
        iota_region = sb("iota_region", [P, E])
        onehot = sb("onehot", [P, HT, TOP_K, E])
        picked = sb("picked", [P, HT, TOP_K, E])
        mask_b = sb("mask_b", [P, NT, E], BF16)
        wk = sb("wk", [P, HT, TOP_K])
        wsum = sb("wsum", [P, HT])
        pos = sb("pos", [P, HT, E])
        dest_f = sb("dest_f", [P, HT, TOP_K])
        dest = sb("dest", [P, NT, TOP_K], I32)
        slot_id = sb("slot_id", [P, NT, TOP_K], I32)
        rows = sb("rows", [P, HT, TOP_K, ROW])
        pad = sb("pad", [P, ROW])
        cnt = sb("cnt", [1, 4, E])
        cnt_i = sb("cnt_i", [1, E], I32)
        zrow = sb("zrow", [1, E])
        tj = sb("tj", [1, TILES])
        t_mask, t_prod = (sbuf_s[n][0:1, :, :].rearrange("a c t -> a (c t)")[:, 0:TILES * E].rearrange(
            "a (t e) -> a t e", e=E) for n in range(2))
        t_f = sb("t_f", [1, 3, TILES])
        t_exp = sb("t_exp", [1, TILES], I32)
        t_row = sb("t_row", [1, TILES], I32)

        xr = [sbuf_s[n // 4][:, 2 * (n % 4):2 * (n % 4) + 2, :].rearrange("p a b -> p (a b)")[:, 0:ROW] for n in range(RING)]
        yr = [zb[:, n // 4, (n % 4) * D:(n % 4 + 1) * D] for n in range(RING)]
        xTe = [x1T[:, :, n * P:(n + 1) * P] for n in range(2)]
        sg = [yk[:, n, 0:HI] for n in range(2)]
        he = [ya[:, n, 0:HI] for n in range(2)]
        hTe = [za[:, n, 0:HI] for n in range(2)]
        slots = [rows[:, 2 * n:2 * n + 1, :, 0:D] for n in range(4)]

        s_const = sem("s_const"); s_ident = sem("s_ident"); s_iota = sem("s_iota")
        s_w1 = sem("s_w1"); s_w2 = sem("s_w2"); s_small = sem("s_small"); s_ew = sem("s_ew")
        s_x = [sem(f"s_in{n}") for n in range(2)]
        s_p0 = [sem(f"s_p0_{n}") for n in range(2)]
        s_p1 = [sem(f"s_p1_{n}") for n in range(2)]
        s_dve = sem("s_dve")
        s_wsum = sem("s_wsum"); s_wtot = sem("s_wtot"); s_tern = sem("s_tern")
        s_hT = sem("s_hT"); s_hr = sem("s_hr"); s_ya = sem("s_ya"); s_mva = sem("s_mva")
        s_rsa = sem("s_rsa"); s_q1 = sem("s_q1"); s_za = sem("s_za"); s_rb = sem("s_rb")
        s_zaT = sem("s_zaT"); s_qT = sem("s_qT"); s_rbT = sem("s_rbT"); s_deq = sem("s_deq")
        s_h = sem("s_h"); s_g = sem("s_g"); s_c0 = sem("s_c0"); s_tap = sem("s_tap"); s_silu = sem("s_silu")
        s_sT = sem("s_sT"); s_q2 = sem("s_q2"); s_zb = sem("s_zb"); s_zbT = sem("s_zbT")
        s_q2d = sem("s_q2d"); s_q2a = sem("s_q2a"); s_y2 = sem("s_y2"); s_x1 = sem("s_x1")
        s_x1b = sem("s_x1b"); s_x1T = sem("s_x1T"); s_x1Te = sem("s_x1Te"); s_zk = sem("s_zk")
        s_zr = sem("s_zr"); s_yk = sem("s_yk"); s_mvc = sem("s_mvc"); s_rsc = sem("s_rsc")
        s_xf = sem("s_xf"); s_xfT = sem("s_xfT"); s_xfTe = sem("s_xfTe"); s_rows = sem("s_rows")
        s_lgp = sem("s_lgp"); s_lg = sem("s_lg"); s_pool = sem("s_pool")
        s_ex = sem("s_ex"); s_mask = sem("s_mask"); s_pre = sem("s_pre"); s_dest = sem("s_dest")
        s_cnt = sem("s_cnt"); s_table = sem("s_table"); s_padr = sem("s_padr")
        s_sent = [sem(f"s_sent{n}") for n in range(HT)]
        s_pad = sem("s_pad")
        s_xr = [sem(f"s_xr{n}") for n in range(RING)]
        s_back = [sem(f"s_back{n}") for n in range(RING)]
        e_xT = sem("e_xT"); e_xTc = sem("e_xTc"); e_gu = sem("e_gu"); e_sg = sem("e_sg")
        e_h = sem("e_h"); e_hT = sem("e_hT"); e_hTc = sem("e_hTc"); e_y = sem("e_y"); e_yc = sem("e_yc"); e_turn = sem("e_turn")
        s_slots = [sem(f"s_slots{n}") for n in range(4)]
        s_sum = sem("s_sum"); s_out = [sem(f"s_out{n}") for n in range(4)]

        N_P0 = 6 * 16
        N_P1 = 6 * 16

        def seq(b):
            return b // 2 + 1

        block = ctx.enter_context(nc.Block())
        ITER = range(NB + 3)

        @block.sync
        def _(sp):
            sp.dma_start(zb[:, :, :].rearrange("p a b -> p (a b)"),
                         w1T.rearrange("(k p) f -> p k f", p=P)).then_inc(s_w1, 16)
            sp.dma_start(convs[:], conv).then_inc(s_small, 16)
            sp.dma_start(sbuf_s[1][:], w2T.rearrange("(c p) d -> p c d", p=P)).then_inc(s_w2, 16)
            sp.dma_start(router[:], routerT.rearrange("(k p) e -> p k e", p=P)).then_inc(s_small, 16)
            sp.dma_start(rbias[:], router_bias.partition_broadcast(P)).then_inc(s_small, 16)

            def load_layer0(b):
                n = b % 2
                if b >= 2:
                    sp.wait_ge(s_ya, b - 1)
                    sp.wait_ge(s_q1, b - 1)
                sp.dma_start(xTb[n][:], xT[:, b * S:(b + 1) * S].rearrange("(k p) t -> p k t", p=P)).then_inc(s_x[n], 16)
                sp.dma_start(xs[:, TB * b:TB * b + TB, :], x[b].rearrange("(j p) d -> p j d", p=P)).then_inc(s_x[n], 16)
                r = sp.value_load(id0[0:1, b:b + 1], min_val=0, max_val=l0_w1.shape[0] - 1)
                one = bass.ds(r, 1)
                sp.dma_start(w1b[n][:], l0_w1[one].rearrange("a (k p) n -> p (a k) n", p=P)).then_inc(s_p0[n], 16)
                sp.dma_start(w2b[n][:], l0_w2b2[one].rearrange("a k n -> (a k) n")).then_inc(s_p0[n], 16)
                sp.dma_start(b1b[n][:], l0_b1[one].rearrange("a n -> n a")).then_inc(s_p0[n], 16)
                sp.dma_start(ga0[n][:], l0_gamma[one].rearrange("a n -> (a n)").partition_broadcast(P)).then_inc(s_p0[n], 16)
                sp.dma_start(be0[n][:], l0_beta[one].rearrange("a n -> (a n)").partition_broadcast(P)).then_inc(s_p0[n], 32)

            def load_layer1(b):
                n = b % 2
                if b >= 2:
                    sp.wait_ge(s_yk, b - 1)
                    sp.wait_ge(s_xf, b - 1)
                    sp.wait_ge(s_x1b, b - 1)
                r = sp.value_load(id1[0:1, b:b + 1], min_val=0, max_val=l1_down.shape[0] - 1)
                one = bass.ds(r, 1)
                sp.dma_start(wdn[n][:], l1_down[one].rearrange("a (k p) n -> p (a k) n", p=P)).then_inc(s_p1[n], 16)
                sp.dma_start(wup[n][:], l1_up[one].rearrange("a k n -> (a k) n")).then_inc(s_p1[n], 16)
                sp.dma_start(bdn[n][:], l1_down_b[one].rearrange("a n -> n a")).then_inc(s_p1[n], 16)
                sp.dma_start(bup[n][:], l1_up_b[one].rearrange("a n -> (a n)").partition_broadcast(P)).then_inc(s_p1[n], 16)
                sp.dma_start(ga1[n][:], l1_gamma[one].rearrange("a n -> (a n)").partition_broadcast(P)).then_inc(s_p1[n], 16)
                sp.dma_start(be1[n][:], l1_beta[one].rearrange("a n -> (a n)").partition_broadcast(P)).then_inc(s_p1[n], 16)

            load_layer0(0)
            load_layer0(1)
            load_layer1(0)
            load_layer1(1)
            sp.dma_start(gate_up[:], gate_upT.rearrange("e (k p) n -> p e k n", p=P)).then_inc(s_ew, 16)
            sp.dma_start(down[:], downT).then_inc(s_ew, 16)
            for i in ITER:
                if 2 <= i < NB:
                    load_layer0(i)
                if 2 <= i - 3 < NB:
                    load_layer1(i - 3)
            sp.wait_ge(s_padr, 1)
            sp.dma_start(sent[E * REGION:E * REGION + P, :], pad[:]).then_inc(s_pad, 16)
            sp.wait_ge(s_cnt, 1)
            for e in range(E):
                c = sp.value_load(cnt_i[0:1, e:e + 1], min_val=0, max_val=TOK)
                sp.dma_start(sent[bass.ds(c + e * REGION, P), :], pad[:]).then_inc(s_pad, 16)
            sp.wait_ge(s_pad, 16 * (E + 1))
            for n in range(HT):
                sp.wait_ge(s_sent[n], 2 * TOP_K * 16)
            sp.wait_ge(s_table, 1)

            def load_tile(n, u, first):
                if not first:
                    sp.wait_ge(s_back[u], (n - u) * (16 // RING))
                r = sp.value_load(t_row[0:1, bass.ds(n, 1)], min_val=0, max_val=E * REGION)
                sp.dma_start(xr[u], sent[bass.ds(r, P), :]).then_inc(s_xr[u], 16)

            for u in range(RING):
                load_tile(u, u, True)
            with sp.Fori(1, TILES // RING) as i:
                for u in range(RING):
                    load_tile(i * RING + u, u, False)
            for u in range(RING):
                sp.wait_ge(s_back[u], 16 * (TILES // RING))
            for t in range(NT):
                if t >= 4:
                    sp.wait_ge(s_sum, t - 3)
                sp.dma_start(slots[t % 4], done[TOP_K * P * t:TOP_K * P * (t + 1), :].rearrange(
                    "(p a k) d -> p a k d", k=TOP_K, a=1)).then_inc(s_slots[t % 4], 16)
            for n in range(4):
                sp.wait_ge(s_out[n], 16 * (NT // 4))

        @block.gpsimd
        def _(pool):
            chain = [0]

            def link(ins):
                chain[0] += 1
                ins.then_inc(s_pool, 1)
                pool.wait_ge(s_pool, chain[0])

            pool.memset(ones[:], 1.0).then_inc(s_const, 1)
            pool.memset(gb[0][:], 0.0).then_inc(s_const, 1)
            pool.memset(gb[1][:], 0.0).then_inc(s_const, 1)
            pool.memset(hT[:], 1.0).then_inc(s_const, 1)
            pool.memset(ones_b[:], 1.0).then_inc(s_const, 1)
            pool.memset(half[:], -0.5).then_inc(s_const, 1)
            pool.memset(inv_e[:], INV_E).then_inc(s_const, 1)
            pool.memset(zrow[:], 0.0).then_inc(s_const, 1)
            link(pool.memset(ident[:], 0.0))
            pool.affine_select(out=ident[:], in_=ident[:], compare_op=ALU.not_equal, fill=1.0, base=0,
                               pattern=[[-1, P]], channel_multiplier=1).then_inc(s_ident, 1)
            link(pool.memset(before[:], 0.0))
            pool.affine_select(out=before[:], in_=before[:], compare_op=ALU.is_ge, fill=1.0, base=0,
                               pattern=[[-1, P]], channel_multiplier=1).then_inc(s_ident, 1)
            link(pool.memset(g_first[:], 0.0))
            for g in range(GROUPS):
                if g:
                    pool.memset(g_first[:, :, g, 0:g], 1.0).then_inc(s_const, 1)
            pool.iota(iota_e[:], pattern=[[1, E]], base=0, channel_multiplier=0,
                      allow_small_or_imprecise_dtypes=True).then_inc(s_iota, 1)
            pool.iota(iota_region[:], pattern=[[REGION, E]], base=0, channel_multiplier=0,
                      allow_small_or_imprecise_dtypes=True).then_inc(s_iota, 1)
            pool.iota(slot_id[:], pattern=[[P * TOP_K, NT], [1, TOP_K]], base=0,
                      channel_multiplier=TOP_K).then_inc(s_iota, 1)
            pool.iota(tj[:], pattern=[[1, TILES]], base=0, channel_multiplier=0,
                      allow_small_or_imprecise_dtypes=True).then_inc(s_iota, 1)
            link(pool.memset(pad[:], 0.0))
            pool.iota(pad[:, D:D + 1].bitcast(I32), pattern=[[0, 1]], base=TOK * TOP_K,
                      channel_multiplier=1).then_inc(s_padr, 1)

            def rstd(mv, out_, ready, b, signal):
                pool.wait_ge(ready, b + 1)
                link(pool.tensor_scalar(out_[:], mv[:, :, 1], LN_EPS, None, ALU.add))
                pool.tensor_tensor(out_[:], out_[:], half[:, 0:TB], op=ALU.pow).then_inc(signal, 1)

            for i in ITER:
                if i < NB:
                    rstd(mv_a, rstd_a, s_mva, i, s_rsa)
                b = i - 3
                if 0 <= b:
                    pool.wait_ge(s_x1, TB * (b + 1))
                    pool.wait_ge(s_p1[b % 2], N_P1 * seq(b))
                    for j in range(TB):
                        ins = pool.tensor_tensor(x1b[:, j, :], xs[:, TB * b + j, :], bup[b % 2][:], op=ALU.add)
                    ins.then_inc(s_x1b, 1)
                    rstd(mv_c, rstd_c, s_mvc, b, s_rsc)
                if i < NB:
                    pool.wait_ge(s_q1, i + 1)
                    if i:
                        pool.wait_ge(s_rbT, i)
                    for j in range(TB):
                        pool.tensor_scalar(rb[:, j, :], ones[:], q1[:, 2, j:j + 1], None, ALU.mult).then_inc(s_rb, 1)
                if 0 <= b:
                    if b % HB == HB - 1:
                        h = b // HB
                        pool.wait_ge(s_lg, b + 1)
                        pool.tensor_tensor(ex[:].rearrange("p t e -> p (t e)"), inv_e[:],
                                           lg[:, HT * h:HT * h + HT, :].rearrange("p t e -> p (t e)"),
                                           op=ALU.pow).then_inc(s_ex, 1)
                        pool.wait_ge(s_dest, h + 1)
                        pool.wait_ge(s_rows, NB // 2 * (h + 1))
                        for t in range(HT):
                            for k in range(TOP_K):
                                pool.indirect_dma_start(
                                    out=sent[:, :], in_=rows[:, t, k, :], in_offset=None,
                                    out_offset=bass.IndirectOffsetOnAxis(ap=dest[:, HT * h + t, k:k + 1], axis=0),
                                ).then_inc(s_sent[t], 16)

            last_slot = pool.to_reg(TOK * TOP_K - 1)

            def give_back(n, u):
                pool.wait_ge(e_yc, n + 1)
                pool.sem_inc(e_turn, 1)
                pool.indirect_dma_start(
                    out=done[:, :], in_=yr[u], in_offset=None,
                    out_offset=bass.IndirectOffsetOnAxis(ap=xr[u][:, D:D + 1].bitcast(I32), axis=0),
                    bounds_check=last_slot, oob_is_err=False).then_inc(s_back[u], 16)

            with pool.Fori(0, TILES // RING) as i:
                for u in range(RING):
                    give_back(i * RING + u, u)

        @block.tensor
        def _(pe):
            pe.wait_ge(s_const, 8 + GROUPS - 1)
            pe.wait_ge(s_ident, 2)
            pe.wait_ge(s_wsum, 2)
            pe.matmul(p_a[:, 0:2], ones[:], wstat[:], start=True, stop=True).then_inc(s_wtot, 1)

            def adapter0_hidden(b):
                pe.wait_ge(s_x[b % 2], 32 * seq(b))
                pe.wait_ge(s_p0[b % 2], N_P0 * seq(b))
                if b:
                    pe.wait_ge(s_deq, b)
                else:
                    pe.wait_ge(s_tern, 1)
                for k in range(DK):
                    ins = pe.matmul(p_a[0:A0, 0:S], w1b[b % 2][:, k, :], xTb[b % 2][:, k, :],
                                    start=k == 0, stop=k == DK - 1)
                ins.then_inc(s_hT, 1)

            def adapter0_out(b):
                pe.wait_ge(s_hr, b + 1)
                for j in range(TB):
                    ins = pe.matmul(p_a[:, j * D:(j + 1) * D], hT[:, j * P:(j + 1) * P], w2b[b % 2][:],
                                    start=True, stop=True)
                ins.then_inc(s_ya, 1)

            def adapter0_quant(b):
                pe.wait_ge(s_za, TB * (b + 1))
                for k in range(DK):
                    for j in range(TB):
                        ins = pe.transpose(p_a[:, k * S + j * P:k * S + (j + 1) * P], za[:, j, k * P:(k + 1) * P], ident[:])
                ins.then_inc(s_zaT, 1)
                pe.wait_ge(s_qT, b + 1)
                pe.wait_ge(s_rb, TB * (b + 1))
                for j in range(TB):
                    ins = pe.transpose(p_a[:, j * P:(j + 1) * P], rb[:, j, :], ident[:])
                ins.then_inc(s_rbT, 1)

            def up_pair(b, p):
                m = NP * b + p
                if p == 0:
                    pe.wait_ge(s_tern, 2)
                    pe.wait_ge(s_qT, b + 1)
                if m >= 2:
                    pe.wait_ge(s_g, m - 1)
                for c in range(2):
                    ch = (2 * p + c) * P
                    for k in range(DK):
                        ins = pe.matmul(p_pair[m % 2][:, c * S:(c + 1) * S], ternary1[:, k, ch:ch + P],
                                        qT[b % 2][:, k, :], start=k == 0, stop=k == DK - 1)
                ins.then_inc(s_h, 1)

            def hidden_by_token(b):
                pe.wait_ge(s_silu, NP * (b + 1))
                if b:
                    pe.wait_ge(s_x1, TB * b)
                for c in range(FC):
                    for j in range(TB):
                        ins = pe.transpose(p_tok[:, j * F + c * P:j * F + (c + 1) * P],
                                           sbuf_s[b % 2][:, c, j * P:(j + 1) * P], ident[:])
                ins.then_inc(s_sT, 1)

            def quant_by_channel(b):
                pe.wait_ge(s_zb, TB * (b + 1))
                for p in range(NP):
                    for c in range(2):
                        for j in range(TB):
                            o = p * 2 * S + c * S + j * P
                            ch = (2 * p + c) * P
                            ins = pe.transpose(p_tok[:, o:o + P], zb[:, j, ch:ch + P], ident[:])
                    ins.then_inc(s_zbT, 1)

            def ffn_out(b):
                pe.wait_ge(s_q2d, NP // 2 * (b + 1))
                pe.wait_ge(s_q2a, NP // 2 * (b + 1))
                for j in range(TB):
                    for c in range(FC):
                        ins = pe.matmul(p_tok[:, j * D:(j + 1) * D], q2T[:, c, j * P:(j + 1) * P], ternary2[:, c, :],
                                        start=c == 0, stop=c == FC - 1)
                ins.then_inc(s_y2, 1)

            def adapter1_in(b):
                pe.wait_ge(s_x1, TB * (b + 1))
                if b:
                    pe.wait_ge(s_lg, b)
                if b == HB:
                    pe.wait_ge(s_dest, 1)
                for k in range(DK):
                    for j in range(TB):
                        ins = pe.transpose(p_c[:, k * S + j * P:k * S + (j + 1) * P],
                                           xs[:, TB * b + j, k * P:(k + 1) * P], ident[:])
                ins.then_inc(s_x1T, 1)

            def adapter1_hidden(b):
                pe.wait_ge(s_x1Te, b + 1)
                pe.wait_ge(s_p1[b % 2], N_P1 * seq(b))
                for k in range(DK):
                    ins = pe.matmul(p_c[:, 0:S], wdn[b % 2][:, k, :], x1T[:, k, :], start=k == 0, stop=k == DK - 1)
                ins.then_inc(s_zk, 1)

            def adapter1_out(b):
                pe.wait_ge(s_zr, b + 1)
                for j in range(TB):
                    ins = pe.matmul(p_c[:, j * D:(j + 1) * D], zk[:, j * P:(j + 1) * P], wup[b % 2][:],
                                    start=True, stop=True)
                ins.then_inc(s_yk, 1)

            def logits(b):
                pe.wait_ge(s_xf, b + 1)
                for k in range(DK):
                    for j in range(TB):
                        ins = pe.transpose(p_c[:, k * S + j * P:k * S + (j + 1) * P], xf[:, j, k * P:(k + 1) * P], ident[:])
                ins.then_inc(s_xfT, 1)
                pe.wait_ge(s_xfTe, b + 1)
                if b == 0:
                    pe.wait_ge(s_small, 48)
                for j in range(TB):
                    for k in range(DK):
                        ins = pe.matmul(p_c[:, j * E:(j + 1) * E], xfT[:, k, j * P:(j + 1) * P], router[:, k, :],
                                        start=k == 0, stop=k == DK - 1)
                ins.then_inc(s_lgp, 1)

            def places(h):
                pe.wait_ge(s_mask, h + 1)
                pe.matmul(p_c[:, 0:HT * E], before[:], mask_b[:, HT * h:HT * h + HT, :], start=True, stop=False,
                          skip_group_check=True)
                for t in range(HT * h):
                    pe.matmul(p_c[:, 0:HT * E], ones_b[:], mask_b[:, t:t + 1, :].to_broadcast([P, HT, E]),
                              start=False, stop=False, skip_group_check=True)
                for t in range(HT - 1):
                    n = HT - 1 - t
                    ins = pe.matmul(p_c[:, (t + 1) * E:HT * E], ones_b[:],
                                    mask_b[:, HT * h + t:HT * h + t + 1, :].to_broadcast([P, n, E]),
                                    start=False, stop=t == HT - 2, skip_group_check=True)
                if h == 1:
                    for t in range(NT):
                        ins = pe.matmul(p_c[:, HT * E:HT * E + E], ones_b[:], mask_b[:, t, :],
                                        start=t == 0, stop=t == NT - 1)
                ins.then_inc(s_pre, 1)

            for i in ITER:
                b1, b2, b3 = i - 1, i - 2, i - 3
                if 0 <= b1 < NB:
                    up_pair(b1, 0)
                if i < NB:
                    adapter0_hidden(i)
                if 0 <= b2 < NB:
                    hidden_by_token(b2)
                if 0 <= b3:
                    adapter1_in(b3)
                if i < NB:
                    adapter0_out(i)
                if 0 <= b3:
                    adapter1_hidden(b3)
                if 0 <= b1 < NB:
                    up_pair(b1, 1)
                if 0 <= b3:
                    adapter1_out(b3)
                if 0 <= b1 < NB:
                    up_pair(b1, 2)
                if 0 <= b2 < NB:
                    quant_by_channel(b2)
                    ffn_out(b2)
                if 0 <= b1 < NB:
                    up_pair(b1, 3)
                if i < NB:
                    adapter0_quant(i)
                if 0 <= b3:
                    logits(b3)
                    if b3 % HB == HB - 1:
                        places(b3 // HB)

            pe.wait_ge(s_ew, 32)
            pe.wait_ge(s_table, 1)

            def x_by_width(n, u):
                pe.wait_ge(s_xr[u], 16 * (n // RING + 1) if isinstance(n, int) else (n - u) * (16 // RING) + 16)
                if not (isinstance(n, int) and n < 2):
                    pe.wait_ge(e_xTc, n - 1)
                for k in range(DK):
                    ins = pe.transpose(p_pair[u % 2][:, k * P:(k + 1) * P], xr[u][:, k * P:(k + 1) * P], ident[:])
                ins.then_inc(e_xT, 1)

            def gate_and_up(n, u, e):
                pe.wait_ge(e_xTc, n + 1)
                if not (isinstance(n, int) and n < 2):
                    pe.wait_ge(e_h, n - 1)
                for k in range(DK):
                    ins = pe.matmul(p_tok[:, u % 2 * 512:u % 2 * 512 + 2 * HI], xTe[u % 2][:, k, :],
                                    gate_up[:, bass.ds(e, 1), k, :], start=k == 0, stop=k == DK - 1)
                ins.then_inc(e_gu, 1)

            def hidden_by_width(n, u):
                pe.wait_ge(e_h, n + 1)
                if not (isinstance(n, int) and n < 2):
                    pe.wait_ge(e_hTc, n - 1)
                pe.transpose((p_a, p_c)[u % 2][:, 0:P], he[u % 2], ident[:]).then_inc(e_hT, 1)

            def expert_out(n, u, e):
                pe.wait_ge(e_hTc, n + 1)
                if not (isinstance(n, int) and n < 2):
                    pe.wait_ge(e_yc, n - 1)
                pe.matmul(p_tok[:, 1024 + u % 2 * 512:1024 + u % 2 * 512 + D], hTe[u % 2],
                          down[:, bass.ds(e, 1), :], start=True, stop=True).then_inc(e_y, 1)

            def expert_of(n):
                return pe.value_load(t_exp[0:1, bass.ds(n, 1)], min_val=0, max_val=E - 1)

            def step(n, u, last=False):
                if not (last and n + 1 >= TILES):
                    x_by_width(n + 1, (u + 1) % RING)
                if not (last and n >= TILES):
                    gate_and_up(n, u, expert_of(n))
                if not (isinstance(n, int) and (n < 1 or n > TILES)):
                    hidden_by_width(n - 1, (u - 1) % RING)
                if not (isinstance(n, int) and n < 2):
                    expert_out(n - 2, (u - 2) % RING, expert_of(n - 2))

            x_by_width(0, 0)
            for n in range(RING):
                step(n, n)
            with pe.Fori(1, TILES // RING - 1) as i:
                for u in range(RING):
                    step(i * RING + u, u)
            for n in range(TILES - RING, TILES + 2):
                step(n, n % RING, last=True)

        @block.scalar
        def _(act):
            def copy(o, i_):
                return act.activation(o, i_, ACT.Copy)

            def conv_centre(b, p):
                m = NP * b + p
                act.wait_ge(s_g, m + 1)
                if m == 0:
                    act.wait_ge(s_small, 48)
                if m >= 2:
                    act.wait_ge(s_silu, m - 1)
                for c in range(2):
                    ch = 2 * p + c
                    ins = act.activation(cb[m % 2][:, c, :], gb[m % 2][:, c, 1:S + 1], ACT.Identity,
                                         bias=convs[:, ch, 3:4], scale=convs[:, ch, 1:2])
                ins.then_inc(s_c0, 1)

            def silu(m):
                b, p = m // NP, m % NP
                act.wait_ge(s_tap, m + 1)
                if p == 0 and b >= 2:
                    act.wait_ge(s_sT, b - 1)
                if m == NP:
                    act.wait_ge(s_tern, 2)
                act.activation(sbuf_s[b % 2][:, 2 * p:2 * p + 2, :], cb[m % 2][:], ACT.Silu).then_inc(s_silu, 1)

            for i in ITER:
                b1, b2, b3 = i - 1, i - 2, i - 3
                for p in range(NP):
                    m = NP * b1 + p
                    if 0 <= b1 < NB:
                        conv_centre(b1, p)
                    if 0 <= m - 1 < NP * NB:
                        silu(m - 1)
                    if p == 0 and i < NB:
                        act.wait_ge(s_hT, i + 1)
                        act.activation(hT[0:A0, :], p_a[0:A0, 0:S], ACT.Relu, bias=b1b[i % 2][:, 0:1]).then_inc(s_hr, 1)
                    if p == 0 and 0 <= b3:
                        act.wait_ge(s_x1T, b3 + 1)
                        copy(x1T[:].rearrange("p k t -> p (k t)"), p_c[:, :]).then_inc(s_x1Te, 1)
                    if p == 1 and 0 <= b3:
                        act.wait_ge(s_zk, b3 + 1)
                        act.activation(zk[:], p_c[:, 0:S], ACT.Relu, bias=bdn[b3 % 2][:, 0:1]).then_inc(s_zr, 1)
                    if p == 1 and 0 <= b2 < NB:
                        act.wait_ge(s_q2, b2 + 1)
                        if b2:
                            act.wait_ge(s_zbT, NP * b2)
                        else:
                            act.wait_ge(s_tern, 1)
                        for j in range(TB):
                            act.activation(zb[:, j, :], p_tok[:, j * F:(j + 1) * F], ACT.Identity,
                                           bias=MAGIC, scale=q2[:, 1, j:j + 1]).then_inc(s_zb, 1)
                    if p == 2 and i < NB:
                        act.wait_ge(s_q1, i + 1)
                        if i:
                            act.wait_ge(s_zaT, i)
                        for j in range(TB):
                            act.activation(za[:, j, :], ya[:, j, :], ACT.Identity,
                                           bias=MAGIC, scale=q1[:, 1, j:j + 1]).then_inc(s_za, 1)
                    if p == 2 and 0 <= b2 < NB:
                        for q in range(NP // 2, NP):
                            act.wait_ge(s_zbT, NP * b2 + q + 1)
                            act.activation(q2T[:, 2 * q:2 * q + 2, :], p_tok[:, q * 512:(q + 1) * 512].rearrange(
                                "p (c t) -> p c t", c=2), ACT.Identity, bias=-MAGIC).then_inc(s_q2a, 1)
                    if p == 3 and i < NB:
                        act.wait_ge(s_zaT, i + 1)
                        if i >= 2:
                            act.wait_ge(s_h, NP * (i - 1))
                        act.activation(qT[i % 2][:].rearrange("p k t -> p (k t)"), p_a[:, :], ACT.Identity,
                                       bias=-MAGIC).then_inc(s_qT, 1)
                    if p == 3 and 0 <= b3:
                        act.wait_ge(s_xfT, b3 + 1)
                        copy(xfT[:].rearrange("p k t -> p (k t)"), p_c[:, :]).then_inc(s_xfTe, 1)
                        for j in range(TB):
                            t = TB * b3 + j
                            if t >= HT:
                                act.wait_ge(s_sent[t % HT], TOP_K * 16)
                            ins = copy(rows[:, t % HT, :, 0:D], xf[:, j:j + 1, :].to_broadcast([P, TOP_K, D]))
                        ins.then_inc(s_rows, 1)

            def x_copy(n, u):
                act.wait_ge(e_xT, n + 1)
                if not (isinstance(n, int) and n < 2):
                    act.wait_ge(e_gu, n - 1)
                copy(xTe[u % 2], p_pair[u % 2][:, 0:D].rearrange("p (k t) -> p k t", k=DK)).then_inc(e_xTc, 1)

            def gate(n, u):
                act.wait_ge(e_gu, n + 1)
                if not (isinstance(n, int) and n < 2):
                    act.wait_ge(e_h, n - 1)
                act.activation(sg[u % 2], p_tok[:, u % 2 * 512:u % 2 * 512 + HI], ACT.Silu).then_inc(e_sg, 1)

            x_copy(0, 0)
            for n in range(RING):
                x_copy(n + 1, (n + 1) % RING)
                gate(n, n)
            with act.Fori(1, TILES // RING - 1) as i:
                for u in range(RING):
                    x_copy(i * RING + u + 1, (u + 1) % RING)
                    gate(i * RING + u, u)
            for n in range(TILES - RING, TILES):
                if n + 1 < TILES:
                    x_copy(n + 1, (n + 1) % RING)
                gate(n, n % RING)
            for t in range(NT):
                act.wait_ge(s_sum, t + 1)
                act.dma_start(out[t // TB, t % TB * P:(t % TB + 1) * P, :], xs[:, t, :]).then_inc(s_out[t % 4], 16)

        @block.vector
        def _(dve):
            chain = [0]

            def mark(ins):
                chain[0] += 1
                ins.then_inc(s_dve, 1)
                return chain[0]

            def link(ins):
                dve.wait_ge(s_dve, mark(ins))

            w1f = zb[:, :, :].rearrange("p a b -> p (a b)")
            w2f = sbuf_s[1][:, :, :].rearrange("p a b -> p (a b)")
            dve.wait_ge(s_w1, 16)
            dve.tensor_reduce(wstat[:, 0:1], w1f, AX_X, ALU.add, apply_absolute_value=True).then_inc(s_wsum, 1)
            dve.wait_ge(s_w2, 16)
            dve.tensor_reduce(wstat[:, 1:2], w2f, AX_X, ALU.add, apply_absolute_value=True).then_inc(s_wsum, 1)
            dve.wait_ge(s_wtot, 1)
            link(dve.tensor_scalar(wmean[:], p_a[:, 0:2], 1.0 / (F * D), QUANT_MIN, ALU.mult, ALU.max))
            link(dve.reciprocal(wscale[:], wmean[:]))
            link(dve.tensor_scalar(wdeq[:], wmean[:], 1.0 / QMAX, None, ALU.mult))
            for n, (w, o) in enumerate(((w1f, ternary1), (w2f, ternary2))):
                link(dve.tensor_scalar(w, w, wscale[:, n:n + 1], 1.0, ALU.mult, ALU.min))
                link(dve.tensor_scalar(w, w, -1.0, MAGIC, ALU.max, ALU.add))
                dve.tensor_scalar(o[:].rearrange("p a b -> p (a b)"), w, MAGIC, None, ALU.subtract).then_inc(s_tern, 1)

            def stats(y, bn, mv, ready):
                for j in range(TB):
                    n = mark(dve.bn_stats(bn[:, j, :], y[:, j, :]))
                dve.wait_ge(s_dve, n)
                for j in range(TB):
                    ins = dve.bn_aggr(mv[:, j, :], bn[:, j, :])
                ins.then_inc(ready, 1)

            def norm(y, o, mv, rs, ga, be):
                for j in range(TB):
                    n = mark(dve.scalar_tensor_tensor(y[:, j, :], y[:, j, :], mv[:, j, 0:1], ga[:], ALU.subtract, ALU.mult))
                dve.wait_ge(s_dve, n)
                for j in range(TB):
                    ins = dve.scalar_tensor_tensor(o[:, j, :], y[:, j, :], rs[:, j:j + 1], be[:], ALU.mult, ALU.add)
                return ins

            def scales(q, deq, signal):
                link(dve.tensor_scalar(q[:, 3, :], q[:, 0, :], QUANT_MIN, None, ALU.max))
                link(dve.reciprocal(q[:, 0, :], q[:, 3, :]))
                dve.tensor_scalar(q[:, 2, :], q[:, 3, :], deq, None, ALU.mult)
                dve.tensor_scalar(q[:, 1, :], q[:, 0, :], QMAX, None, ALU.mult).then_inc(signal, 1)

            def adapter0_residual(b):
                dve.wait_ge(s_ya, b + 1)
                if b:
                    dve.wait_ge(s_za, TB * b)
                link(dve.tensor_tensor(ya[:].rearrange("p j d -> p (j d)"), p_a[:, :],
                                       xs[:, TB * b:TB * b + TB, :].rearrange("p j d -> p (j d)"), ALU.add))
                stats(ya, bn_a, mv_a, s_mva)

            def adapter0_norm(b):
                dve.wait_ge(s_rsa, b + 1)
                if b:
                    dve.wait_ge(s_rb, TB * b)
                link(norm(ya, ya, mv_a, rstd_a, ga0[b % 2], be0[b % 2]))
                link(dve.tensor_reduce(q1[:, 0, :], ya[:], AX_X, ALU.max, apply_absolute_value=True))
                scales(q1, wdeq[:, 0:1], s_q1)

            def dequant_pair(m):
                b = m // NP
                dve.wait_ge(s_h, m + 1)
                if m == 0:
                    dve.wait_ge(s_const, 8 + GROUPS - 1)
                if m % NP == 0:
                    dve.wait_ge(s_deq, b + 1)
                if m >= 2:
                    dve.wait_ge(s_c0, m - 1)
                    dve.wait_ge(s_tap, m - 1)
                dve.tensor_tensor(gb[m % 2][:, :, 1:S + 1], p_pair[m % 2][:, :].rearrange("p (c t) -> p c t", c=2),
                                  deq_bc[b % 2][:].rearrange("p (a t) -> p a t", a=1).to_broadcast([P, 2, S]),
                                  ALU.mult).then_inc(s_g, 1)

            def conv_sides(m):
                dve.wait_ge(s_c0, m + 1)
                dve.wait_ge(s_g, m + 1)
                marks = []
                for c in range(2):
                    ch = 2 * (m % NP) + c
                    marks.append(mark(dve.scalar_tensor_tensor(cb[m % 2][:, c, :], gb[m % 2][:, c, 0:S], convs[:, ch, 0:1],
                                                               cb[m % 2][:, c, :], ALU.mult, ALU.add)))
                for c in range(2):
                    ch = 2 * (m % NP) + c
                    dve.wait_ge(s_dve, marks[c])
                    ins = dve.scalar_tensor_tensor(cb[m % 2][:, c, :], gb[m % 2][:, c, 2:S + 2], convs[:, ch, 2:3],
                                                   cb[m % 2][:, c, :], ALU.mult, ALU.add)
                ins.then_inc(s_tap, 1)

            def hidden_scales(b):
                dve.wait_ge(s_sT, b + 1)
                link(dve.tensor_reduce(q2[:, 0, :], p_tok[:, :].rearrange("p (j f) -> p j f", j=TB), AX_X, ALU.max,
                                       apply_absolute_value=True))
                scales(q2, wdeq[:, 1:2], s_q2)

            def route(h):
                ts = slice(HT * h, HT * h + HT)
                dve.wait_ge(s_ex, h + 1)
                dve.wait_ge(s_iota, 4)
                link(dve.tensor_scalar(ex[:], ex[:], 1.0, None, ALU.add))
                link(dve.reciprocal(score[:], ex[:]))
                link(dve.tensor_tensor(choice[:], score[:], rbias[:].rearrange("p (a e) -> p a e", a=1).to_broadcast([P, HT, E]), ALU.add))
                four = choice[:].rearrange("p t (g a b) -> p (t g) a b", g=GROUPS, a=2)
                dve.tensor_tensor(g_hi[:], four[:, :, :, 0], four[:, :, :, 1], ALU.max)
                link(dve.tensor_tensor(g_lo[:], four[:, :, :, 0], four[:, :, :, 1], ALU.min))
                dve.tensor_tensor(g_t[:, 0, :], g_hi[:, :, 0], g_hi[:, :, 1], ALU.max)
                dve.tensor_tensor(g_t[:, 1, :], g_hi[:, :, 0], g_hi[:, :, 1], ALU.min)
                link(dve.tensor_tensor(g_t[:, 2, :], g_lo[:, :, 0], g_lo[:, :, 1], ALU.max))
                link(dve.tensor_tensor(g_t[:, 1, :], g_t[:, 1, :], g_t[:, 2, :], ALU.max))
                link(dve.tensor_tensor(g_sum[:].rearrange("p t g -> p (t g)"), g_t[:, 0, :], g_t[:, 1, :], ALU.add))
                mine = g_sum[:].rearrange("p t (g a) -> p t g a", a=1).to_broadcast([P, HT, GROUPS, GROUPS])
                theirs = g_sum[:].rearrange("p t (a g) -> p t a g", a=1).to_broadcast([P, HT, GROUPS, GROUPS])
                dve.tensor_tensor(g_gt[:], theirs, mine, ALU.is_gt)
                link(dve.tensor_tensor(g_ge[:], theirs, mine, ALU.is_ge))
                link(dve.tensor_tensor(g_ge[:], g_ge[:], g_first[:], ALU.mult))
                link(dve.tensor_tensor(g_ge[:], g_ge[:], g_gt[:], ALU.max))
                link(dve.tensor_reduce(g_rank[:], g_ge[:], AX_X, ALU.add))
                link(dve.tensor_scalar(g_mask[:], g_rank[:], float(GROUPS_KEPT), None, ALU.is_lt))
                link(dve.tensor_scalar(g_pen[:], g_mask[:], -1.0, -NEG_INF, ALU.add, ALU.mult))
                per = E // GROUPS

                def wide(a):
                    return a[:].rearrange("p t (g a) -> p (t g) a", a=1).to_broadcast([P, HT * GROUPS, per])

                flat = masked[:].rearrange("p t (g a) -> p (t g) a", g=GROUPS)
                link(dve.tensor_tensor(flat, choice[:].rearrange("p t (g a) -> p (t g) a", g=GROUPS), wide(g_mask), ALU.mult))
                link(dve.tensor_tensor(flat, flat, wide(g_pen), ALU.add))
                for t in range(HT):
                    n = mark(dve.max(top8[:, t, :], masked[:, t, :]))
                dve.wait_ge(s_dve, n)
                for t in range(HT):
                    n = mark(dve.max_index(idx8[:, t, :], top8[:, t, :], masked[:, t, :]))
                dve.wait_ge(s_dve, n)
                link(dve.tensor_copy(idxf[:], idx8[:, :, 0:TOP_K]))
                link(dve.tensor_tensor(onehot[:], iota_e[:].rearrange("p (a b e) -> p a b e", a=1, b=1).to_broadcast([P, HT, TOP_K, E]),
                                       idxf[:].rearrange("p t (k a) -> p t k a", a=1).to_broadcast([P, HT, TOP_K, E]), ALU.is_equal))
                with nc.allow_low_precision(reason="a sum that is 0 or 1 is exact in bfloat16"):
                    dve.tensor_reduce(mask_b[:, ts, :], onehot[:].rearrange("p t k e -> p t e k"), AX_X, ALU.add).then_inc(s_mask, 1)
                link(dve.tensor_tensor(picked[:], onehot[:], score[:].rearrange("p t (a e) -> p t a e", a=1).to_broadcast([P, HT, TOP_K, E]), ALU.mult))
                link(dve.tensor_reduce(wk[:], picked[:], AX_X, ALU.add))
                link(dve.tensor_reduce(wsum[:], wk[:], AX_X, ALU.add))
                link(dve.tensor_scalar(wsum[:], wsum[:], 1e-20, None, ALU.add))
                link(dve.reciprocal(wsum[:], wsum[:]))
                dve.wait_ge(s_rows, NB // 2 * h) if h else None
                if h:
                    for t in range(HT):
                        dve.wait_ge(s_sent[t], TOP_K * 16)
                link(dve.scalar_tensor_tensor(rows[:, :, :, D + 1], wk[:], ROUTED_SCALE,
                                              wsum[:].rearrange("p (t a) -> p t a", a=1).to_broadcast([P, HT, TOP_K]), ALU.mult, ALU.mult))
                link(dve.tensor_copy(rows[:, :, :, D].bitcast(I32), slot_id[:, ts, :]))
                dve.wait_ge(s_pre, h + 1)
                if h == 1:
                    expert_tiles()
                link(dve.tensor_tensor(pos[:], p_c[:, 0:HT * E].rearrange("p (t e) -> p t e", t=HT),
                                       iota_region[:].rearrange("p (a e) -> p a e", a=1).to_broadcast([P, HT, E]), ALU.add))
                link(dve.tensor_tensor(picked[:], onehot[:], pos[:].rearrange("p t (a e) -> p t a e", a=1).to_broadcast([P, HT, TOP_K, E]), ALU.mult))
                link(dve.tensor_reduce(dest_f[:], picked[:], AX_X, ALU.add))
                dve.tensor_copy(dest[:, ts, :], dest_f[:]).then_inc(s_dest, 1)

            def expert_tiles():
                link(dve.tensor_copy(cnt[:, 0, :], p_c[0:1, HT * E:HT * E + E]))
                dve.tensor_copy(cnt_i[:], cnt[:, 0, :]).then_inc(s_cnt, 1)
                link(dve.tensor_scalar(cnt[:, 1, :], cnt[:, 0, :], 1.0 / P, 0.5 - 0.5 / P, ALU.mult, ALU.add))
                link(dve.tensor_scalar(cnt[:, 1, :], cnt[:, 1, :], MAGIC, None, ALU.add))
                link(dve.tensor_scalar(cnt[:, 1, :], cnt[:, 1, :], MAGIC, None, ALU.subtract))
                dve.tensor_scalar(cnt[:, 3, :], cnt[:, 1, :], -float(P), float(REGION), ALU.mult, ALU.add)
                link(dve.tensor_tensor_scan(cnt[:, 2, :], cnt[:, 1, :], zrow[:], 0.0, ALU.add, ALU.add))

            def tile_list():
                full = [1, TILES, E]
                link(dve.tensor_tensor(t_mask, tj[:].rearrange("p (t a) -> p t a", a=1).to_broadcast(full),
                                       cnt[:, 2:3, :].to_broadcast(full), ALU.is_ge))
                link(dve.tensor_reduce(t_f[:, 0, :], t_mask, AX_X, ALU.add))
                link(dve.tensor_scalar(t_f[:, 0, :], t_f[:, 0, :], float(E - 1), None, ALU.min))
                link(dve.tensor_tensor(t_prod, t_mask, cnt[:, 3:4, :].to_broadcast(full), ALU.mult))
                link(dve.tensor_reduce(t_f[:, 1, :], t_prod, AX_X, ALU.add))
                link(dve.scalar_tensor_tensor(t_f[:, 1, :], tj[:], float(P), t_f[:, 1, :], ALU.mult, ALU.add))
                link(dve.tensor_scalar(t_f[:, 1, :], t_f[:, 1, :], float(E * REGION), None, ALU.min))
                link(dve.tensor_copy(t_exp[:], t_f[:, 0, :]))
                dve.tensor_copy(t_row[:], t_f[:, 1, :]).then_inc(s_table, 1)

            for i in ITER:
                b1, b2, b3 = i - 1, i - 2, i - 3
                for p in range(NP):
                    m = NP * b1 + p
                    if 0 <= b1 < NB:
                        dequant_pair(m)
                    if 0 <= m - 1 < NP * NB:
                        conv_sides(m - 1)
                    if p == 0:
                        if i < NB:
                            adapter0_residual(i)
                        if 0 <= b2 < NB:
                            hidden_scales(b2)
                    if p == 1:
                        if 0 <= b3:
                            dve.wait_ge(s_yk, b3 + 1)
                            if b3:
                                dve.wait_ge(s_xf, b3)
                            dve.wait_ge(s_x1b, b3 + 1)
                            link(dve.tensor_tensor(yk[:].rearrange("p j d -> p (j d)"), p_c[:, :],
                                                   x1b[:].rearrange("p j d -> p (j d)"), ALU.add))
                            stats(yk, bn_c, mv_c, s_mvc)
                        if i < NB:
                            adapter0_norm(i)
                    if p == 2:
                        if 0 <= b2 < NB:
                            for q in range(NP // 2):
                                dve.wait_ge(s_zbT, NP * b2 + q + 1)
                                dve.tensor_scalar(q2T[:, 2 * q:2 * q + 2, :], p_tok[:, q * 512:(q + 1) * 512].rearrange(
                                    "p (c t) -> p c t", c=2), MAGIC, None, ALU.subtract).then_inc(s_q2d, 1)
                        if 0 <= b3:
                            dve.wait_ge(s_rsc, b3 + 1)
                            if b3:
                                dve.wait_ge(s_xfT, b3)
                                dve.wait_ge(s_rows, b3)
                            norm(yk, xf, mv_c, rstd_c, ga1[b3 % 2], be1[b3 % 2]).then_inc(s_xf, 1)
                    if p == 3:
                        if 0 <= b2 < NB:
                            dve.wait_ge(s_y2, b2 + 1)
                            for j in range(TB):
                                t = TB * b2 + j
                                dve.scalar_tensor_tensor(xs[:, t, :], p_tok[:, j * D:(j + 1) * D], q2[:, 2, j:j + 1],
                                                         xs[:, t, :], ALU.mult, ALU.add).then_inc(s_x1, 1)
                        if i < NB:
                            dve.wait_ge(s_rbT, i + 1)
                            if i >= 2:
                                dve.wait_ge(s_g, NP * (i - 1))
                            dve.tensor_copy(deq_bc[i % 2][:], p_a[:, 0:S]).then_inc(s_deq, 1)
                        if 0 <= b3:
                            dve.wait_ge(s_lgp, b3 + 1)
                            dve.tensor_copy(lg[:, TB * b3:TB * b3 + TB, :].rearrange("p t e -> p (t e)"),
                                            p_c[:, 0:TB * E]).then_inc(s_lg, 1)
                            if b3 % HB == HB - 1:
                                route(b3 // HB)
            tile_list()

            def hidden(n, u):
                dve.wait_ge(e_sg, n + 1)
                dve.wait_ge(s_xr[u], 16 * (n // RING + 1) if isinstance(n, int) else (n - u) * (16 // RING) + 16)
                if not (isinstance(n, int) and n < 2):
                    dve.wait_ge(e_hT, n - 1)
                dve.scalar_tensor_tensor(he[u % 2], sg[u % 2], xr[u][:, D + 1:D + 2],
                                         p_tok[:, u % 2 * 512 + HI:u % 2 * 512 + 2 * HI], ALU.mult, ALU.mult).then_inc(e_h, 1)

            def hidden_copy(n, u):
                dve.wait_ge(e_hT, n + 1)
                if not (isinstance(n, int) and n < 2):
                    dve.wait_ge(e_y, n - 1)
                dve.tensor_copy(hTe[u % 2], (p_a, p_c)[u % 2][:, 0:P]).then_inc(e_hTc, 1)

            def out_copy(n, u):
                dve.wait_ge(e_y, n + 1)
                if not (isinstance(n, int) and n < RING):
                    dve.wait_ge(s_back[u], 16 * (n // RING) if isinstance(n, int) else (n - u) * (16 // RING))
                dve.tensor_copy(yr[u], p_tok[:, 1024 + u % 2 * 512:1024 + u % 2 * 512 + D]).then_inc(e_yc, 1)

            def step(n, u):
                if not (isinstance(n, int) and n >= TILES):
                    hidden(n, u)
                if not (isinstance(n, int) and (n < 1 or n > TILES)):
                    hidden_copy(n - 1, (u - 1) % RING)
                if not (isinstance(n, int) and n < 2):
                    out_copy(n - 2, (u - 2) % RING)

            for n in range(2 * RING):
                step(n, n % RING)
            with dve.Fori(2, TILES // RING) as i:
                for u in range(RING):
                    step(i * RING + u, u)
            for n in range(TILES, TILES + 2):
                step(n, n % RING)

            for t in range(NT):
                dve.wait_ge(s_slots[t % 4], 16 * (t // 4 + 1))
                sl = slots[t % 4][:, 0]
                link(dve.tensor_tensor(sl[:, 0:2, :], sl[:, 0:2, :], sl[:, 2:4, :], ALU.add))
                link(dve.tensor_tensor(sl[:, 0, :], sl[:, 0, :], sl[:, 1, :], ALU.add))
                dve.tensor_tensor(xs[:, t, :], xs[:, t, :], sl[:, 0, :], ALU.add).then_inc(s_sum, 1)


def kernel(**inputs):
    import numpy as _np
    import concourse.bacc as _bacc
    from concourse import mybir as _mybir
    from concourse.bass_utils import run_bass_kernel_spmd as _run

    i = {k: _np.asarray(v) for k, v in inputs.items()}
    F, D = i["L0_ffn_w1"].shape
    conv = _np.concatenate([i["L0_ffn_conv_w"][:, 0, :], i["L0_ffn_conv_b"][:, None]], axis=1)
    E = i["L1_ffn_w_gate"].shape[0]
    NB, S, _ = i["x"].shape
    arrays = {
        "x": i["x"],
        "xT": i["x"].reshape(NB * S, D).T,
        "id0": i["itok_B_0_8"][None, :],
        "id1": i["itok_B_0_6"][None, :],
        "l0_w1": i["L0_cond_W1"],
        "l0_b1": i["L0_cond_b1"],
        "l0_w2b2": _np.concatenate([i["L0_cond_W2"], i["L0_cond_b2"][:, None, :]], axis=1),
        "l0_gamma": i["L0_cond_gamma"],
        "l0_beta": i["L0_cond_beta"],
        "w1T": i["L0_ffn_w1"].T,
        "conv": conv.reshape(F // 128, 128, 4).transpose(1, 0, 2),
        "w2T": i["L0_ffn_w2"].T,
        "l1_down": i["L1_cond_down_w"],
        "l1_down_b": i["L1_cond_down_b"],
        "l1_up": i["L1_cond_up_w"],
        "l1_up_b": i["L1_cond_up_b"],
        "l1_gamma": i["L1_cond_ln_g"],
        "l1_beta": i["L1_cond_ln_b"],
        "routerT": i["L1_ffn_router_weight"].T,
        "router_bias": i["L1_ffn_router_bias"],
        "gate_upT": _np.concatenate([i["L1_ffn_w_gate"].transpose(0, 2, 1), i["L1_ffn_w_up"].transpose(0, 2, 1)], axis=2),
        "downT": i["L1_ffn_w_down"].transpose(2, 0, 1),
    }
    arrays = {f"in_{k}": _np.ascontiguousarray(v) for k, v in arrays.items()}
    nc = _bacc.Bacc("TRN2", target_bir_lowering=False, num_devices=1)
    f32 = _mybir.dt.float32
    args = [nc.dram_tensor(k, v.shape, _mybir.dt.from_np(v.dtype), kind="ExternalInput").ap() for k, v in arrays.items()]
    args.append(nc.dram_tensor("out_0", i["x"].shape, f32, kind="ExternalOutput").ap())
    args.append(nc.dram_tensor("sent", (E * (NB * S + 128) + 128, D + 2), f32, kind="Internal").ap())
    args.append(nc.dram_tensor("done", (4 * NB * S, D), f32, kind="Internal").ap())
    build(nc, *args)
    r = _run(nc, [arrays], core_ids=[0])
    return r.results[0]["out_0"]
```

```python
from contextlib import ExitStack

import concourse.bass as bass
from concourse import mybir

ALU = mybir.AluOpType
ACT = mybir.ActivationFunctionType
AX_X = mybir.AxisListType.X
F32 = mybir.dt.float32
BF16 = mybir.dt.bfloat16
I32 = mybir.dt.int32
U32 = mybir.dt.uint32

P = 128
MAGIC = 1.5 * 2.0 ** 23
LN_EPS = 1e-5
QUANT_MIN = 1e-5
QMAX = 127.0
GROUPS, GROUPS_KEPT, TOP_K = 4, 2, 4
NEG_INF = -1e9
ROUTED_SCALE = 2.5


def build(nc, x, xT, id0, id1, l0_w1, l0_b1, l0_w2b2, l0_gamma, l0_beta, w1T, conv, w2T,
          l1_down, l1_down_b, l1_up, l1_up_b, l1_gamma, l1_beta, routerT, router_bias,
          gate_upT, downT, out, sent, done):
    NB, S, D = x.shape
    TOK = NB * S
    NT = TOK // P
    TB = S // P
    DK = D // P
    A0 = l0_w1.shape[2]
    A1 = l1_down.shape[2]
    F = w1T.shape[1]
    FC = F // P
    NP = FC // 2
    E = routerT.shape[1]
    HI = downT.shape[0]
    ROW = sent.shape[1]
    REGION = TOK + P
    ROUTE = [(0, 3), (3, 6), (6, 8)]
    GT = max(TB * (hi - lo) for lo, hi in ROUTE)
    RT = 8
    assert A1 == P and HI == P and TB == 2 and DK == 2 and ROUTE[-1][1] == NB
    LIVE = (TOP_K * TOK + E * (P - 1)) // P
    RING = 8
    TILES = (LIVE + RING - 1) // RING * RING

    with ExitStack() as ctx:
        def sb(name, shape, dt=F32):
            return ctx.enter_context(nc.sbuf_tensor(name, shape, dt))

        def ps(name, cols):
            return ctx.enter_context(nc.psum_tensor(name, [P, cols], F32))

        def sem(name):
            return ctx.enter_context(nc.semaphore(name))

        p_pair = [ps(f"p_pair{n}", 512) for n in range(2)]
        p_tok = ps("p_tok", 2048)
        p_a = ps("p_a", 512)
        p_c = ps("p_c", 512)

        ident = sb("ident", [P, P])
        ones = sb("ones", [P, P])
        ones_b = sb("ones_b", [P, P], BF16)
        before = sb("before", [P, P], BF16)
        ternary1 = sb("ternary1", [P, DK, F], BF16)
        ternary2 = sb("ternary2", [P, FC, D], BF16)
        convs = sb("convs", [P, FC, 4])
        wstat = sb("wstat", [P, 2])
        wmean = sb("wmean", [P, 2])
        wscale = sb("wscale", [P, 2])
        gate_up = sb("gate_up", [P, E, DK, 2 * HI])
        down = sb("down", [P, E, D])
        router = sb("router", [P, DK, E])
        rbias = sb("rbias", [P, E])

        xs = sb("xs", [P, NT, D])
        xTb = [sb(f"xTb{n}", [P, DK, S]) for n in range(2)]
        w1b = [sb(f"w1b{n}", [P, DK, A0]) for n in range(2)]
        w2b = [sb(f"w2b{n}", [A0 + 1, D]) for n in range(2)]
        b1b = [sb(f"b1b{n}", [A0, 1]) for n in range(2)]
        ga0 = [sb(f"ga0_{n}", [P, D]) for n in range(2)]
        be0 = [sb(f"be0_{n}", [P, D]) for n in range(2)]
        hT = sb("hT", [A0 + 1, S])
        ya = sb("ya", [P, TB, D])
        bn_a = sb("bn_a", [P, TB, 6])
        mv_a = sb("mv_a", [P, TB, 2])
        rstd_a = sb("rstd_a", [P, TB])
        q1 = sb("q1", [P, 4, TB])
        za = sb("za", [P, TB, D])
        rb = sb("rb", [P, TB, P])
        qT = [sb(f"qT{n}", [P, DK, S], BF16) for n in range(2)]
        deq_bc = [sb(f"deq_bc{n}", [P, S]) for n in range(2)]
        gb = [sb(f"gb{n}", [P, 2, S + 2]) for n in range(2)]
        cb = [sb(f"cb{n}", [P, 2, S]) for n in range(2)]
        sbuf_s = [sb(f"act{n}", [P, FC, S]) for n in range(2)]
        q2 = sb("q2", [P, 4, TB])
        zb = sb("zb", [P, TB, F])
        q2T = sb("q2T", [P, FC, S], BF16)

        wdn = [sb(f"wdn{n}", [P, DK, A1]) for n in range(2)]
        wup = [sb(f"wup{n}", [P, D]) for n in range(2)]
        bdn = [sb(f"bdn{n}", [P, 1]) for n in range(2)]
        bup = [sb(f"bup{n}", [P, D]) for n in range(2)]
        ga1 = [sb(f"ga1_{n}", [P, D]) for n in range(2)]
        be1 = [sb(f"be1_{n}", [P, D]) for n in range(2)]
        x1b = sb("x1b", [P, TB, D])
        x1T = sb("x1T", [P, DK, S])
        zk = sb("zk", [P, S])
        yk = sb("yk", [P, TB, D])
        bn_c = sb("bn_c", [P, TB, 6])
        mv_c = sb("mv_c", [P, TB, 2])
        rstd_c = sb("rstd_c", [P, TB])
        xf = sb("xf", [P, TB, D])
        xfT = sb("xfT", [P, DK, S])
        half = sb("half", [P, NT])

        lg = sb("lg", [P, NT, E])
        score = sb("score", [P, GT, E])
        choice = sb("choice", [P, GT, E])
        g_hi = sb("g_hi", [P, GT * GROUPS, 2])
        g_lo = sb("g_lo", [P, GT * GROUPS, 2])
        g_t = sb("g_t", [P, 3, GT * GROUPS])
        g_sum = sb("g_sum", [P, GT, GROUPS])
        g_gt = sb("g_gt", [P, GT, GROUPS, GROUPS])
        g_ge = sb("g_ge", [P, GT, GROUPS, GROUPS])
        g_first = sb("g_first", [P, GT, GROUPS, GROUPS])
        g_rank = sb("g_rank", [P, GT, GROUPS])
        g_mask = sb("g_mask", [P, GT, GROUPS])
        g_pen = sb("g_pen", [P, GT, GROUPS])
        masked = sb("masked", [P, GT, E])
        top8 = sb("top8", [P, GT, 8])
        idx8 = sb("idx8", [P, GT, 8], U32)
        idxf = sb("idxf", [P, GT, TOP_K])
        iota_e = sb("iota_e", [P, E])
        iota_region = sb("iota_region", [P, E])
        onehot = sb("onehot", [P, GT, TOP_K, E])
        picked = sb("picked", [P, GT, TOP_K, E])
        mask_b = sb("mask_b", [P, NT, E], BF16)
        wk = sb("wk", [P, GT, TOP_K])
        wsum = sb("wsum", [P, GT])
        pos = sb("pos", [P, GT, E])
        dest_f = sb("dest_f", [P, GT, TOP_K])
        dest = sb("dest", [P, NT, TOP_K], I32)
        slot_id = sb("slot_id", [P, NT, TOP_K], I32)
        rows = sb("rows", [P, RT, TOP_K, ROW])
        pad = sb("pad", [P, ROW])
        cnt = sb("cnt", [1, 4, E])
        cnt_i = sb("cnt_i", [1, E], I32)
        zrow = sb("zrow", [1, E])
        tj = sb("tj", [1, TILES])
        t_mask, t_prod = (sbuf_s[n][0:1, :, :].rearrange("a c t -> a (c t)")[:, 0:TILES * E].rearrange(
            "a (t e) -> a t e", e=E) for n in range(2))
        t_f = sb("t_f", [1, 3, TILES])
        t_exp = sb("t_exp", [1, 2 + TILES], I32)
        t_row = sb("t_row", [1, TILES], I32)

        xr = [sbuf_s[n // 4][:, 2 * (n % 4):2 * (n % 4) + 2, :].rearrange("p a b -> p (a b)")[:, 0:ROW] for n in range(RING)]
        yr = [zb[:, n // 4, (n % 4) * D:(n % 4 + 1) * D] for n in range(RING)]
        xTe = [x1T[:, :, n * P:(n + 1) * P] for n in range(2)]
        sg = [yk[:, n, 0:HI] for n in range(2)]
        he = [ya[:, n, 0:HI] for n in range(2)]
        hTe = [za[:, n, 0:HI] for n in range(2)]
        home = sb("home", [P, RING], I32)
        slots = [rows[:, 2 * n:2 * n + 1, :, 0:D] for n in range(4)]

        s_const = sem("s_const"); s_ident = sem("s_ident"); s_iota = sem("s_iota")
        s_w1 = sem("s_w1"); s_w2 = sem("s_w2"); s_small = sem("s_small"); s_ew = sem("s_ew")
        s_x = [sem(f"s_in{n}") for n in range(2)]
        s_p0 = [sem(f"s_p0_{n}") for n in range(2)]
        s_p1 = [sem(f"s_p1_{n}") for n in range(2)]
        s_dve = sem("s_dve")
        s_wsum = sem("s_wsum"); s_wtot = sem("s_wtot"); s_tern = sem("s_tern")
        s_hT = sem("s_hT"); s_hr = sem("s_hr"); s_ya = sem("s_ya"); s_mva = sem("s_mva")
        s_rsa = sem("s_rsa"); s_q1 = sem("s_q1"); s_za = sem("s_za"); s_rb = sem("s_rb")
        s_zaT = sem("s_zaT"); s_qT = sem("s_qT"); s_rbT = sem("s_rbT"); s_deq = sem("s_deq")
        s_h = sem("s_h"); s_g = sem("s_g"); s_c0 = sem("s_c0"); s_tap = sem("s_tap"); s_silu = sem("s_silu")
        s_sT = sem("s_sT"); s_q2 = sem("s_q2"); s_zb = sem("s_zb"); s_zbT = sem("s_zbT")
        s_q2T = sem("s_q2T"); s_y2 = sem("s_y2"); s_x1 = sem("s_x1")
        s_x1b = sem("s_x1b"); s_x1T = sem("s_x1T"); s_x1Te = sem("s_x1Te"); s_zk = sem("s_zk")
        s_zr = sem("s_zr"); s_yk = sem("s_yk"); s_mvc = sem("s_mvc"); s_rsc = sem("s_rsc")
        s_xf = sem("s_xf"); s_xfT = sem("s_xfT"); s_xfTe = sem("s_xfTe"); s_rows = sem("s_rows")
        s_lgp = sem("s_lgp"); s_lg = sem("s_lg"); s_pool = sem("s_pool")
        s_score = sem("s_score"); s_route = sem("s_route"); s_mask = sem("s_mask"); s_pre = sem("s_pre"); s_dest = sem("s_dest")
        s_cnt = sem("s_cnt"); s_table = sem("s_table"); s_padr = sem("s_padr")
        s_sent = [sem(f"s_sent{n}") for n in range(RT)]
        s_pad = sem("s_pad")
        s_xr = [sem(f"s_xr{n}") for n in range(RING)]
        s_back = [sem(f"s_back{n}") for n in range(RING)]
        e_xT = sem("e_xT"); e_xTc = sem("e_xTc"); e_gu = sem("e_gu"); e_sg = sem("e_sg")
        e_h = sem("e_h"); e_hT = sem("e_hT"); e_hTc = sem("e_hTc"); e_y = sem("e_y"); e_yc = sem("e_yc"); e_turn = sem("e_turn")
        e_home = sem("e_home")
        s_slots = [sem(f"s_slots{n}") for n in range(4)]
        s_sum = sem("s_sum"); s_out = [sem(f"s_out{n}") for n in range(4)]

        N_P0 = 6 * 16
        N_P1 = 6 * 16
        N_CONST = 8 + GROUPS - 1

        def seq(b):
            return b // 2 + 1

        def registers(eng, table, first, count, most):
            return nc.values_load_multi_w_load_instructions(
                table[0:1, bass.ds(first, count)], engines=(eng.engine,), min_val=0, max_val=most)[1]

        def run(stage, b, *part):
            if 0 <= b < NB:
                stage(b, *part)

        def run_group(stage, b, *part):
            for h, (_, hi) in enumerate(ROUTE):
                if b == hi - 1:
                    stage(h, *part)

        def tiles_of(h):
            return TB * ROUTE[h][0], TB * ROUTE[h][1]

        def send_padding(eng, first):
            eng.wait_ge(s_padr, 1)
            eng.wait_ge(s_cnt, 1)
            for e, c in enumerate(registers(eng, cnt_i, 0, E, TOK)):
                if e % 2 == first:
                    eng.dma_start(sent[bass.ds(c + e * REGION, P), :], pad[:]).then_inc(s_pad, 16)

        block = ctx.enter_context(nc.Block())

        @block.sync
        def _(sp):
            def load_layer0(b):
                n = b % 2
                if b >= 2:
                    sp.wait_ge(s_ya, b - 1)
                    sp.wait_ge(s_q1, b - 1)
                sp.dma_start(xTb[n][:], xT[:, b * S:(b + 1) * S].rearrange("(k p) t -> p k t", p=P)).then_inc(s_x[n], 16)
                sp.dma_start(xs[:, TB * b:TB * b + TB, :], x[b].rearrange("(j p) d -> p j d", p=P)).then_inc(s_x[n], 16)
                r = sp.value_load(id0[0:1, b:b + 1], min_val=0, max_val=l0_w1.shape[0] - 1)
                one = bass.ds(r, 1)
                sp.dma_start(w1b[n][:], l0_w1[one].rearrange("a (k p) n -> p (a k) n", p=P)).then_inc(s_p0[n], 16)
                sp.dma_start(w2b[n][:], l0_w2b2[one].rearrange("a k n -> (a k) n")).then_inc(s_p0[n], 16)
                sp.dma_start(b1b[n][:], l0_b1[one].rearrange("a n -> n a")).then_inc(s_p0[n], 16)
                sp.dma_start(ga0[n][:], l0_gamma[one].rearrange("a n -> (a n)").partition_broadcast(P)).then_inc(s_p0[n], 16)
                sp.dma_start(be0[n][:], l0_beta[one].rearrange("a n -> (a n)").partition_broadcast(P)).then_inc(s_p0[n], 32)

            def load_layer1(b):
                n = b % 2
                if b >= 2:
                    sp.wait_ge(s_yk, b - 1)
                    sp.wait_ge(s_xf, b - 1)
                    sp.wait_ge(s_x1b, b - 1)
                r = sp.value_load(id1[0:1, b:b + 1], min_val=0, max_val=l1_down.shape[0] - 1)
                one = bass.ds(r, 1)
                sp.dma_start(wdn[n][:], l1_down[one].rearrange("a (k p) n -> p (a k) n", p=P)).then_inc(s_p1[n], 16)
                sp.dma_start(wup[n][:], l1_up[one].rearrange("a k n -> (a k) n")).then_inc(s_p1[n], 16)
                sp.dma_start(bdn[n][:], l1_down_b[one].rearrange("a n -> n a")).then_inc(s_p1[n], 16)
                sp.dma_start(bup[n][:], l1_up_b[one].rearrange("a n -> (a n)").partition_broadcast(P)).then_inc(s_p1[n], 16)
                sp.dma_start(ga1[n][:], l1_gamma[one].rearrange("a n -> (a n)").partition_broadcast(P)).then_inc(s_p1[n], 16)
                sp.dma_start(be1[n][:], l1_beta[one].rearrange("a n -> (a n)").partition_broadcast(P)).then_inc(s_p1[n], 16)

            load_layer0(0)
            sp.dma_start(zb[:, :, :].rearrange("p a b -> p (a b)"),
                         w1T.rearrange("(k p) f -> p k f", p=P)).then_inc(s_w1, 16)
            sp.dma_start(convs[:], conv).then_inc(s_small, 16)
            sp.dma_start(sbuf_s[1][:], w2T.rearrange("(c p) d -> p c d", p=P)).then_inc(s_w2, 16)
            sp.dma_start(router[:], routerT.rearrange("(k p) e -> p k e", p=P)).then_inc(s_small, 16)
            sp.dma_start(rbias[:], router_bias.partition_broadcast(P)).then_inc(s_small, 16)
            load_layer0(1)
            load_layer1(0)
            load_layer1(1)
            sp.dma_start(gate_up[:], gate_upT.rearrange("e (k p) n -> p e k n", p=P)).then_inc(s_ew, 16)
            sp.dma_start(down[:], downT).then_inc(s_ew, 16)
            for i in range(2, NB + 3):
                if i < NB:
                    load_layer0(i)
                if 2 <= i - 3:
                    load_layer1(i - 3)
            sp.wait_ge(s_padr, 1)
            sp.dma_start(sent[E * REGION:E * REGION + P, :], pad[:]).then_inc(s_pad, 16)
            send_padding(sp, 0)
            sp.wait_ge(s_pad, 16 * (E + 1))
            for n in range(RT):
                sp.wait_ge(s_sent[n], NT // RT * TOP_K * 16)
            sp.wait_ge(s_table, 1)

            def load_tile(u, row):
                sp.dma_start(xr[u], sent[bass.ds(row, P), :]).then_inc(s_xr[u], 16)

            for u, row in enumerate(registers(sp, t_row, 0, RING, E * REGION)):
                load_tile(u, row)
            with sp.Fori(1, TILES // RING) as i:
                for u, row in enumerate(registers(sp, t_row, i * RING, RING, E * REGION)):
                    sp.wait_ge(e_home, (i - 1) * RING + u + 1)
                    load_tile(u, row)
            for u in range(RING):
                sp.wait_ge(s_back[u], 16 * (TILES // RING))
            for t in range(NT):
                if t >= 4:
                    sp.wait_ge(s_sum, t - 3)
                sp.dma_start(slots[t % 4], done[TOP_K * P * t:TOP_K * P * (t + 1), :].rearrange(
                    "(p a k) d -> p a k d", k=TOP_K, a=1)).then_inc(s_slots[t % 4], 16)
            for n in range(4):
                sp.wait_ge(s_out[n], 16 * (NT // 4))

        @block.gpsimd
        def _(pool):
            chain = [0]

            def link(ins):
                chain[0] += 1
                ins.then_inc(s_pool, 1)
                pool.wait_ge(s_pool, chain[0])

            pool.memset(ones[:], 1.0).then_inc(s_const, 1)
            pool.memset(gb[0][:], 0.0).then_inc(s_const, 1)
            pool.memset(gb[1][:], 0.0).then_inc(s_const, 1)
            pool.memset(hT[:], 1.0).then_inc(s_const, 1)
            pool.memset(ones_b[:], 1.0).then_inc(s_const, 1)
            pool.memset(half[:], -0.5).then_inc(s_const, 1)
            pool.memset(zrow[:], 0.0).then_inc(s_const, 1)
            pool.memset(t_exp[:], 0).then_inc(s_const, 1)
            link(pool.memset(ident[:], 0.0))
            pool.affine_select(out=ident[:], in_=ident[:], compare_op=ALU.not_equal, fill=1.0, base=0,
                               pattern=[[-1, P]], channel_multiplier=1).then_inc(s_ident, 1)
            link(pool.memset(before[:], 0.0))
            pool.affine_select(out=before[:], in_=before[:], compare_op=ALU.is_ge, fill=1.0, base=0,
                               pattern=[[-1, P]], channel_multiplier=1).then_inc(s_ident, 1)
            link(pool.memset(g_first[:], 0.0))
            for g in range(GROUPS):
                if g:
                    pool.memset(g_first[:, :, g, 0:g], 1.0).then_inc(s_const, 1)
            pool.iota(iota_e[:], pattern=[[1, E]], base=0, channel_multiplier=0,
                      allow_small_or_imprecise_dtypes=True).then_inc(s_iota, 1)
            pool.iota(iota_region[:], pattern=[[REGION, E]], base=0, channel_multiplier=0,
                      allow_small_or_imprecise_dtypes=True).then_inc(s_iota, 1)
            pool.iota(slot_id[:], pattern=[[P * TOP_K, NT], [1, TOP_K]], base=0,
                      channel_multiplier=TOP_K).then_inc(s_iota, 1)
            pool.iota(tj[:], pattern=[[1, TILES]], base=0, channel_multiplier=0,
                      allow_small_or_imprecise_dtypes=True).then_inc(s_iota, 1)
            link(pool.memset(pad[:], 0.0))
            pool.iota(pad[:, D:D + 1].bitcast(I32), pattern=[[0, 1]], base=TOK * TOP_K,
                      channel_multiplier=1).then_inc(s_padr, 1)

            def rstd(b, mv, out_, ready, signal):
                pool.wait_ge(ready, b + 1)
                link(pool.tensor_scalar(out_[:], mv[:, :, 1], LN_EPS, None, ALU.add))
                pool.tensor_tensor(out_[:], out_[:], half[:, 0:TB], op=ALU.pow).then_inc(signal, 1)

            def token_scales(b):
                pool.wait_ge(s_q1, b + 1)
                if b:
                    pool.wait_ge(s_rbT, b)
                for j in range(TB):
                    pool.tensor_scalar(rb[:, j, :], ones[:], q1[:, 2, j:j + 1], None, ALU.mult).then_inc(s_rb, 1)

            def residual_and_bias(b):
                pool.wait_ge(s_x1, TB * (b + 1))
                pool.wait_ge(s_p1[b % 2], N_P1 * seq(b))
                if b:
                    pool.wait_ge(s_yk, b)
                for j in range(TB):
                    ins = pool.tensor_tensor(x1b[:, j, :], xs[:, TB * b + j, :], bup[b % 2][:], op=ALU.add)
                ins.then_inc(s_x1b, 1)

            def send(h, k):
                lo, hi = tiles_of(h)
                if k >= hi - lo:
                    return
                t = lo + k
                pool.wait_ge(s_dest, h + 1)
                pool.wait_ge(s_rows, t + 1)
                for c in range(TOP_K):
                    pool.indirect_dma_start(
                        out=sent[:, :], in_=rows[:, t % RT, c, :], in_offset=None,
                        out_offset=bass.IndirectOffsetOnAxis(ap=dest[:, t, c:c + 1], axis=0),
                    ).then_inc(s_sent[t % RT], 16)

            for i in range(NB + 132):
                run_group(send, i - 68, 5)
                run_group(send, i - 66, 0)
                run(token_scales, i - 61)
                run_group(send, i - 52, 6)
                run(rstd, i - 64, mv_c, rstd_c, s_mvc, s_rsc)
                run_group(send, i - 132, 7)
                run_group(send, i - 67, 4)
                run_group(send, i - 66, 1)
                run_group(send, i - 66, 2)
                run(residual_and_bias, i - 63)
                run_group(send, i - 66, 3)
                run(rstd, i - 60, mv_a, rstd_a, s_mva, s_rsa)
            last_slot = pool.to_reg(TOK * TOP_K - 1)

            def give_back(n, u):
                pool.wait_ge(e_yc, n + 1)
                pool.sem_inc(e_turn, 1)
                pool.indirect_dma_start(
                    out=done[:, :], in_=yr[u], in_offset=None,
                    out_offset=bass.IndirectOffsetOnAxis(ap=home[:, u:u + 1], axis=0),
                    bounds_check=last_slot, oob_is_err=False).then_inc(s_back[u], 16)

            with pool.Fori(0, TILES // RING) as i:
                for u in range(RING):
                    give_back(i * RING + u, u)

        @block.tensor
        def _(pe):
            pe.wait_ge(s_const, N_CONST)
            pe.wait_ge(s_ident, 2)

            def weight_sums():
                pe.wait_ge(s_wsum, 2)
                pe.matmul(p_pair[0][:, 0:2], ones[:], wstat[:], start=True, stop=True).then_inc(s_wtot, 1)

            p_tok_use = {"sequence": None, "places": 0}

            def adapter0_hidden(b):
                pe.wait_ge(s_x[b % 2], 32 * seq(b))
                pe.wait_ge(s_p0[b % 2], N_P0 * seq(b))
                if b:
                    pe.wait_ge(s_deq, b)
                for k in range(DK):
                    ins = pe.matmul(p_a[0:A0, 0:S], w1b[b % 2][:, k, :], xTb[b % 2][:, k, :],
                                    start=k == 0, stop=k == DK - 1)
                ins.then_inc(s_hT, 1)

            def adapter0_out(b):
                pe.wait_ge(s_hr, b + 1)
                for j in range(TB):
                    pe.matmul(p_a[:, j * D:(j + 1) * D], ident[:], xs[:, TB * b + j, :], start=True, stop=False)
                    ins = pe.matmul(p_a[:, j * D:(j + 1) * D], hT[:, j * P:(j + 1) * P], w2b[b % 2][:],
                                    start=False, stop=True)
                ins.then_inc(s_ya, 1)

            def adapter0_quant(b):
                pe.wait_ge(s_za, TB * (b + 1))
                for k in range(DK):
                    for j in range(TB):
                        ins = pe.transpose(p_a[:, k * S + j * P:k * S + (j + 1) * P], za[:, j, k * P:(k + 1) * P], ident[:])
                ins.then_inc(s_zaT, 1)

            def token_scales(b):
                pe.wait_ge(s_qT, b + 1)
                pe.wait_ge(s_rb, TB * (b + 1))
                for j in range(TB):
                    ins = pe.transpose(p_a[:, j * P:(j + 1) * P], rb[:, j, :], ident[:])
                ins.then_inc(s_rbT, 1)

            def up_pair(b, p):
                m = NP * b + p
                if p == 0:
                    pe.wait_ge(s_tern, 1)
                    pe.wait_ge(s_qT, b + 1)
                if m >= 2:
                    pe.wait_ge(s_g, m - 1)
                for c in range(2):
                    ch = (2 * p + c) * P
                    for k in range(DK):
                        ins = pe.matmul(p_pair[m % 2][:, c * S:(c + 1) * S], ternary1[:, k, ch:ch + P],
                                        qT[b % 2][:, k, :], start=k == 0, stop=k == DK - 1)
                ins.then_inc(s_h, 1)

            def hidden_by_token(b, j):
                pe.wait_ge(s_silu, NP * (b + 1))
                if b:
                    pe.wait_ge(s_x1, TB * (b - 1) + j + 1)
                if j == 0:
                    if p_tok_use["places"]:
                        pe.wait_ge(s_dest, p_tok_use["places"])
                    p_tok_use["sequence"] = b
                for c in range(FC):
                    ins = pe.transpose(p_tok[:, j * F + c * P:j * F + (c + 1) * P],
                                       sbuf_s[b % 2][:, c, j * P:(j + 1) * P], ident[:])
                ins.then_inc(s_sT, 1)

            def quant_by_channel(b, j):
                pe.wait_ge(s_zb, TB * b + j + 1)
                for c in range(FC):
                    ins = pe.transpose(p_tok[:, j * F + c * P:j * F + (c + 1) * P], zb[:, j, c * P:(c + 1) * P], ident[:])
                ins.then_inc(s_zbT, 1)

            def ffn_out(b, j):
                pe.wait_ge(s_q2T, TB * b + j + 1)
                pe.wait_ge(s_tern, 2)
                for c in range(FC):
                    ins = pe.matmul(p_tok[:, j * F:j * F + D], q2T[:, c, j * P:(j + 1) * P], ternary2[:, c, :],
                                    start=c == 0, stop=c == FC - 1)
                ins.then_inc(s_y2, 1)

            def adapter1_in(b):
                pe.wait_ge(s_x1, TB * (b + 1))
                if b:
                    pe.wait_ge(s_lg, b)
                for k in range(DK):
                    for j in range(TB):
                        ins = pe.transpose(p_c[:, k * S + j * P:k * S + (j + 1) * P],
                                           xs[:, TB * b + j, k * P:(k + 1) * P], ident[:])
                ins.then_inc(s_x1T, 1)

            def adapter1_hidden(b):
                pe.wait_ge(s_x1Te, b + 1)
                pe.wait_ge(s_p1[b % 2], N_P1 * seq(b))
                for k in range(DK):
                    ins = pe.matmul(p_c[:, 0:S], wdn[b % 2][:, k, :], x1T[:, k, :], start=k == 0, stop=k == DK - 1)
                ins.then_inc(s_zk, 1)

            def adapter1_out(b):
                pe.wait_ge(s_zr, b + 1)
                pe.wait_ge(s_x1b, b + 1)
                for j in range(TB):
                    pe.matmul(p_c[:, j * D:(j + 1) * D], ident[:], x1b[:, j, :], start=True, stop=False)
                    ins = pe.matmul(p_c[:, j * D:(j + 1) * D], zk[:, j * P:(j + 1) * P], wup[b % 2][:],
                                    start=False, stop=True)
                ins.then_inc(s_yk, 1)

            def normed_by_width(b):
                pe.wait_ge(s_xf, b + 1)
                for k in range(DK):
                    for j in range(TB):
                        ins = pe.transpose(p_c[:, k * S + j * P:k * S + (j + 1) * P], xf[:, j, k * P:(k + 1) * P], ident[:])
                ins.then_inc(s_xfT, 1)

            def logits(b):
                pe.wait_ge(s_xfTe, b + 1)
                if b == 0:
                    pe.wait_ge(s_small, 48)
                for j in range(TB):
                    for k in range(DK):
                        ins = pe.matmul(p_c[:, j * E:(j + 1) * E], xfT[:, k, j * P:(j + 1) * P], router[:, k, :],
                                        start=k == 0, stop=k == DK - 1)
                ins.then_inc(s_lgp, 1)

            def places(h):
                lo, hi = tiles_of(h)
                n = hi - lo
                pe.wait_ge(s_mask, h + 1)
                pe.wait_ge(s_x1, TB * p_tok_use["sequence"] + 1)
                p_tok_use["places"] = h + 1
                pe.matmul(p_tok[:, 0:n * E], before[:], mask_b[:, lo:hi, :], start=True, stop=False,
                          skip_group_check=True)
                for t in range(hi - 1):
                    first = max(t + 1, lo)
                    ins = pe.matmul(p_tok[:, (first - lo) * E:n * E], ones_b[:],
                                    mask_b[:, t:t + 1, :].to_broadcast([P, hi - first, E]),
                                    start=False, stop=t == hi - 2, skip_group_check=True)
                if hi == NT:
                    for t in range(NT):
                        ins = pe.matmul(p_tok[:, n * E:n * E + E], ones_b[:], mask_b[:, t, :],
                                        start=t == 0, stop=t == NT - 1)
                ins.then_inc(s_pre, 1)

            for i in range(NB + 26):
                run(ffn_out, i - 24, 0)
                run(token_scales, i - 22)
                run(up_pair, i - 22, 0)
                run(quant_by_channel, i - 24, 1)
                run(up_pair, i - 22, 1)
                run(adapter0_hidden, i - 21)
                run(ffn_out, i - 24, 1)
                run(up_pair, i - 22, 2)
                run_group(places, i - 26)
                run(hidden_by_token, i - 23, 0)
                run(normed_by_width, i - 25)
                run(adapter0_out, i - 21)
                if i == 21:
                    weight_sums()
                run(hidden_by_token, i - 23, 1)
                run(logits, i - 25)
                run(up_pair, i - 22, 3)
                run(adapter1_in, i - 24)
                run(quant_by_channel, i - 23, 0)
                run(adapter1_hidden, i - 24)
                run(adapter1_out, i - 24)
                run(adapter0_quant, i - 21)
            pe.wait_ge(s_ew, 32)
            pe.wait_ge(s_table, 1)

            def x_by_width(n, u):
                pe.wait_ge(s_xr[u], 16 * (n // RING + 1) if isinstance(n, int) else (n - u) * (16 // RING) + 16)
                if not (isinstance(n, int) and n < 2):
                    pe.wait_ge(e_xTc, n - 1)
                for k in range(DK):
                    ins = pe.transpose(p_pair[u % 2][:, k * P:(k + 1) * P], xr[u][:, k * P:(k + 1) * P], ident[:])
                ins.then_inc(e_xT, 1)

            def gate_and_up(n, u, e):
                pe.wait_ge(e_xTc, n + 1)
                if not (isinstance(n, int) and n < 2):
                    pe.wait_ge(e_h, n - 1)
                for k in range(DK):
                    ins = pe.matmul(p_tok[:, u % 2 * 512:u % 2 * 512 + 2 * HI], xTe[u % 2][:, k, :],
                                    gate_up[:, bass.ds(e, 1), k, :], start=k == 0, stop=k == DK - 1)
                ins.then_inc(e_gu, 1)

            def hidden_by_width(n, u):
                pe.wait_ge(e_h, n + 1)
                if not (isinstance(n, int) and n < 2):
                    pe.wait_ge(e_hTc, n - 1)
                pe.transpose((p_a, p_c)[u % 2][:, 0:P], he[u % 2], ident[:]).then_inc(e_hT, 1)

            def expert_out(n, u, e):
                pe.wait_ge(e_hTc, n + 1)
                if not (isinstance(n, int) and n < 2):
                    pe.wait_ge(e_yc, n - 1)
                pe.matmul(p_tok[:, 1024 + u % 2 * 512:1024 + u % 2 * 512 + D], hTe[u % 2],
                          down[:, bass.ds(e, 1), :], start=True, stop=True).then_inc(e_y, 1)

            def step(n, u, e, last=False):
                if not (last and n + 1 >= TILES):
                    x_by_width(n + 1, (u + 1) % RING)
                if not (last and n >= TILES):
                    gate_and_up(n, u, e[u + 2])
                if not (isinstance(n, int) and (n < 1 or n > TILES)):
                    hidden_by_width(n - 1, (u - 1) % RING)
                if not (isinstance(n, int) and n < 2):
                    expert_out(n - 2, (u - 2) % RING, e[u])

            x_by_width(0, 0)
            e = registers(pe, t_exp, 0, RING + 2, E - 1)
            for n in range(RING):
                step(n, n, e)
            with pe.Fori(1, TILES // RING - 1) as i:
                e = registers(pe, t_exp, i * RING, RING + 2, E - 1)
                for u in range(RING):
                    step(i * RING + u, u, e)
            e = registers(pe, t_exp, TILES - RING, RING + 2, E - 1)
            for n in range(TILES - RING, TILES):
                step(n, n % RING, e, last=True)
            for u in range(2):
                step(TILES + u, u, e[RING:], last=True)

        @block.scalar
        def _(act):
            def copy(o, i_):
                return act.activation(o, i_, ACT.Copy)

            def conv_centre(b, p):
                m = NP * b + p
                act.wait_ge(s_g, m + 1)
                if m == 0:
                    act.wait_ge(s_small, 48)
                if m >= 2:
                    act.wait_ge(s_silu, m - 1)
                for c in range(2):
                    ch = 2 * p + c
                    ins = act.activation(cb[m % 2][:, c, :], gb[m % 2][:, c, 1:S + 1], ACT.Identity,
                                         bias=convs[:, ch, 3:4], scale=convs[:, ch, 1:2])
                ins.then_inc(s_c0, 1)

            def silu(b, p):
                m = NP * b + p
                act.wait_ge(s_tap, m + 1)
                if p == 0 and b >= 2:
                    act.wait_ge(s_sT, TB * (b - 1))
                if m == NP:
                    act.wait_ge(s_tern, 2)
                act.activation(sbuf_s[b % 2][:, 2 * p:2 * p + 2, :], cb[m % 2][:], ACT.Silu).then_inc(s_silu, 1)

            def adapter0_relu(b):
                act.wait_ge(s_hT, b + 1)
                act.activation(hT[0:A0, :], p_a[0:A0, 0:S], ACT.Relu, bias=b1b[b % 2][:, 0:1]).then_inc(s_hr, 1)

            def adapter0_round(b):
                act.wait_ge(s_q1, b + 1)
                if b:
                    act.wait_ge(s_zaT, b)
                for j in range(TB):
                    act.activation(za[:, j, :], ya[:, j, :], ACT.Identity,
                                   bias=MAGIC, scale=q1[:, 1, j:j + 1]).then_inc(s_za, 1)

            def adapter0_integers(b):
                act.wait_ge(s_zaT, b + 1)
                if b >= 2:
                    act.wait_ge(s_h, NP * (b - 1))
                act.activation(qT[b % 2][:].rearrange("p k t -> p (k t)"), p_a[:, :], ACT.Identity,
                               bias=-MAGIC).then_inc(s_qT, 1)

            def hidden_round(b, j):
                act.wait_ge(s_q2, TB * b + j + 1)
                if b:
                    act.wait_ge(s_zbT, TB * (b - 1) + j + 1)
                else:
                    act.wait_ge(s_tern, 1)
                act.activation(zb[:, j, :], p_tok[:, j * F:(j + 1) * F], ACT.Identity,
                               bias=MAGIC, scale=q2[:, 1, j:j + 1]).then_inc(s_zb, 1)

            def hidden_integers(b, j):
                act.wait_ge(s_zbT, TB * b + j + 1)
                if b:
                    act.wait_ge(s_y2, TB * (b - 1) + j + 1)
                act.activation(q2T[:, :, j * P:(j + 1) * P], p_tok[:, j * F:(j + 1) * F].rearrange("p (c t) -> p c t", c=FC),
                               ACT.Identity, bias=-MAGIC).then_inc(s_q2T, 1)

            def adapter1_x(b):
                act.wait_ge(s_x1T, b + 1)
                copy(x1T[:].rearrange("p k t -> p (k t)"), p_c[:, :]).then_inc(s_x1Te, 1)

            def adapter1_relu(b):
                act.wait_ge(s_zk, b + 1)
                act.activation(zk[:], p_c[:, 0:S], ACT.Relu, bias=bdn[b % 2][:, 0:1]).then_inc(s_zr, 1)

            def normed_by_width(b):
                act.wait_ge(s_xfT, b + 1)
                copy(xfT[:].rearrange("p k t -> p (k t)"), p_c[:, :]).then_inc(s_xfTe, 1)

            def normed_rows(b, j):
                act.wait_ge(s_xf, b + 1)
                t = TB * b + j
                if t >= RT:
                    act.wait_ge(s_sent[t % RT], t // RT * TOP_K * 16)
                copy(rows[:, t % RT, :, 0:D], xf[:, j:j + 1, :].to_broadcast([P, TOP_K, D])).then_inc(s_rows, 1)

            def scores(h):
                lo, hi = tiles_of(h)
                act.wait_ge(s_lg, ROUTE[h][1])
                if h:
                    act.wait_ge(s_route, h)
                act.activation(score[:, 0:hi - lo, :], lg[:, lo:hi, :], ACT.Sigmoid).then_inc(s_score, 1)

            for i in range(NB + 10):
                run(normed_by_width, i - 10)
                run(normed_rows, i - 10, 1)
                run(conv_centre, i - 7, 1)
                run(silu, i - 7, 0)
                run(hidden_round, i - 8, 0)
                run_group(scores, i - 10)
                run(adapter1_x, i - 9)
                run(conv_centre, i - 7, 2)
                run(adapter1_relu, i - 9)
                run(silu, i - 7, 1)
                run(hidden_integers, i - 8, 0)
                run(adapter0_round, i - 6)
                run(adapter0_integers, i - 6)
                run(hidden_round, i - 8, 1)
                run(conv_centre, i - 7, 3)
                run(silu, i - 7, 2)
                run(hidden_integers, i - 8, 1)
                run(conv_centre, i - 6, 0)
                run(adapter0_relu, i - 5)
                run(silu, i - 7, 3)
                run(normed_rows, i - 9, 0)
            send_padding(act, 1)

            def x_copy(n, u):
                act.wait_ge(e_xT, n + 1)
                if not (isinstance(n, int) and n < 2):
                    act.wait_ge(e_gu, n - 1)
                copy(xTe[u % 2], p_pair[u % 2][:, 0:D].rearrange("p (k t) -> p k t", k=DK)).then_inc(e_xTc, 1)

            def gate(n, u):
                act.wait_ge(e_gu, n + 1)
                if not (isinstance(n, int) and n < 2):
                    act.wait_ge(e_h, n - 1)
                act.activation(sg[u % 2], p_tok[:, u % 2 * 512:u % 2 * 512 + HI], ACT.Silu).then_inc(e_sg, 1)

            x_copy(0, 0)
            for n in range(RING):
                x_copy(n + 1, (n + 1) % RING)
                gate(n, n)
            with act.Fori(1, TILES // RING - 1) as i:
                for u in range(RING):
                    x_copy(i * RING + u + 1, (u + 1) % RING)
                    gate(i * RING + u, u)
            for n in range(TILES - RING, TILES):
                if n + 1 < TILES:
                    x_copy(n + 1, (n + 1) % RING)
                gate(n, n % RING)
            for t in range(NT):
                act.wait_ge(s_sum, t + 1)
                act.dma_start(out[t // TB, t % TB * P:(t % TB + 1) * P, :], xs[:, t, :]).then_inc(s_out[t % 4], 16)

        @block.vector
        def _(dve):
            chain = [0]

            def mark(ins):
                chain[0] += 1
                ins.then_inc(s_dve, 1)
                return chain[0]

            def link(ins):
                dve.wait_ge(s_dve, mark(ins))

            w1f = zb[:, :, :].rearrange("p a b -> p (a b)")
            w2f = sbuf_s[1][:, :, :].rearrange("p a b -> p (a b)")

            def weight_means():
                dve.wait_ge(s_w1, 16)
                dve.tensor_reduce(wstat[:, 0:1], w1f, AX_X, ALU.add, apply_absolute_value=True).then_inc(s_wsum, 1)
                dve.wait_ge(s_w2, 16)
                dve.tensor_reduce(wstat[:, 1:2], w2f, AX_X, ALU.add, apply_absolute_value=True).then_inc(s_wsum, 1)
                dve.wait_ge(s_wtot, 1)
                link(dve.tensor_scalar(wmean[:], p_pair[0][:, 0:2], 1.0 / (F * D), QUANT_MIN, ALU.mult, ALU.max))
                link(dve.reciprocal(wscale[:], wmean[:]))

            def ternary(n, w, o):
                link(dve.tensor_scalar(w, w, wscale[:, n:n + 1], 1.0, ALU.mult, ALU.min))
                link(dve.tensor_scalar(w, w, -1.0, MAGIC, ALU.max, ALU.add))
                dve.tensor_scalar(o[:].rearrange("p a b -> p (a b)"), w, MAGIC, None, ALU.subtract).then_inc(s_tern, 1)

            def stats(y, bn, mv, ready):
                for j in range(TB):
                    n = mark(dve.bn_stats(bn[:, j, :], y[:, j * D:(j + 1) * D]))
                dve.wait_ge(s_dve, n)
                for j in range(TB):
                    ins = dve.bn_aggr(mv[:, j, :], bn[:, j, :])
                ins.then_inc(ready, 1)

            def norm(x_, y, o, mv, rs, ga, be):
                for j in range(TB):
                    n = mark(dve.scalar_tensor_tensor(y[:, j, :], x_[:, j * D:(j + 1) * D], mv[:, j, 0:1], ga[:],
                                                      ALU.subtract, ALU.mult))
                dve.wait_ge(s_dve, n)
                for j in range(TB):
                    ins = dve.scalar_tensor_tensor(o[:, j, :], y[:, j, :], rs[:, j:j + 1], be[:], ALU.mult, ALU.add)
                return ins

            def scales(q, w_mean, signal):
                link(dve.tensor_scalar(q[:, 3, :], q[:, 0, :], QUANT_MIN, 1.0 / QMAX, ALU.max, ALU.mult))
                dve.tensor_scalar(q[:, 2, :], q[:, 3, :], w_mean, None, ALU.mult)
                dve.reciprocal(q[:, 1, :], q[:, 3, :]).then_inc(signal, 1)

            def adapter0_stats(b):
                dve.wait_ge(s_ya, b + 1)
                if b:
                    dve.wait_ge(s_rsa, b)
                stats(p_a, bn_a, mv_a, s_mva)

            def adapter0_norm(b):
                dve.wait_ge(s_rsa, b + 1)
                if b:
                    dve.wait_ge(s_za, TB * b)
                    dve.wait_ge(s_rb, TB * b)
                link(norm(p_a, ya, ya, mv_a, rstd_a, ga0[b % 2], be0[b % 2]))
                link(dve.tensor_reduce(q1[:, 0, :], ya[:], AX_X, ALU.max, apply_absolute_value=True))
                scales(q1, wmean[:, 0:1], s_q1)

            def token_scales(b):
                dve.wait_ge(s_rbT, b + 1)
                if b >= 2:
                    dve.wait_ge(s_g, NP * (b - 1))
                dve.tensor_copy(deq_bc[b % 2][:], p_a[:, 0:S]).then_inc(s_deq, 1)

            def dequant_pair(b, p):
                m = NP * b + p
                dve.wait_ge(s_h, m + 1)
                if m == 0:
                    dve.wait_ge(s_const, N_CONST)
                if m % NP == 0:
                    dve.wait_ge(s_deq, b + 1)
                if m >= 2:
                    dve.wait_ge(s_c0, m - 1)
                    dve.wait_ge(s_tap, m - 1)
                dve.tensor_tensor(gb[m % 2][:, :, 1:S + 1], p_pair[m % 2][:, :].rearrange("p (c t) -> p c t", c=2),
                                  deq_bc[b % 2][:].rearrange("p (a t) -> p a t", a=1).to_broadcast([P, 2, S]),
                                  ALU.mult).then_inc(s_g, 1)

            def conv_sides(b, p):
                m = NP * b + p
                dve.wait_ge(s_c0, m + 1)
                dve.wait_ge(s_g, m + 1)
                marks = []
                for c in range(2):
                    ch = 2 * p + c
                    marks.append(mark(dve.scalar_tensor_tensor(cb[m % 2][:, c, :], gb[m % 2][:, c, 0:S], convs[:, ch, 0:1],
                                                               cb[m % 2][:, c, :], ALU.mult, ALU.add)))
                for c in range(2):
                    ch = 2 * p + c
                    dve.wait_ge(s_dve, marks[c])
                    ins = dve.scalar_tensor_tensor(cb[m % 2][:, c, :], gb[m % 2][:, c, 2:S + 2], convs[:, ch, 2:3],
                                                   cb[m % 2][:, c, :], ALU.mult, ALU.add)
                ins.then_inc(s_tap, 1)

            def hidden_scales(b, j):
                q = q2[:, :, j:j + 1]
                dve.wait_ge(s_sT, TB * b + j + 1)
                if b:
                    dve.wait_ge(s_zb, TB * (b - 1) + j + 1)
                link(dve.tensor_reduce(q[:, 0, :], p_tok[:, j * F:(j + 1) * F], AX_X, ALU.max, apply_absolute_value=True))
                scales(q, wmean[:, 1:2], s_q2)

            def hidden_residual(b, j):
                dve.wait_ge(s_y2, TB * b + j + 1)
                t = TB * b + j
                dve.scalar_tensor_tensor(xs[:, t, :], p_tok[:, j * F:j * F + D], q2[:, 2, j:j + 1],
                                         xs[:, t, :], ALU.mult, ALU.add).then_inc(s_x1, 1)

            def adapter1_stats(b):
                dve.wait_ge(s_yk, b + 1)
                if b:
                    dve.wait_ge(s_rsc, b)
                stats(p_c, bn_c, mv_c, s_mvc)

            def adapter1_norm(b):
                dve.wait_ge(s_rsc, b + 1)
                if b:
                    dve.wait_ge(s_xfT, b)
                    dve.wait_ge(s_rows, TB * b)
                norm(p_c, yk, xf, mv_c, rstd_c, ga1[b % 2], be1[b % 2]).then_inc(s_xf, 1)

            def keep_logits(b):
                dve.wait_ge(s_lgp, b + 1)
                dve.tensor_copy(lg[:, TB * b:TB * b + TB, :].rearrange("p t e -> p (t e)"),
                                p_c[:, 0:TB * E]).then_inc(s_lg, 1)

            routed = (score, choice, g_sum, g_gt, g_ge, g_first, g_rank, g_mask, g_pen, masked, top8, idx8, idxf,
                      onehot, picked, wk, wsum)

            def choose(h):
                lo, hi = tiles_of(h)
                n_t = hi - lo
                (score_, choice_, g_sum_, g_gt_, g_ge_, g_first_, g_rank_, g_mask_, g_pen_, masked_, top8_, idx8_, idxf_,
                 onehot_, picked_, wk_, wsum_) = (a[:, 0:n_t] for a in routed)
                n_g = n_t * GROUPS
                dve.wait_ge(s_score, h + 1)
                if h == 0:
                    dve.wait_ge(s_iota, 4)
                    dve.wait_ge(s_small, 48)
                link(dve.tensor_tensor(choice_, score_, rbias[:].rearrange("p (a e) -> p a e", a=1).to_broadcast([P, n_t, E]), ALU.add))
                four = choice_.rearrange("p t (g a b) -> p (t g) a b", g=GROUPS, a=2)
                dve.tensor_tensor(g_hi[:, 0:n_g], four[:, :, :, 0], four[:, :, :, 1], ALU.max)
                link(dve.tensor_tensor(g_lo[:, 0:n_g], four[:, :, :, 0], four[:, :, :, 1], ALU.min))
                dve.tensor_tensor(g_t[:, 0, 0:n_g], g_hi[:, 0:n_g, 0], g_hi[:, 0:n_g, 1], ALU.max)
                dve.tensor_tensor(g_t[:, 1, 0:n_g], g_hi[:, 0:n_g, 0], g_hi[:, 0:n_g, 1], ALU.min)
                link(dve.tensor_tensor(g_t[:, 2, 0:n_g], g_lo[:, 0:n_g, 0], g_lo[:, 0:n_g, 1], ALU.max))
                link(dve.tensor_tensor(g_t[:, 1, 0:n_g], g_t[:, 1, 0:n_g], g_t[:, 2, 0:n_g], ALU.max))
                link(dve.tensor_tensor(g_sum_.rearrange("p t g -> p (t g)"), g_t[:, 0, 0:n_g], g_t[:, 1, 0:n_g], ALU.add))
                mine = g_sum_.rearrange("p t (g a) -> p t g a", a=1).to_broadcast([P, n_t, GROUPS, GROUPS])
                theirs = g_sum_.rearrange("p t (a g) -> p t a g", a=1).to_broadcast([P, n_t, GROUPS, GROUPS])
                dve.tensor_tensor(g_gt_, theirs, mine, ALU.is_gt)
                link(dve.tensor_tensor(g_ge_, theirs, mine, ALU.is_ge))
                link(dve.tensor_tensor(g_ge_, g_ge_, g_first_, ALU.mult))
                link(dve.tensor_tensor(g_ge_, g_ge_, g_gt_, ALU.max))
                link(dve.tensor_reduce(g_rank_, g_ge_, AX_X, ALU.add))
                link(dve.tensor_scalar(g_mask_, g_rank_, float(GROUPS_KEPT), None, ALU.is_lt))
                link(dve.tensor_scalar(g_pen_, g_mask_, -1.0, -NEG_INF, ALU.add, ALU.mult))
                per = E // GROUPS

                def wide(a):
                    return a.rearrange("p t (g a) -> p (t g) a", a=1).to_broadcast([P, n_g, per])

                flat = masked_.rearrange("p t (g a) -> p (t g) a", g=GROUPS)
                link(dve.tensor_tensor(flat, choice_.rearrange("p t (g a) -> p (t g) a", g=GROUPS), wide(g_mask_), ALU.mult))
                link(dve.tensor_tensor(flat, flat, wide(g_pen_), ALU.add))
                for t in range(n_t):
                    n = mark(dve.max(top8[:, t, :], masked[:, t, :]))
                dve.wait_ge(s_dve, n)
                for t in range(n_t):
                    n = mark(dve.max_index(idx8[:, t, :], top8[:, t, :], masked[:, t, :]))
                dve.wait_ge(s_dve, n)
                link(dve.tensor_copy(idxf_, idx8_[:, :, 0:TOP_K]))
                link(dve.tensor_tensor(onehot_, iota_e[:].rearrange("p (a b e) -> p a b e", a=1, b=1).to_broadcast([P, n_t, TOP_K, E]),
                                       idxf_.rearrange("p t (k a) -> p t k a", a=1).to_broadcast([P, n_t, TOP_K, E]), ALU.is_equal))
                with nc.allow_low_precision(reason="a sum that is 0 or 1 is exact in bfloat16"):
                    dve.tensor_reduce(mask_b[:, lo:hi, :], onehot_.rearrange("p t k e -> p t e k"), AX_X, ALU.add).then_inc(s_mask, 1)
                link(dve.tensor_tensor(picked_, onehot_, score_.rearrange("p t (a e) -> p t a e", a=1).to_broadcast([P, n_t, TOP_K, E]), ALU.mult))
                link(dve.tensor_reduce(wk_, picked_, AX_X, ALU.add))
                link(dve.tensor_reduce(wsum_, wk_, AX_X, ALU.add))
                link(dve.tensor_scalar(wsum_, wsum_, 1e-20, None, ALU.add))
                link(dve.reciprocal(wsum_, wsum_))
                dve.scalar_tensor_tensor(wk_, wk_, ROUTED_SCALE, wsum_.rearrange("p (t a) -> p t a", a=1).to_broadcast(
                    [P, n_t, TOP_K]), ALU.mult, ALU.mult).then_inc(s_route, 1)

            def destinations(h):
                lo, hi = tiles_of(h)
                n_t = hi - lo
                onehot_, picked_, pos_, dest_ = (a[:, 0:n_t] for a in (onehot, picked, pos, dest_f))
                dve.wait_ge(s_route, h + 1)
                for t in range(lo, hi):
                    if t >= RT:
                        dve.wait_ge(s_sent[t % RT], t // RT * TOP_K * 16)
                for t in range(lo, hi):
                    if t == lo or t % RT == 0:
                        to = min(hi, (t // RT + 1) * RT)
                        r = slice(t % RT, t % RT + to - t)
                        mark(dve.tensor_copy(rows[:, r, :, D + 1], wk[:, t - lo:to - lo, :]))
                        mark(dve.tensor_copy(rows[:, r, :, D].bitcast(I32), slot_id[:, t:to, :]))
                dve.wait_ge(s_pre, h + 1)
                if hi == NT:
                    expert_counts()
                link(dve.tensor_tensor(pos_, p_tok[:, 0:n_t * E].rearrange("p (t e) -> p t e", t=n_t),
                                       iota_region[:].rearrange("p (a e) -> p a e", a=1).to_broadcast([P, n_t, E]), ALU.add))
                link(dve.tensor_tensor(picked_, onehot_, pos_.rearrange("p t (a e) -> p t a e", a=1).to_broadcast(
                    [P, n_t, TOP_K, E]), ALU.mult))
                link(dve.tensor_reduce(dest_, picked_, AX_X, ALU.add))
                dve.tensor_copy(dest[:, lo:hi, :], dest_).then_inc(s_dest, 1)

            def expert_counts():
                lo, hi = tiles_of(-1)
                mark(dve.tensor_copy(cnt[:, 0, :], p_tok[0:1, (hi - lo) * E:(hi - lo) * E + E]))
                dve.tensor_copy(cnt_i[:], p_tok[0:1, (hi - lo) * E:(hi - lo) * E + E]).then_inc(s_cnt, 1)

            def tile_list():
                link(dve.tensor_scalar(cnt[:, 1, :], cnt[:, 0, :], 1.0 / P, 0.5 - 0.5 / P, ALU.mult, ALU.add))
                link(dve.tensor_scalar(cnt[:, 1, :], cnt[:, 1, :], MAGIC, None, ALU.add))
                link(dve.tensor_scalar(cnt[:, 1, :], cnt[:, 1, :], MAGIC, None, ALU.subtract))
                dve.tensor_scalar(cnt[:, 3, :], cnt[:, 1, :], -float(P), float(REGION), ALU.mult, ALU.add)
                link(dve.tensor_tensor_scan(cnt[:, 2, :], cnt[:, 1, :], zrow[:], 0.0, ALU.add, ALU.add))
                full = [1, TILES, E]
                link(dve.tensor_tensor(t_mask, tj[:].rearrange("p (t a) -> p t a", a=1).to_broadcast(full),
                                       cnt[:, 2:3, :].to_broadcast(full), ALU.is_ge))
                link(dve.tensor_reduce(t_f[:, 0, :], t_mask, AX_X, ALU.add))
                link(dve.tensor_scalar(t_f[:, 0, :], t_f[:, 0, :], float(E - 1), None, ALU.min))
                link(dve.tensor_tensor(t_prod, t_mask, cnt[:, 3:4, :].to_broadcast(full), ALU.mult))
                link(dve.tensor_reduce(t_f[:, 1, :], t_prod, AX_X, ALU.add))
                link(dve.scalar_tensor_tensor(t_f[:, 1, :], tj[:], float(P), t_f[:, 1, :], ALU.mult, ALU.add))
                link(dve.tensor_scalar(t_f[:, 1, :], t_f[:, 1, :], float(E * REGION), None, ALU.min))
                link(dve.tensor_copy(t_exp[:, 2:], t_f[:, 0, :]))
                dve.tensor_copy(t_row[:], t_f[:, 1, :]).then_inc(s_table, 1)

            for i in range(NB + 6):
                run(hidden_scales, i - 4, 1)
                run(dequant_pair, i - 3, 3)
                run(conv_sides, i - 3, 2)
                run(token_scales, i - 2)
                run_group(choose, i - 6)
                run(adapter1_stats, i - 5)
                run(hidden_residual, i - 4, 0)
                run(dequant_pair, i - 2, 0)
                run(conv_sides, i - 3, 3)
                if i == 3:
                    ternary(1, w2f, ternary2)
                run(adapter1_norm, i - 5)
                run_group(destinations, i - 6)
                run(dequant_pair, i - 2, 1)
                run(hidden_residual, i - 4, 1)
                run(conv_sides, i - 2, 0)
                run(hidden_scales, i - 3, 0)
                run(dequant_pair, i - 2, 2)
                run(adapter0_stats, i - 1)
                run(keep_logits, i - 5)
                run(conv_sides, i - 2, 1)
                if i == 1:
                    weight_means()
                run(adapter0_norm, i - 1)
                if i == 1:
                    ternary(0, w1f, ternary1)
            tile_list()

            def hidden(n, u):
                dve.wait_ge(e_sg, n + 1)
                dve.wait_ge(s_xr[u], 16 * (n // RING + 1) if isinstance(n, int) else (n - u) * (16 // RING) + 16)
                if not (isinstance(n, int) and n < 2):
                    dve.wait_ge(e_hT, n - 1)
                dve.scalar_tensor_tensor(he[u % 2], sg[u % 2], xr[u][:, D + 1:D + 2],
                                         p_tok[:, u % 2 * 512 + HI:u % 2 * 512 + 2 * HI], ALU.mult, ALU.mult).then_inc(e_h, 1)
                if not (isinstance(n, int) and n < RING):
                    dve.wait_ge(s_back[u], 16 * (n // RING) if isinstance(n, int) else (n - u) * (16 // RING))
                dve.tensor_copy(home[:, u:u + 1], xr[u][:, D:D + 1].bitcast(I32)).then_inc(e_home, 1)

            def hidden_copy(n, u):
                dve.wait_ge(e_hT, n + 1)
                if not (isinstance(n, int) and n < 2):
                    dve.wait_ge(e_y, n - 1)
                dve.tensor_copy(hTe[u % 2], (p_a, p_c)[u % 2][:, 0:P]).then_inc(e_hTc, 1)

            def out_copy(n, u):
                dve.wait_ge(e_y, n + 1)
                dve.tensor_copy(yr[u], p_tok[:, 1024 + u % 2 * 512:1024 + u % 2 * 512 + D]).then_inc(e_yc, 1)

            def step(n, u):
                if not (isinstance(n, int) and n >= TILES):
                    hidden(n, u)
                if not (isinstance(n, int) and (n < 1 or n > TILES)):
                    hidden_copy(n - 1, (u - 1) % RING)
                if not (isinstance(n, int) and n < 2):
                    out_copy(n - 2, (u - 2) % RING)

            for n in range(2 * RING):
                step(n, n % RING)
            with dve.Fori(2, TILES // RING) as i:
                for u in range(RING):
                    step(i * RING + u, u)
            for n in range(TILES, TILES + 2):
                step(n, n % RING)

            for t in range(NT):
                dve.wait_ge(s_slots[t % 4], 16 * (t // 4 + 1))
                sl = slots[t % 4][:, 0]
                link(dve.tensor_tensor(sl[:, 0:2, :], sl[:, 0:2, :], sl[:, 2:4, :], ALU.add))
                link(dve.tensor_tensor(sl[:, 0, :], sl[:, 0, :], sl[:, 1, :], ALU.add))
                dve.tensor_tensor(xs[:, t, :], xs[:, t, :], sl[:, 0, :], ALU.add).then_inc(s_sum, 1)


def kernel(**inputs):
    import numpy as _np
    import concourse.bacc as _bacc
    from concourse import mybir as _mybir
    from concourse.bass_utils import run_bass_kernel_spmd as _run

    i = {k: _np.asarray(v) for k, v in inputs.items()}
    F, D = i["L0_ffn_w1"].shape
    conv = _np.concatenate([i["L0_ffn_conv_w"][:, 0, :], i["L0_ffn_conv_b"][:, None]], axis=1)
    E = i["L1_ffn_w_gate"].shape[0]
    NB, S, _ = i["x"].shape
    arrays = {
        "x": i["x"],
        "xT": i["x"].reshape(NB * S, D).T,
        "id0": i["itok_B_0_8"][None, :],
        "id1": i["itok_B_0_6"][None, :],
        "l0_w1": i["L0_cond_W1"],
        "l0_b1": i["L0_cond_b1"],
        "l0_w2b2": _np.concatenate([i["L0_cond_W2"], i["L0_cond_b2"][:, None, :]], axis=1),
        "l0_gamma": i["L0_cond_gamma"],
        "l0_beta": i["L0_cond_beta"],
        "w1T": i["L0_ffn_w1"].T,
        "conv": conv.reshape(F // 128, 128, 4).transpose(1, 0, 2),
        "w2T": i["L0_ffn_w2"].T,
        "l1_down": i["L1_cond_down_w"],
        "l1_down_b": i["L1_cond_down_b"],
        "l1_up": i["L1_cond_up_w"],
        "l1_up_b": i["L1_cond_up_b"],
        "l1_gamma": i["L1_cond_ln_g"],
        "l1_beta": i["L1_cond_ln_b"],
        "routerT": i["L1_ffn_router_weight"].T,
        "router_bias": i["L1_ffn_router_bias"],
        "gate_upT": _np.concatenate([i["L1_ffn_w_gate"].transpose(0, 2, 1), i["L1_ffn_w_up"].transpose(0, 2, 1)], axis=2),
        "downT": i["L1_ffn_w_down"].transpose(2, 0, 1),
    }
    arrays = {f"in_{k}": _np.ascontiguousarray(v) for k, v in arrays.items()}
    nc = _bacc.Bacc("TRN2", target_bir_lowering=False, num_devices=1)
    f32 = _mybir.dt.float32
    args = [nc.dram_tensor(k, v.shape, _mybir.dt.from_np(v.dtype), kind="ExternalInput").ap() for k, v in arrays.items()]
    args.append(nc.dram_tensor("out_0", i["x"].shape, f32, kind="ExternalOutput").ap())
    args.append(nc.dram_tensor("sent", (E * (NB * S + 128) + 128, D + 2), f32, kind="Internal").ap())
    args.append(nc.dram_tensor("done", (4 * NB * S, D), f32, kind="Internal").ap())
    build(nc, *args)
    r = _run(nc, [arrays], core_ids=[0])
    return r.results[0]["out_0"]
```

```python
from contextlib import ExitStack

import concourse.bass as bass
from concourse import mybir

ALU = mybir.AluOpType
ACT = mybir.ActivationFunctionType
AX_X = mybir.AxisListType.X
F32 = mybir.dt.float32
BF16 = mybir.dt.bfloat16
I32 = mybir.dt.int32
U32 = mybir.dt.uint32

P = 128
MAGIC = 1.5 * 2.0 ** 23
LN_EPS = 1e-5
QUANT_MIN = 1e-5
QMAX = 127.0
GROUPS, GROUPS_KEPT, TOP_K = 4, 2, 4
NEG_INF = -1e9
ROUTED_SCALE = 2.5


def build(nc, x, xT, id0, id1, l0_w1, l0_b1, l0_w2b2, l0_gamma, l0_beta, w1T, conv, w2T,
          l1_down, l1_down_b, l1_up, l1_up_b, l1_gamma, l1_beta, routerT, router_bias,
          gate_upT, downT, out, sent, done):
    NB, S, D = x.shape
    TOK = NB * S
    NT = TOK // P
    TB = S // P
    DK = D // P
    A0 = l0_w1.shape[2]
    A1 = l1_down.shape[2]
    F = w1T.shape[1]
    FC = F // P
    NP = FC // 2
    E = routerT.shape[1]
    HI = downT.shape[0]
    ROW = sent.shape[1]
    REGION = TOK + P
    ROUTE = [(0, 2), (2, 4), (4, 6), (6, 7), (7, 8)]
    GT = max(TB * (hi - lo) for lo, hi in ROUTE)
    PE_PAIRS = (3,)
    RT = 8
    assert A1 == P and HI == P and TB == 2 and DK == 2 and ROUTE[-1][1] == NB
    LIVE = (TOP_K * TOK + E * (P - 1)) // P
    RING = 8
    DIGITS = 5
    WORDS = (RING + 2) // DIGITS
    TILES = (LIVE + RING - 1) // RING * RING

    with ExitStack() as ctx:
        def sb(name, shape, dt=F32):
            return ctx.enter_context(nc.sbuf_tensor(name, shape, dt))

        def ps(name, cols):
            return ctx.enter_context(nc.psum_tensor(name, [P, cols], F32))

        def sem(name):
            return ctx.enter_context(nc.semaphore(name))

        p_pair = [ps(f"p_pair{n}", 512) for n in range(2)]
        p_tok = ps("p_tok", 2048)
        p_a = ps("p_a", 512)
        p_c = ps("p_c", 512)

        ident = sb("ident", [P, P])
        ones = sb("ones", [P, P])
        ones_b = sb("ones_b", [P, P], BF16)
        before = sb("before", [P, P], BF16)
        ternary1 = sb("ternary1", [P, DK, F], BF16)
        ternary2 = sb("ternary2", [P, FC, D], BF16)
        convs = sb("convs", [P, FC, 4])
        diag = sb("diag", [P, len(PE_PAIRS), 2, 3, P])
        wstat = sb("wstat", [P, 2])
        wmean = sb("wmean", [P, 2])
        wscale = sb("wscale", [P, 2])
        gate_up = sb("gate_up", [P, E, DK, 2 * HI])
        down = sb("down", [P, E, D])
        router = sb("router", [P, DK, E])
        rbias = sb("rbias", [P, E])

        xs = sb("xs", [P, NT, D])
        xTb = [sb(f"xTb{n}", [P, DK, S]) for n in range(2)]
        w1b = [sb(f"w1b{n}", [P, DK, A0]) for n in range(2)]
        w2b = [sb(f"w2b{n}", [A0 + 1, D]) for n in range(2)]
        b1b = [sb(f"b1b{n}", [A0, 1]) for n in range(2)]
        ga0 = [sb(f"ga0_{n}", [P, D]) for n in range(2)]
        be0 = [sb(f"be0_{n}", [P, D]) for n in range(2)]
        hT = sb("hT", [A0 + 1, S])
        ya = sb("ya", [P, TB, D])
        bn_a = sb("bn_a", [P, TB, 6])
        mv_a = sb("mv_a", [P, TB, 2])
        rstd_a = sb("rstd_a", [P, TB])
        q1 = sb("q1", [P, 4, TB])
        za = sb("za", [P, TB, D])
        qT = [sb(f"qT{n}", [P, DK, S], BF16) for n in range(2)]
        deq_bc = [sb(f"deq_bc{n}", [P, S]) for n in range(2)]
        gb = [sb(f"gb{n}", [P, 2, S + 2]) for n in range(2)]
        cb = [sb(f"cb{n}", [P, 2, S]) for n in range(2)]
        sbuf_s = [sb(f"act{n}", [P, FC, S]) for n in range(2)]
        q2 = sb("q2", [P, 4, TB])
        zb = sb("zb", [P, TB, F])
        q2T = sb("q2T", [P, FC, S], BF16)

        wdn = [sb(f"wdn{n}", [P, DK, A1]) for n in range(2)]
        wup = [sb(f"wup{n}", [P, D]) for n in range(2)]
        bdn = [sb(f"bdn{n}", [P, 1]) for n in range(2)]
        bup = [sb(f"bup{n}", [P, D]) for n in range(2)]
        ga1 = [sb(f"ga1_{n}", [P, D]) for n in range(2)]
        be1 = [sb(f"be1_{n}", [P, D]) for n in range(2)]
        x1b = sb("x1b", [P, TB, D])
        x1T = sb("x1T", [P, DK, S])
        zk = sb("zk", [P, S])
        yk = sb("yk", [P, TB, D])
        bn_c = sb("bn_c", [P, TB, 6])
        mv_c = sb("mv_c", [P, TB, 2])
        rstd_c = sb("rstd_c", [P, TB])
        xf = sb("xf", [P, TB, D])
        xfT = sb("xfT", [P, DK, S])
        half = sb("half", [P, NT])

        lg = sb("lg", [P, NT, E])
        score = sb("score", [P, GT, E])
        choice = sb("choice", [P, GT, E])
        g_hi = sb("g_hi", [P, GT * GROUPS, 2])
        g_two = sb("g_two", [P, GT * GROUPS, 2])
        g_t = sb("g_t", [P, 2, GT * GROUPS])
        g_sum = sb("g_sum", [P, GT, GROUPS])
        g_gt = sb("g_gt", [P, GT, GROUPS, GROUPS])
        g_ge = sb("g_ge", [P, GT, GROUPS, GROUPS])
        g_first = sb("g_first", [P, GT, GROUPS, GROUPS])
        g_rank = sb("g_rank", [P, GT, GROUPS])
        g_mask = sb("g_mask", [P, GT, GROUPS])
        g_pen = sb("g_pen", [P, GT, GROUPS])
        masked = sb("masked", [P, GT, E])
        top8 = sb("top8", [P, GT, 8])
        idx8 = sb("idx8", [P, GT, 8], U32)
        iota_e = sb("iota_e", [P, E])
        iota_region = sb("iota_region", [P, E])
        onehot = sb("onehot", [P, GT, TOP_K, E])
        picked = sb("picked", [P, GT, TOP_K, E])
        mask_b = sb("mask_b", [P, NT, E], BF16)
        wk = sb("wk", [P, GT, TOP_K])
        wsum = sb("wsum", [P, GT])
        pos = sb("pos", [P, GT, E])
        dest_f = sb("dest_f", [P, GT, TOP_K])
        dest = sb("dest", [P, NT, TOP_K], I32)
        slot_id = sb("slot_id", [P, NT, TOP_K], I32)
        rows = sb("rows", [P, RT, TOP_K, ROW])
        pad = sb("pad", [P, ROW])
        cnt = sb("cnt", [1, 4, E])
        cnt_i = sb("cnt_i", [1, E], I32)
        zrow = sb("zrow", [1, E])
        tj = sb("tj", [1, TILES])
        t_mask, t_prod = (sbuf_s[n][0:1, :, :].rearrange("a c t -> a (c t)")[:, 0:TILES * E].rearrange(
            "a (t e) -> a t e", e=E) for n in range(2))
        t_f = sb("t_f", [1, 3, TILES])
        t_exp = sb("t_exp", [1, TILES + RING])
        t_digit = sb("t_digit", [1, TILES // RING, WORDS, DIGITS])
        t_place = sb("t_place", [1, TILES // RING, DIGITS])
        t_sum = sb("t_sum", [1, TILES // RING, WORDS])
        t_word = sb("t_word", [1, TILES // RING * WORDS], I32)
        t_row = sb("t_row", [1, TILES], I32)

        xr = [sbuf_s[n // 4][:, 2 * (n % 4):2 * (n % 4) + 2, :].rearrange("p a b -> p (a b)")[:, 0:ROW] for n in range(RING)]
        yr = [zb[:, n // 4, (n % 4) * D:(n % 4 + 1) * D] for n in range(RING)]
        xTe = [x1T[:, :, n * P:(n + 1) * P] for n in range(2)]
        sg = [yk[:, n, 0:HI] for n in range(2)]
        he = [ya[:, n, 0:HI] for n in range(2)]
        hTe = [za[:, n, 0:HI] for n in range(2)]
        home = sb("home", [P, RING], I32)
        slots = [rows[:, 2 * n:2 * n + 1, :, 0:D] for n in range(4)]

        s_const = sem("s_const"); s_ident = sem("s_ident"); s_iota = sem("s_iota")
        s_w1 = sem("s_w1"); s_w2 = sem("s_w2"); s_small = sem("s_small"); s_conv_w = sem("s_conv_w"); s_ew = sem("s_ew")
        s_x = [sem(f"s_in{n}") for n in range(2)]
        s_p0 = [sem(f"s_p0_{n}") for n in range(2)]
        s_p1 = [sem(f"s_p1_{n}") for n in range(2)]
        s_dve = sem("s_dve")
        s_wsum = sem("s_wsum"); s_wtot = sem("s_wtot"); s_wscale = sem("s_wscale"); s_wround = sem("s_wround"); s_wclip = sem("s_wclip"); s_tern = sem("s_tern")
        s_hT = sem("s_hT"); s_hr = sem("s_hr"); s_ya = sem("s_ya"); s_mva = sem("s_mva")
        s_rsa = sem("s_rsa"); s_q1 = sem("s_q1"); s_za = sem("s_za");
        s_zaT = sem("s_zaT"); s_qT = sem("s_qT"); s_rbT = sem("s_rbT"); s_deq = sem("s_deq")
        s_h = sem("s_h"); s_g = sem("s_g"); s_c0 = sem("s_c0"); s_tap = sem("s_tap"); s_diag = sem("s_diag"); s_conv = sem("s_conv"); s_silu = sem("s_silu")
        s_sT = sem("s_sT"); s_q2 = sem("s_q2"); s_zb = sem("s_zb"); s_zbT = sem("s_zbT")
        s_q2T = sem("s_q2T"); s_y2 = sem("s_y2"); s_x1 = sem("s_x1")
        s_x1b = sem("s_x1b"); s_x1T = sem("s_x1T"); s_x1Te = sem("s_x1Te"); s_zk = sem("s_zk")
        s_zr = sem("s_zr"); s_yk = sem("s_yk"); s_mvc = sem("s_mvc"); s_rsc = sem("s_rsc")
        s_xf = sem("s_xf"); s_xfT = sem("s_xfT"); s_xfTe = sem("s_xfTe"); s_rows = sem("s_rows")
        s_lgp = sem("s_lgp"); s_lg = sem("s_lg"); s_pool = sem("s_pool")
        s_score = sem("s_score"); s_route = sem("s_route"); s_mask = sem("s_mask"); s_pre = sem("s_pre"); s_dest = sem("s_dest")
        s_cnt = sem("s_cnt"); s_table = sem("s_table"); s_padr = sem("s_padr")
        s_sent = [sem(f"s_sent{n}") for n in range(RT)]
        s_pad = sem("s_pad")
        s_xr = [sem(f"s_xr{n}") for n in range(RING)]
        s_back = [sem(f"s_back{n}") for n in range(RING)]
        e_xT = sem("e_xT"); e_xTc = sem("e_xTc"); e_gu = sem("e_gu"); e_sg = sem("e_sg")
        e_h = sem("e_h"); e_hT = sem("e_hT"); e_hTc = sem("e_hTc"); e_y = sem("e_y"); e_yc = sem("e_yc"); e_turn = sem("e_turn")
        e_home = sem("e_home")
        s_slots = [sem(f"s_slots{n}") for n in range(4)]
        s_sum = sem("s_sum"); s_out = [sem(f"s_out{n}") for n in range(4)]

        N_P0 = 6 * 16
        N_P1 = 6 * 16
        N_CONST = 8 + DIGITS + GROUPS - 1

        def seq(b):
            return b // 2 + 1

        def registers(eng, table, first, count, most):
            return nc.values_load_multi_w_load_instructions(
                table[0:1, bass.ds(first, count)], engines=(eng.engine,), min_val=0, max_val=most)[1]

        def run(stage, b, *part):
            if 0 <= b < NB:
                stage(b, *part)

        def run_group(stage, b, *part):
            for h, (_, hi) in enumerate(ROUTE):
                if b == hi - 1:
                    stage(h, *part)

        def side_pairs(m):
            side = [p for p in range(NP) if p not in PE_PAIRS]
            return m // NP * len(side) + sum(p <= m % NP for p in side)

        def pe_pairs(m):
            return m + 1 - side_pairs(m)

        def tiles_of(h):
            return TB * ROUTE[h][0], TB * ROUTE[h][1]

        def send_padding(eng, first):
            eng.wait_ge(s_padr, 1)
            eng.wait_ge(s_cnt, 1)
            for e, c in enumerate(registers(eng, cnt_i, 0, E, TOK)):
                if e % 2 == first:
                    eng.dma_start(sent[bass.ds(c + e * REGION, P), :], pad[:]).then_inc(s_pad, 16)

        w1f = zb[:, :, :].rearrange("p a b -> p (a b)")
        w2f = sbuf_s[1][:, :, :].rearrange("p a b -> p (a b)")

        block = ctx.enter_context(nc.Block())

        @block.sync
        def _(sp):
            def load_layer0(b):
                n = b % 2
                if b >= 2:
                    sp.wait_ge(s_ya, b - 1)
                    sp.wait_ge(s_q1, b - 1)
                sp.dma_start(xTb[n][:], xT[:, b * S:(b + 1) * S].rearrange("(k p) t -> p k t", p=P)).then_inc(s_x[n], 16)
                sp.dma_start(xs[:, TB * b:TB * b + TB, :], x[b].rearrange("(j p) d -> p j d", p=P)).then_inc(s_x[n], 16)
                r = sp.value_load(id0[0:1, b:b + 1], min_val=0, max_val=l0_w1.shape[0] - 1)
                one = bass.ds(r, 1)
                sp.dma_start(w1b[n][:], l0_w1[one].rearrange("a (k p) n -> p (a k) n", p=P)).then_inc(s_p0[n], 16)
                sp.dma_start(w2b[n][:], l0_w2b2[one].rearrange("a k n -> (a k) n")).then_inc(s_p0[n], 16)
                sp.dma_start(b1b[n][:], l0_b1[one].rearrange("a n -> n a")).then_inc(s_p0[n], 16)
                sp.dma_start(ga0[n][:], l0_gamma[one].rearrange("a n -> (a n)").partition_broadcast(P)).then_inc(s_p0[n], 16)
                sp.dma_start(be0[n][:], l0_beta[one].rearrange("a n -> (a n)").partition_broadcast(P)).then_inc(s_p0[n], 32)

            def load_layer1(b):
                n = b % 2
                if b >= 2:
                    sp.wait_ge(s_yk, b - 1)
                    sp.wait_ge(s_xf, b - 1)
                    sp.wait_ge(s_x1b, b - 1)
                r = sp.value_load(id1[0:1, b:b + 1], min_val=0, max_val=l1_down.shape[0] - 1)
                one = bass.ds(r, 1)
                sp.dma_start(wdn[n][:], l1_down[one].rearrange("a (k p) n -> p (a k) n", p=P)).then_inc(s_p1[n], 16)
                sp.dma_start(wup[n][:], l1_up[one].rearrange("a k n -> (a k) n")).then_inc(s_p1[n], 16)
                sp.dma_start(bdn[n][:], l1_down_b[one].rearrange("a n -> n a")).then_inc(s_p1[n], 16)
                sp.dma_start(bup[n][:], l1_up_b[one].rearrange("a n -> (a n)").partition_broadcast(P)).then_inc(s_p1[n], 16)
                sp.dma_start(ga1[n][:], l1_gamma[one].rearrange("a n -> (a n)").partition_broadcast(P)).then_inc(s_p1[n], 16)
                sp.dma_start(be1[n][:], l1_beta[one].rearrange("a n -> (a n)").partition_broadcast(P)).then_inc(s_p1[n], 16)

            load_layer0(0)
            sp.dma_start(zb[:, :, :].rearrange("p a b -> p (a b)"),
                         w1T.rearrange("(k p) f -> p k f", p=P)).then_inc(s_w1, 16)
            sp.dma_start(convs[:], conv).then_inc(s_conv_w, 16)
            sp.dma_start(sbuf_s[1][:], w2T.rearrange("(c p) d -> p c d", p=P)).then_inc(s_w2, 16)
            sp.dma_start(router[:], routerT.rearrange("(k p) e -> p k e", p=P)).then_inc(s_small, 16)
            sp.dma_start(rbias[:], router_bias.partition_broadcast(P)).then_inc(s_small, 16)
            load_layer0(1)
            load_layer0(2)
            load_layer1(0)
            load_layer0(3)
            load_layer1(1)
            for i in range(4, NB + 3):
                if i < NB:
                    load_layer0(i)
                    n = E // (NB - 4)
                    part = slice((i - 4) * n, (i - 3) * n)
                    sp.dma_start(gate_up[:, part], gate_upT[part].rearrange("e (k p) n -> p e k n", p=P)).then_inc(s_ew, 16)
                    sp.dma_start(down[:, part], downT[:, part]).then_inc(s_ew, 16)
                if 2 <= i - 3:
                    load_layer1(i - 3)
            sp.wait_ge(s_padr, 1)
            sp.dma_start(sent[E * REGION:E * REGION + P, :], pad[:]).then_inc(s_pad, 16)
            send_padding(sp, 0)
            def load_tile(u, row):
                sp.dma_start(xr[u], sent[bass.ds(row, P), :]).then_inc(s_xr[u], 16)

            sp.wait_ge(s_table, 1)
            first = registers(sp, t_row, 0, RING, E * REGION)
            sp.wait_ge(s_pad, 16 * (E + 1))
            for n in range(RT):
                sp.wait_ge(s_sent[n], NT // RT * TOP_K * 16)
            for u, row in enumerate(first):
                load_tile(u, row)
            with sp.Fori(1, TILES // RING) as i:
                for u, row in enumerate(registers(sp, t_row, i * RING, RING, E * REGION)):
                    sp.wait_ge(e_home, (i - 1) * RING + u + 1)
                    load_tile(u, row)
            for u in range(RING):
                sp.wait_ge(s_back[u], 16 * (TILES // RING))
            for t in range(NT):
                if t >= 4:
                    sp.wait_ge(s_sum, t - 3)
                sp.dma_start(slots[t % 4], done[TOP_K * P * t:TOP_K * P * (t + 1), :].rearrange(
                    "(p a k) d -> p a k d", k=TOP_K, a=1)).then_inc(s_slots[t % 4], 16)
            for n in range(4):
                sp.wait_ge(s_out[n], 16 * (NT // 4))

        @block.gpsimd
        def _(pool):
            chain = [0]

            def link(ins):
                chain[0] += 1
                ins.then_inc(s_pool, 1)
                pool.wait_ge(s_pool, chain[0])

            pool.memset(ones[:], 1.0).then_inc(s_const, 1)
            pool.memset(gb[0][:], 0.0).then_inc(s_const, 1)
            pool.memset(gb[1][:], 0.0).then_inc(s_const, 1)
            pool.memset(hT[:], 1.0).then_inc(s_const, 1)
            pool.memset(ones_b[:], 1.0).then_inc(s_const, 1)
            pool.memset(half[:], -0.5).then_inc(s_const, 1)
            pool.memset(zrow[:], 0.0).then_inc(s_const, 1)
            pool.memset(t_exp[:], 0.0).then_inc(s_const, 1)
            for n in range(DIGITS):
                pool.memset(t_place[:, :, n], float(E ** n)).then_inc(s_const, 1)
            link(pool.memset(ident[:], 0.0))
            pool.affine_select(out=ident[:], in_=ident[:], compare_op=ALU.not_equal, fill=1.0, base=0,
                               pattern=[[-1, P]], channel_multiplier=1).then_inc(s_ident, 1)
            link(pool.memset(before[:], 0.0))
            pool.affine_select(out=before[:], in_=before[:], compare_op=ALU.is_ge, fill=1.0, base=0,
                               pattern=[[-1, P]], channel_multiplier=1).then_inc(s_ident, 1)
            link(pool.memset(g_first[:], 0.0))
            for g in range(GROUPS):
                if g:
                    pool.memset(g_first[:, :, g, 0:g], 1.0).then_inc(s_const, 1)
            pool.wait_ge(s_ident, 2)
            pool.wait_ge(s_conv_w, 16)
            for n, p in enumerate(PE_PAIRS):
                for c in range(2):
                    for k in range(3):
                        pool.tensor_scalar(diag[:, n, c, k, :], ident[:], convs[:, 2 * p + c, k:k + 1], None,
                                           ALU.mult).then_inc(s_diag, 1)
            pool.iota(iota_e[:], pattern=[[1, E]], base=0, channel_multiplier=0,
                      allow_small_or_imprecise_dtypes=True).then_inc(s_iota, 1)
            pool.iota(iota_region[:], pattern=[[REGION, E]], base=0, channel_multiplier=0,
                      allow_small_or_imprecise_dtypes=True).then_inc(s_iota, 1)
            pool.iota(slot_id[:], pattern=[[P * TOP_K, NT], [1, TOP_K]], base=0,
                      channel_multiplier=TOP_K).then_inc(s_iota, 1)
            pool.iota(tj[:], pattern=[[1, TILES]], base=0, channel_multiplier=0,
                      allow_small_or_imprecise_dtypes=True).then_inc(s_iota, 1)
            link(pool.memset(pad[:], 0.0))
            pool.iota(pad[:, D:D + 1].bitcast(I32), pattern=[[0, 1]], base=TOK * TOP_K,
                      channel_multiplier=1).then_inc(s_padr, 1)

            def rstd(b, mv, out_, ready, signal):
                pool.wait_ge(ready, b + 1)
                link(pool.tensor_scalar(out_[:], mv[:, :, 1], LN_EPS, None, ALU.add))
                pool.tensor_tensor(out_[:], out_[:], half[:, 0:TB], op=ALU.pow).then_inc(signal, 1)

            def residual_and_bias(b):
                pool.wait_ge(s_x1, TB * (b + 1))
                pool.wait_ge(s_p1[b % 2], N_P1 * seq(b))
                if b:
                    pool.wait_ge(s_yk, b)
                for j in range(TB):
                    ins = pool.tensor_tensor(x1b[:, j, :], xs[:, TB * b + j, :], bup[b % 2][:], op=ALU.add)
                ins.then_inc(s_x1b, 1)

            def send(h, k):
                lo, hi = tiles_of(h)
                if k >= hi - lo:
                    return
                t = lo + k
                pool.wait_ge(s_dest, h + 1)
                pool.wait_ge(s_rows, t + 1)
                for c in range(TOP_K):
                    pool.indirect_dma_start(
                        out=sent[:, :], in_=rows[:, t % RT, c, :], in_offset=None,
                        out_offset=bass.IndirectOffsetOnAxis(ap=dest[:, t, c:c + 1], axis=0),
                    ).then_inc(s_sent[t % RT], 16)

            for i in range(NB + 7):
                run_group(send, i - 6, 2)
                run_group(send, i - 7, 1)
                run(residual_and_bias, i - 4)
                run_group(send, i - 7, 3)
                run_group(send, i - 6, 0)
                run(rstd, i - 4, mv_c, rstd_c, s_mvc, s_rsc)
                run(rstd, i, mv_a, rstd_a, s_mva, s_rsa)

            last_slot = pool.to_reg(TOK * TOP_K - 1)

            def give_back(n, u):
                pool.wait_ge(e_yc, n + 1)
                pool.sem_inc(e_turn, 1)
                pool.indirect_dma_start(
                    out=done[:, :], in_=yr[u], in_offset=None,
                    out_offset=bass.IndirectOffsetOnAxis(ap=home[:, u:u + 1], axis=0),
                    bounds_check=last_slot, oob_is_err=False).then_inc(s_back[u], 16)

            with pool.Fori(0, TILES // RING) as i:
                for u in range(RING):
                    give_back(i * RING + u, u)

        @block.tensor
        def _(pe):
            pe.wait_ge(s_const, N_CONST)
            pe.wait_ge(s_ident, 2)

            def weight_sums():
                pe.wait_ge(s_wsum, 2)
                pe.matmul(p_pair[0][:, 0:2], ones[:], wstat[:], start=True, stop=True).then_inc(s_wtot, 1)

            p_tok_use = {"sequence": None, "places": 0}

            def adapter0_hidden(b):
                pe.wait_ge(s_x[b % 2], 32 * seq(b))
                pe.wait_ge(s_p0[b % 2], N_P0 * seq(b))
                if b:
                    pe.wait_ge(s_deq, b)
                for k in range(DK):
                    ins = pe.matmul(p_a[0:A0, 0:S], w1b[b % 2][:, k, :], xTb[b % 2][:, k, :],
                                    start=k == 0, stop=k == DK - 1)
                ins.then_inc(s_hT, 1)

            def adapter0_out(b):
                pe.wait_ge(s_hr, b + 1)
                for j in range(TB):
                    pe.matmul(p_a[:, j * D:(j + 1) * D], ident[:], xs[:, TB * b + j, :], start=True, stop=False)
                    ins = pe.matmul(p_a[:, j * D:(j + 1) * D], hT[:, j * P:(j + 1) * P], w2b[b % 2][:],
                                    start=False, stop=True)
                ins.then_inc(s_ya, 1)

            def adapter0_quant(b):
                pe.wait_ge(s_za, TB * (b + 1))
                for k in range(DK):
                    for j in range(TB):
                        ins = pe.transpose(p_a[:, k * S + j * P:k * S + (j + 1) * P], za[:, j, k * P:(k + 1) * P], ident[:])
                ins.then_inc(s_zaT, 1)

            def token_scales(b):
                pe.wait_ge(s_qT, b + 1)
                pe.wait_ge(s_q1, b + 1)
                for j in range(TB):
                    ins = pe.transpose(p_a[:, j * P:(j + 1) * P], q1[:, 2, j:j + 1].to_broadcast([P, P]), ident[:])
                ins.then_inc(s_rbT, 1)

            def up_pair(b, p):
                m = NP * b + p
                if p == 0:
                    pe.wait_ge(s_tern, 1)
                    pe.wait_ge(s_qT, b + 1)
                if m >= 2:
                    pe.wait_ge(s_silu if (m - 2) % NP in PE_PAIRS else s_g, m - 1)
                for c in range(2):
                    ch = (2 * p + c) * P
                    for k in range(DK):
                        ins = pe.matmul(p_pair[m % 2][:, c * S:(c + 1) * S], ternary1[:, k, ch:ch + P],
                                        qT[b % 2][:, k, :], start=k == 0, stop=k == DK - 1)
                ins.then_inc(s_h, 1)

            def conv_pair(b, p):
                m = NP * b + p
                if b == 0:
                    pe.wait_ge(s_diag, len(PE_PAIRS) * 6)
                pe.wait_ge(s_g, m + 1)
                for c in range(2):
                    for k in range(3):
                        ins = pe.matmul(p_pair[m % 2][:, c * S:(c + 1) * S], diag[:, PE_PAIRS.index(p), c, k, :],
                                        gb[m % 2][:, c, k:k + S], start=k == 0, stop=k == 2)
                ins.then_inc(s_conv, 1)

            def hidden_by_token(b, j):
                pe.wait_ge(s_silu, NP * (b + 1))
                if b:
                    pe.wait_ge(s_x1, TB * (b - 1) + j + 1)
                if j == 0:
                    if p_tok_use["places"]:
                        pe.wait_ge(s_dest, p_tok_use["places"])
                    p_tok_use["sequence"] = b
                for c in range(FC):
                    ins = pe.transpose(p_tok[:, j * F + c * P:j * F + (c + 1) * P],
                                       sbuf_s[b % 2][:, c, j * P:(j + 1) * P], ident[:])
                ins.then_inc(s_sT, 1)

            def quant_by_channel(b, j):
                pe.wait_ge(s_zb, TB * b + j + 1)
                for c in range(FC):
                    ins = pe.transpose(p_tok[:, j * F + c * P:j * F + (c + 1) * P], zb[:, j, c * P:(c + 1) * P], ident[:])
                ins.then_inc(s_zbT, 1)

            def ffn_out(b, j):
                pe.wait_ge(s_q2T, TB * b + j + 1)
                pe.wait_ge(s_tern, 2)
                for c in range(FC):
                    ins = pe.matmul(p_tok[:, j * F:j * F + D], q2T[:, c, j * P:(j + 1) * P], ternary2[:, c, :],
                                    start=c == 0, stop=c == FC - 1)
                ins.then_inc(s_y2, 1)

            def adapter1_in(b):
                pe.wait_ge(s_x1, TB * (b + 1))
                if b:
                    pe.wait_ge(s_lg, b)
                for k in range(DK):
                    for j in range(TB):
                        ins = pe.transpose(p_c[:, k * S + j * P:k * S + (j + 1) * P],
                                           xs[:, TB * b + j, k * P:(k + 1) * P], ident[:])
                ins.then_inc(s_x1T, 1)

            def adapter1_hidden(b):
                pe.wait_ge(s_x1Te, b + 1)
                pe.wait_ge(s_p1[b % 2], N_P1 * seq(b))
                for k in range(DK):
                    ins = pe.matmul(p_c[:, 0:S], wdn[b % 2][:, k, :], x1T[:, k, :], start=k == 0, stop=k == DK - 1)
                ins.then_inc(s_zk, 1)

            def adapter1_out(b):
                pe.wait_ge(s_zr, b + 1)
                pe.wait_ge(s_x1b, b + 1)
                for j in range(TB):
                    pe.matmul(p_c[:, j * D:(j + 1) * D], ident[:], x1b[:, j, :], start=True, stop=False)
                    ins = pe.matmul(p_c[:, j * D:(j + 1) * D], zk[:, j * P:(j + 1) * P], wup[b % 2][:],
                                    start=False, stop=True)
                ins.then_inc(s_yk, 1)

            def normed_by_width(b):
                pe.wait_ge(s_xf, b + 1)
                for k in range(DK):
                    for j in range(TB):
                        ins = pe.transpose(p_c[:, k * S + j * P:k * S + (j + 1) * P], xf[:, j, k * P:(k + 1) * P], ident[:])
                ins.then_inc(s_xfT, 1)

            def logits(b):
                pe.wait_ge(s_xfTe, b + 1)
                if b == 0:
                    pe.wait_ge(s_small, 32)
                for j in range(TB):
                    for k in range(DK):
                        ins = pe.matmul(p_c[:, j * E:(j + 1) * E], xfT[:, k, j * P:(j + 1) * P], router[:, k, :],
                                        start=k == 0, stop=k == DK - 1)
                ins.then_inc(s_lgp, 1)

            def places(h):
                lo, hi = tiles_of(h)
                n = hi - lo
                pe.wait_ge(s_mask, h + 1)
                pe.wait_ge(s_x1, TB * p_tok_use["sequence"] + 1)
                p_tok_use["places"] = h + 1
                pe.matmul(p_tok[:, 0:n * E], before[:], mask_b[:, lo:hi, :], start=True, stop=False,
                          skip_group_check=True)
                for t in range(hi - 1):
                    first = max(t + 1, lo)
                    ins = pe.matmul(p_tok[:, (first - lo) * E:n * E], ones_b[:],
                                    mask_b[:, t:t + 1, :].to_broadcast([P, hi - first, E]),
                                    start=False, stop=t == hi - 2, skip_group_check=True)
                if hi == NT:
                    for t in range(NT):
                        ins = pe.matmul(p_tok[:, n * E:n * E + E], ones_b[:], mask_b[:, t, :],
                                        start=t == 0, stop=t == NT - 1)
                ins.then_inc(s_pre, 1)

            for i in range(NB + 6):
                run(adapter0_out, i - 1)
                if i == 1:
                    weight_sums()
                run(ffn_out, i - 4, 0)
                run(quant_by_channel, i - 4, 1)
                run(conv_pair, i - 3, 3)
                run_group(places, i - 6)
                run(normed_by_width, i - 5)
                run(ffn_out, i - 4, 1)
                run(up_pair, i - 2, 1)
                run(logits, i - 5)
                run(hidden_by_token, i - 3, 0)
                run(up_pair, i - 2, 2)
                run(adapter0_quant, i - 1)
                run(hidden_by_token, i - 3, 1)
                run(token_scales, i - 1)
                run(adapter1_in, i - 4)
                run(up_pair, i - 2, 3)
                run(adapter0_hidden, i)
                run(adapter1_hidden, i - 4)
                run(quant_by_channel, i - 3, 0)
                run(adapter1_out, i - 4)
                run(up_pair, i - 1, 0)
            pe.wait_ge(s_ew, 2 * (NB - 4) * 16)
            pe.wait_ge(s_table, 1)

            def x_by_width(n, u):
                pe.wait_ge(s_xr[u], 16 * (n // RING + 1) if isinstance(n, int) else (n - u) * (16 // RING) + 16)
                if not (isinstance(n, int) and n < 2):
                    pe.wait_ge(e_xTc, n - 1)
                for k in range(DK):
                    ins = pe.transpose(p_pair[u % 2][:, k * P:(k + 1) * P], xr[u][:, k * P:(k + 1) * P], ident[:])
                ins.then_inc(e_xT, 1)

            def gate_and_up(n, u, e):
                pe.wait_ge(e_xTc, n + 1)
                if not (isinstance(n, int) and n < 2):
                    pe.wait_ge(e_h, n - 1)
                for k in range(DK):
                    ins = pe.matmul(p_tok[:, u % 2 * 512:u % 2 * 512 + 2 * HI], xTe[u % 2][:, k, :],
                                    gate_up[:, bass.ds(e, 1), k, :], start=k == 0, stop=k == DK - 1)
                ins.then_inc(e_gu, 1)

            def hidden_by_width(n, u):
                pe.wait_ge(e_h, n + 1)
                if not (isinstance(n, int) and n < 2):
                    pe.wait_ge(e_hTc, n - 1)
                pe.transpose((p_a, p_c)[u % 2][:, 0:P], he[u % 2], ident[:]).then_inc(e_hT, 1)

            def expert_out(n, u, e):
                pe.wait_ge(e_hTc, n + 1)
                if not (isinstance(n, int) and n < 2):
                    pe.wait_ge(e_yc, n - 1)
                pe.matmul(p_tok[:, 1024 + u % 2 * 512:1024 + u % 2 * 512 + D], hTe[u % 2],
                          down[:, bass.ds(e, 1), :], start=True, stop=True).then_inc(e_y, 1)

            def step(n, u, e, last=False):
                if not (last and n + 1 >= TILES):
                    x_by_width(n + 1, (u + 1) % RING)
                if not (last and n >= TILES):
                    gate_and_up(n, u, e[u + 2])
                if not (isinstance(n, int) and (n < 1 or n > TILES)):
                    hidden_by_width(n - 1, (u - 1) % RING)
                if not (isinstance(n, int) and n < 2):
                    expert_out(n - 2, (u - 2) % RING, e[u])

            def experts(i):
                words = registers(pe, t_word, i * WORDS, WORDS, E ** DIGITS - 1)
                return [(w >> (n * (E.bit_length() - 1))) & (E - 1) for w in words for n in range(DIGITS)]

            e = experts(0)
            x_by_width(0, 0)
            for n in range(RING):
                step(n, n, e)
            with pe.Fori(1, TILES // RING - 1) as i:
                e = experts(i)
                for u in range(RING):
                    step(i * RING + u, u, e)
            e = experts(TILES // RING - 1)
            for n in range(TILES - RING, TILES):
                step(n, n % RING, e, last=True)
            for u in range(2):
                step(TILES + u, u, e[RING:], last=True)

        @block.scalar
        def _(act):
            def copy(o, i_):
                return act.activation(o, i_, ACT.Copy)

            def weight_round(n, w):
                act.wait_ge(s_wscale, 1)
                act.activation(w, w, ACT.Identity, bias=MAGIC, scale=wscale[:, n:n + 1]).then_inc(s_wround, 1)

            def weight_integers(n, w, o):
                act.wait_ge(s_wclip, n + 1)
                act.activation(o[:].rearrange("p a b -> p (a b)"), w, ACT.Identity, bias=-MAGIC).then_inc(s_tern, 1)

            def conv_centre(b, p):
                m = NP * b + p
                act.wait_ge(s_g, m + 1)
                if b == 0:
                    act.wait_ge(s_conv_w, 16)
                if m >= 2:
                    act.wait_ge(s_silu, m - 1)
                for c in range(2):
                    ch = 2 * p + c
                    ins = act.activation(cb[m % 2][:, c, :], gb[m % 2][:, c, 1:S + 1], ACT.Identity,
                                         bias=convs[:, ch, 3:4], scale=convs[:, ch, 1:2])
                ins.then_inc(s_c0, 1)

            def silu(b, p):
                m = NP * b + p
                if p in PE_PAIRS:
                    act.wait_ge(s_conv, pe_pairs(m))
                else:
                    act.wait_ge(s_tap, side_pairs(m))
                if p == 0 and b >= 2:
                    act.wait_ge(s_sT, TB * (b - 1))
                if b == 1:
                    act.wait_ge(s_tern, 2)
                if p in PE_PAIRS:
                    for c in range(2):
                        ch = 2 * p + c
                        ins = act.activation(sbuf_s[b % 2][:, ch, :], p_pair[m % 2][:, c * S:(c + 1) * S], ACT.Silu,
                                             bias=convs[:, ch, 3:4])
                else:
                    ins = act.activation(sbuf_s[b % 2][:, 2 * p:2 * p + 2, :], cb[m % 2][:], ACT.Silu)
                ins.then_inc(s_silu, 1)

            def adapter0_relu(b):
                act.wait_ge(s_hT, b + 1)
                act.activation(hT[0:A0, :], p_a[0:A0, 0:S], ACT.Relu, bias=b1b[b % 2][:, 0:1]).then_inc(s_hr, 1)

            def adapter0_round(b):
                act.wait_ge(s_q1, b + 1)
                if b:
                    act.wait_ge(s_zaT, b)
                for j in range(TB):
                    act.activation(za[:, j, :], ya[:, j, :], ACT.Identity,
                                   bias=MAGIC, scale=q1[:, 1, j:j + 1]).then_inc(s_za, 1)

            def adapter0_integers(b):
                act.wait_ge(s_zaT, b + 1)
                if b >= 2:
                    act.wait_ge(s_h, NP * (b - 1))
                act.activation(qT[b % 2][:].rearrange("p k t -> p (k t)"), p_a[:, :], ACT.Identity,
                               bias=-MAGIC).then_inc(s_qT, 1)

            def token_scales(b):
                act.wait_ge(s_rbT, b + 1)
                if b >= 2:
                    act.wait_ge(s_g, NP * (b - 1))
                copy(deq_bc[b % 2][:], p_a[:, 0:S]).then_inc(s_deq, 1)

            def hidden_round(b, j):
                act.wait_ge(s_q2, TB * b + j + 1)
                if b:
                    act.wait_ge(s_zbT, TB * (b - 1) + j + 1)
                else:
                    act.wait_ge(s_tern, 1)
                act.activation(zb[:, j, :], p_tok[:, j * F:(j + 1) * F], ACT.Identity,
                               bias=MAGIC, scale=q2[:, 1, j:j + 1]).then_inc(s_zb, 1)

            def hidden_integers(b, j):
                act.wait_ge(s_zbT, TB * b + j + 1)
                if b:
                    act.wait_ge(s_y2, TB * (b - 1) + j + 1)
                act.activation(q2T[:, :, j * P:(j + 1) * P], p_tok[:, j * F:(j + 1) * F].rearrange("p (c t) -> p c t", c=FC),
                               ACT.Identity, bias=-MAGIC).then_inc(s_q2T, 1)

            def adapter1_x(b):
                act.wait_ge(s_x1T, b + 1)
                copy(x1T[:].rearrange("p k t -> p (k t)"), p_c[:, :]).then_inc(s_x1Te, 1)

            def adapter1_relu(b):
                act.wait_ge(s_zk, b + 1)
                act.activation(zk[:], p_c[:, 0:S], ACT.Relu, bias=bdn[b % 2][:, 0:1]).then_inc(s_zr, 1)

            def normed_by_width(b):
                act.wait_ge(s_xfT, b + 1)
                copy(xfT[:].rearrange("p k t -> p (k t)"), p_c[:, :]).then_inc(s_xfTe, 1)

            def normed_rows(b, j):
                act.wait_ge(s_xf, b + 1)
                t = TB * b + j
                if t >= RT:
                    act.wait_ge(s_sent[t % RT], t // RT * TOP_K * 16)
                copy(rows[:, t % RT, :, 0:D], xf[:, j:j + 1, :].to_broadcast([P, TOP_K, D])).then_inc(s_rows, 1)

            def scores(h):
                lo, hi = tiles_of(h)
                act.wait_ge(s_lg, ROUTE[h][1])
                if h:
                    act.wait_ge(s_route, h)
                act.activation(score[:, 0:hi - lo, :], lg[:, lo:hi, :], ACT.Sigmoid).then_inc(s_score, 1)

            for i in range(NB + 5):
                run(conv_centre, i - 2, 2)
                run(adapter0_relu, i)
                if i == 0:
                    weight_round(0, w1f)
                    weight_round(1, w2f)
                run(hidden_integers, i - 3, 0)
                run(hidden_round, i - 3, 1)
                run(normed_rows, i - 5, 0)
                run(normed_rows, i - 5, 1)
                run(silu, i - 2, 1)
                run(hidden_integers, i - 3, 1)
                run(silu, i - 2, 2)
                run(silu, i - 2, 3)
                run(normed_by_width, i - 4)
                run(conv_centre, i - 1, 0)
                run(adapter0_round, i)
                if i == 0:
                    weight_integers(0, w1f, ternary1)
                run(conv_centre, i - 1, 1)
                run(adapter0_integers, i)
                run_group(scores, i - 4)
                run(silu, i - 1, 0)
                run(token_scales, i)
                if i == 0:
                    weight_integers(1, w2f, ternary2)
                run(adapter1_x, i - 3)
                run(hidden_round, i - 2, 0)
                run(adapter1_relu, i - 3)
            send_padding(act, 1)

            def x_copy(n, u):
                act.wait_ge(e_xT, n + 1)
                if not (isinstance(n, int) and n < 2):
                    act.wait_ge(e_gu, n - 1)
                copy(xTe[u % 2], p_pair[u % 2][:, 0:D].rearrange("p (k t) -> p k t", k=DK)).then_inc(e_xTc, 1)

            def gate(n, u):
                act.wait_ge(e_gu, n + 1)
                if not (isinstance(n, int) and n < 2):
                    act.wait_ge(e_h, n - 1)
                act.activation(sg[u % 2], p_tok[:, u % 2 * 512:u % 2 * 512 + HI], ACT.Silu).then_inc(e_sg, 1)

            x_copy(0, 0)
            for n in range(RING):
                x_copy(n + 1, (n + 1) % RING)
                gate(n, n)
            with act.Fori(1, TILES // RING - 1) as i:
                for u in range(RING):
                    x_copy(i * RING + u + 1, (u + 1) % RING)
                    gate(i * RING + u, u)
            for n in range(TILES - RING, TILES):
                if n + 1 < TILES:
                    x_copy(n + 1, (n + 1) % RING)
                gate(n, n % RING)
            for t in range(NT):
                act.wait_ge(s_sum, t + 1)
                act.dma_start(out[t // TB, t % TB * P:(t % TB + 1) * P, :], xs[:, t, :]).then_inc(s_out[t % 4], 16)

        @block.vector
        def _(dve):
            chain = [0]

            def mark(ins):
                chain[0] += 1
                ins.then_inc(s_dve, 1)
                return chain[0]

            def link(ins):
                dve.wait_ge(s_dve, mark(ins))


            def weight_sums():
                dve.wait_ge(s_w1, 16)
                dve.tensor_reduce(wstat[:, 0:1], w1f, AX_X, ALU.add, apply_absolute_value=True).then_inc(s_wsum, 1)
                dve.wait_ge(s_w2, 16)
                dve.tensor_reduce(wstat[:, 1:2], w2f, AX_X, ALU.add, apply_absolute_value=True).then_inc(s_wsum, 1)

            def weight_means():
                dve.wait_ge(s_wtot, 1)
                link(dve.tensor_scalar(wmean[:], p_pair[0][:, 0:2], 1.0 / (F * D), QUANT_MIN, ALU.mult, ALU.max))
                dve.reciprocal(wscale[:], wmean[:]).then_inc(s_wscale, 1)

            def weight_clip(n, w):
                dve.wait_ge(s_wround, n + 1)
                dve.tensor_scalar(w, w, MAGIC - 1.0, MAGIC + 1.0, ALU.max, ALU.min).then_inc(s_wclip, 1)

            def stats(y, bn, mv, ready):
                for j in range(TB):
                    n = mark(dve.bn_stats(bn[:, j, :], y[:, j * D:(j + 1) * D]))
                dve.wait_ge(s_dve, n)
                for j in range(TB):
                    ins = dve.bn_aggr(mv[:, j, :], bn[:, j, :])
                ins.then_inc(ready, 1)

            def norm(x_, y, o, mv, rs, ga, be):
                for j in range(TB):
                    n = mark(dve.scalar_tensor_tensor(y[:, j, :], x_[:, j * D:(j + 1) * D], mv[:, j, 0:1], ga[:],
                                                      ALU.subtract, ALU.mult))
                dve.wait_ge(s_dve, n)
                for j in range(TB):
                    ins = dve.scalar_tensor_tensor(o[:, j, :], y[:, j, :], rs[:, j:j + 1], be[:], ALU.mult, ALU.add)
                return ins

            def scales(q, w_mean, signal):
                link(dve.tensor_scalar(q[:, 3, :], q[:, 0, :], QUANT_MIN, 1.0 / QMAX, ALU.max, ALU.mult))
                dve.tensor_scalar(q[:, 2, :], q[:, 3, :], w_mean, None, ALU.mult)
                dve.reciprocal(q[:, 1, :], q[:, 3, :]).then_inc(signal, 1)

            def adapter0_stats(b):
                dve.wait_ge(s_ya, b + 1)
                if b:
                    dve.wait_ge(s_rsa, b)
                stats(p_a, bn_a, mv_a, s_mva)

            def adapter0_norm(b):
                dve.wait_ge(s_rsa, b + 1)
                if b:
                    dve.wait_ge(s_za, TB * b)
                    dve.wait_ge(s_rbT, b)
                link(norm(p_a, ya, ya, mv_a, rstd_a, ga0[b % 2], be0[b % 2]))
                link(dve.tensor_reduce(q1[:, 0, :], ya[:], AX_X, ALU.max, apply_absolute_value=True))
                scales(q1, wmean[:, 0:1], s_q1)

            def dequant_pair(b, p):
                m = NP * b + p
                dve.wait_ge(s_h, m + 1)
                if m == 0:
                    dve.wait_ge(s_const, N_CONST)
                if m % NP == 0:
                    dve.wait_ge(s_deq, b + 1)
                if m >= 2 and (m - 2) % NP in PE_PAIRS:
                    dve.wait_ge(s_conv, pe_pairs(m - 2))
                elif m >= 2:
                    dve.wait_ge(s_c0, side_pairs(m - 2))
                    dve.wait_ge(s_tap, side_pairs(m - 2))
                dve.tensor_tensor(gb[m % 2][:, :, 1:S + 1], p_pair[m % 2][:, :].rearrange("p (c t) -> p c t", c=2),
                                  deq_bc[b % 2][:].rearrange("p (a t) -> p a t", a=1).to_broadcast([P, 2, S]),
                                  ALU.mult).then_inc(s_g, 1)

            def conv_sides(b, p):
                m = NP * b + p
                dve.wait_ge(s_c0, side_pairs(m))
                dve.wait_ge(s_g, m + 1)
                marks = []
                for c in range(2):
                    ch = 2 * p + c
                    marks.append(mark(dve.scalar_tensor_tensor(cb[m % 2][:, c, :], gb[m % 2][:, c, 0:S], convs[:, ch, 0:1],
                                                               cb[m % 2][:, c, :], ALU.mult, ALU.add)))
                for c in range(2):
                    ch = 2 * p + c
                    dve.wait_ge(s_dve, marks[c])
                    ins = dve.scalar_tensor_tensor(cb[m % 2][:, c, :], gb[m % 2][:, c, 2:S + 2], convs[:, ch, 2:3],
                                                   cb[m % 2][:, c, :], ALU.mult, ALU.add)
                ins.then_inc(s_tap, 1)

            def hidden_scales(b, j):
                q = q2[:, :, j:j + 1]
                dve.wait_ge(s_sT, TB * b + j + 1)
                if b:
                    dve.wait_ge(s_zb, TB * (b - 1) + j + 1)
                link(dve.tensor_reduce(q[:, 0, :], p_tok[:, j * F:(j + 1) * F], AX_X, ALU.max, apply_absolute_value=True))
                scales(q, wmean[:, 1:2], s_q2)

            def hidden_residual(b, j):
                dve.wait_ge(s_y2, TB * b + j + 1)
                t = TB * b + j
                dve.scalar_tensor_tensor(xs[:, t, :], p_tok[:, j * F:j * F + D], q2[:, 2, j:j + 1],
                                         xs[:, t, :], ALU.mult, ALU.add).then_inc(s_x1, 1)

            def adapter1_stats(b):
                dve.wait_ge(s_yk, b + 1)
                if b:
                    dve.wait_ge(s_rsc, b)
                stats(p_c, bn_c, mv_c, s_mvc)

            def adapter1_norm(b):
                dve.wait_ge(s_rsc, b + 1)
                if b:
                    dve.wait_ge(s_xfT, b)
                    dve.wait_ge(s_rows, TB * b)
                norm(p_c, yk, xf, mv_c, rstd_c, ga1[b % 2], be1[b % 2]).then_inc(s_xf, 1)

            def keep_logits(b):
                dve.wait_ge(s_lgp, b + 1)
                dve.tensor_copy(lg[:, TB * b:TB * b + TB, :].rearrange("p t e -> p (t e)"),
                                p_c[:, 0:TB * E]).then_inc(s_lg, 1)

            routed = (score, choice, g_sum, g_gt, g_ge, g_first, g_rank, g_mask, g_pen, masked, top8, idx8,
                      onehot, picked, wk, wsum)

            def choose(h):
                lo, hi = tiles_of(h)
                n_t = hi - lo
                (score_, choice_, g_sum_, g_gt_, g_ge_, g_first_, g_rank_, g_mask_, g_pen_, masked_, top8_, idx8_,
                 onehot_, picked_, wk_, wsum_) = (a[:, 0:n_t] for a in routed)
                n_g = n_t * GROUPS
                dve.wait_ge(s_score, h + 1)
                if h == 0:
                    dve.wait_ge(s_iota, 4)
                    dve.wait_ge(s_small, 32)
                link(dve.tensor_tensor(choice_, score_, rbias[:].rearrange("p (a e) -> p a e", a=1).to_broadcast([P, n_t, E]), ALU.add))
                four = choice_.rearrange("p t (g a b) -> p (t g) a b", g=GROUPS, a=2)
                dve.tensor_tensor(g_hi[:, 0:n_g], four[:, :, :, 0], four[:, :, :, 1], ALU.max)
                link(dve.tensor_tensor(g_two[:, 0:n_g], four[:, :, :, 0], four[:, :, :, 1], ALU.add))
                dve.tensor_tensor(g_t[:, 0, 0:n_g], g_hi[:, 0:n_g, 0], g_hi[:, 0:n_g, 1], ALU.add)
                link(dve.tensor_tensor(g_t[:, 1, 0:n_g], g_two[:, 0:n_g, 0], g_two[:, 0:n_g, 1], ALU.max))
                link(dve.tensor_tensor(g_sum_.rearrange("p t g -> p (t g)"), g_t[:, 0, 0:n_g], g_t[:, 1, 0:n_g], ALU.max))
                mine = g_sum_.rearrange("p t (g a) -> p t g a", a=1).to_broadcast([P, n_t, GROUPS, GROUPS])
                theirs = g_sum_.rearrange("p t (a g) -> p t a g", a=1).to_broadcast([P, n_t, GROUPS, GROUPS])
                dve.tensor_tensor(g_gt_, theirs, mine, ALU.is_gt)
                link(dve.tensor_tensor(g_ge_, theirs, mine, ALU.is_ge))
                link(dve.tensor_tensor(g_ge_, g_ge_, g_first_, ALU.mult))
                link(dve.tensor_tensor(g_ge_, g_ge_, g_gt_, ALU.max))
                link(dve.tensor_reduce(g_rank_, g_ge_, AX_X, ALU.add))
                dve.tensor_scalar(g_mask_, g_rank_, float(GROUPS_KEPT), None, ALU.is_lt)
                link(dve.tensor_scalar(g_pen_, g_rank_, float(GROUPS_KEPT), NEG_INF, ALU.is_ge, ALU.mult))
                per = E // GROUPS

                def wide(a):
                    return a.rearrange("p t (g a) -> p (t g) a", a=1).to_broadcast([P, n_g, per])

                flat = masked_.rearrange("p t (g a) -> p (t g) a", g=GROUPS)
                link(dve.tensor_tensor(flat, choice_.rearrange("p t (g a) -> p (t g) a", g=GROUPS), wide(g_mask_), ALU.mult))
                link(dve.tensor_tensor(flat, flat, wide(g_pen_), ALU.add))
                for t in range(n_t):
                    n = mark(dve.max(top8[:, t, :], masked[:, t, :]))
                dve.wait_ge(s_dve, n)
                for t in range(n_t):
                    n = mark(dve.max_index(idx8[:, t, :], top8[:, t, :], masked[:, t, :]))
                dve.wait_ge(s_dve, n)
                link(dve.tensor_tensor(onehot_, iota_e[:].rearrange("p (a b e) -> p a b e", a=1, b=1).to_broadcast([P, n_t, TOP_K, E]),
                                       idx8_[:, :, 0:TOP_K].rearrange("p t (k a) -> p t k a", a=1).to_broadcast([P, n_t, TOP_K, E]), ALU.is_equal))
                with nc.allow_low_precision(reason="a sum that is 0 or 1 is exact in bfloat16"):
                    dve.tensor_reduce(mask_b[:, lo:hi, :], onehot_.rearrange("p t k e -> p t e k"), AX_X, ALU.add).then_inc(s_mask, 1)
                link(dve.tensor_tensor(picked_, onehot_, score_.rearrange("p t (a e) -> p t a e", a=1).to_broadcast([P, n_t, TOP_K, E]), ALU.mult))
                link(dve.tensor_reduce(wk_, picked_, AX_X, ALU.add))
                link(dve.tensor_reduce(wsum_, wk_, AX_X, ALU.add))
                link(dve.tensor_scalar(wsum_, wsum_, 1e-20, None, ALU.add))
                link(dve.reciprocal(wsum_, wsum_))
                dve.scalar_tensor_tensor(wk_, wk_, ROUTED_SCALE, wsum_.rearrange("p (t a) -> p t a", a=1).to_broadcast(
                    [P, n_t, TOP_K]), ALU.mult, ALU.mult).then_inc(s_route, 1)

            def destinations(h):
                lo, hi = tiles_of(h)
                n_t = hi - lo
                onehot_, picked_, pos_, dest_ = (a[:, 0:n_t] for a in (onehot, picked, pos, dest_f))
                dve.wait_ge(s_route, h + 1)
                for t in range(lo, hi):
                    if t >= RT:
                        dve.wait_ge(s_sent[t % RT], t // RT * TOP_K * 16)
                for t in range(lo, hi):
                    if t == lo or t % RT == 0:
                        to = min(hi, (t // RT + 1) * RT)
                        r = slice(t % RT, t % RT + to - t)
                        mark(dve.tensor_copy(rows[:, r, :, D + 1], wk[:, t - lo:to - lo, :]))
                        mark(dve.tensor_copy(rows[:, r, :, D].bitcast(I32), slot_id[:, t:to, :]))
                dve.wait_ge(s_pre, h + 1)
                if hi == NT:
                    expert_counts()
                link(dve.tensor_tensor(pos_, p_tok[:, 0:n_t * E].rearrange("p (t e) -> p t e", t=n_t),
                                       iota_region[:].rearrange("p (a e) -> p a e", a=1).to_broadcast([P, n_t, E]), ALU.add))
                link(dve.tensor_tensor(picked_, onehot_, pos_.rearrange("p t (a e) -> p t a e", a=1).to_broadcast(
                    [P, n_t, TOP_K, E]), ALU.mult))
                link(dve.tensor_reduce(dest_, picked_, AX_X, ALU.add))
                dve.tensor_copy(dest[:, lo:hi, :], dest_).then_inc(s_dest, 1)

            def expert_counts():
                lo, hi = tiles_of(-1)
                mark(dve.tensor_copy(cnt[:, 0, :], p_tok[0:1, (hi - lo) * E:(hi - lo) * E + E]))
                dve.tensor_copy(cnt_i[:], p_tok[0:1, (hi - lo) * E:(hi - lo) * E + E]).then_inc(s_cnt, 1)

            def tile_list():
                link(dve.tensor_scalar(cnt[:, 1, :], cnt[:, 0, :], 1.0 / P, 0.5 - 0.5 / P, ALU.mult, ALU.add))
                link(dve.tensor_scalar(cnt[:, 1, :], cnt[:, 1, :], MAGIC, None, ALU.add))
                link(dve.tensor_scalar(cnt[:, 1, :], cnt[:, 1, :], MAGIC, None, ALU.subtract))
                dve.tensor_scalar(cnt[:, 3, :], cnt[:, 1, :], -float(P), float(REGION), ALU.mult, ALU.add)
                link(dve.tensor_tensor_scan(cnt[:, 2, :], cnt[:, 1, :], zrow[:], 0.0, ALU.add, ALU.add))
                full = [1, TILES, E]
                link(dve.tensor_tensor(t_mask, tj[:].rearrange("p (t a) -> p t a", a=1).to_broadcast(full),
                                       cnt[:, 2:3, :].to_broadcast(full), ALU.is_ge))
                link(dve.tensor_reduce(t_f[:, 0, :], t_mask, AX_X, ALU.add))
                link(dve.tensor_scalar(t_exp[:, 2:2 + TILES], t_f[:, 0, :], float(E - 1), None, ALU.min))
                for w in range(WORDS):
                    digits = t_exp[:, w * DIGITS:w * DIGITS + TILES].rearrange("a (g r) -> a g r", r=RING)[:, :, 0:DIGITS]
                    n = mark(dve.tensor_tensor(t_digit[:, :, w, :], digits, t_place[:], ALU.mult))
                dve.wait_ge(s_dve, n)
                link(dve.tensor_reduce(t_sum[:], t_digit[:], AX_X, ALU.add))
                link(dve.tensor_tensor(t_prod, t_mask, cnt[:, 3:4, :].to_broadcast(full), ALU.mult))
                link(dve.tensor_reduce(t_f[:, 1, :], t_prod, AX_X, ALU.add))
                link(dve.scalar_tensor_tensor(t_f[:, 1, :], tj[:], float(P), t_f[:, 1, :], ALU.mult, ALU.add))
                link(dve.tensor_scalar(t_f[:, 1, :], t_f[:, 1, :], float(E * REGION), None, ALU.min))
                link(dve.tensor_copy(t_word[:], t_sum[:].rearrange("a g w -> a (g w)")))
                dve.tensor_copy(t_row[:], t_f[:, 1, :]).then_inc(s_table, 1)

            for i in range(NB + 5):
                run(dequant_pair, i - 2, 3)
                run_group(choose, i - 5)
                run(adapter1_stats, i - 4)
                run(conv_sides, i - 2, 2)
                if i == 0:
                    weight_sums()
                run(adapter0_stats, i)
                if i == 0:
                    weight_means()
                run(hidden_residual, i - 3, 0)
                run(adapter1_norm, i - 4)
                run(dequant_pair, i - 1, 0)
                run_group(destinations, i - 5)
                run(adapter0_norm, i)
                if i == 0:
                    weight_clip(0, w1f)
                    weight_clip(1, w2f)
                run(hidden_residual, i - 3, 1)
                run(dequant_pair, i - 1, 1)
                run(conv_sides, i - 1, 0)
                run(keep_logits, i - 4)
                run(hidden_scales, i - 2, 0)
                run(dequant_pair, i - 1, 2)
                run(conv_sides, i - 1, 1)
                run(hidden_scales, i - 2, 1)
            tile_list()

            def hidden(n, u):
                dve.wait_ge(e_sg, n + 1)
                dve.wait_ge(s_xr[u], 16 * (n // RING + 1) if isinstance(n, int) else (n - u) * (16 // RING) + 16)
                if not (isinstance(n, int) and n < 2):
                    dve.wait_ge(e_hT, n - 1)
                dve.scalar_tensor_tensor(he[u % 2], sg[u % 2], xr[u][:, D + 1:D + 2],
                                         p_tok[:, u % 2 * 512 + HI:u % 2 * 512 + 2 * HI], ALU.mult, ALU.mult).then_inc(e_h, 1)
                if not (isinstance(n, int) and n < RING):
                    dve.wait_ge(s_back[u], 16 * (n // RING) if isinstance(n, int) else (n - u) * (16 // RING))
                dve.tensor_copy(home[:, u:u + 1], xr[u][:, D:D + 1].bitcast(I32)).then_inc(e_home, 1)

            def hidden_copy(n, u):
                dve.wait_ge(e_hT, n + 1)
                if not (isinstance(n, int) and n < 2):
                    dve.wait_ge(e_y, n - 1)
                dve.tensor_copy(hTe[u % 2], (p_a, p_c)[u % 2][:, 0:P]).then_inc(e_hTc, 1)

            def out_copy(n, u):
                dve.wait_ge(e_y, n + 1)
                dve.tensor_copy(yr[u], p_tok[:, 1024 + u % 2 * 512:1024 + u % 2 * 512 + D]).then_inc(e_yc, 1)

            def step(n, u):
                if not (isinstance(n, int) and n >= TILES):
                    hidden(n, u)
                if not (isinstance(n, int) and (n < 1 or n > TILES)):
                    hidden_copy(n - 1, (u - 1) % RING)
                if not (isinstance(n, int) and n < 2):
                    out_copy(n - 2, (u - 2) % RING)

            for n in range(2 * RING):
                step(n, n % RING)
            with dve.Fori(2, TILES // RING) as i:
                for u in range(RING):
                    step(i * RING + u, u)
            for n in range(TILES, TILES + 2):
                step(n, n % RING)

            for t in range(NT):
                dve.wait_ge(s_slots[t % 4], 16 * (t // 4 + 1))
                sl = slots[t % 4][:, 0]
                link(dve.tensor_tensor(sl[:, 0:2, :], sl[:, 0:2, :], sl[:, 2:4, :], ALU.add))
                link(dve.tensor_tensor(sl[:, 0, :], sl[:, 0, :], sl[:, 1, :], ALU.add))
                dve.tensor_tensor(xs[:, t, :], xs[:, t, :], sl[:, 0, :], ALU.add).then_inc(s_sum, 1)


def kernel(**inputs):
    import numpy as _np
    import concourse.bacc as _bacc
    from concourse import mybir as _mybir
    from concourse.bass_utils import run_bass_kernel_spmd as _run

    i = {k: _np.asarray(v) for k, v in inputs.items()}
    F, D = i["L0_ffn_w1"].shape
    conv = _np.concatenate([i["L0_ffn_conv_w"][:, 0, :], i["L0_ffn_conv_b"][:, None]], axis=1)
    E = i["L1_ffn_w_gate"].shape[0]
    NB, S, _ = i["x"].shape
    arrays = {
        "x": i["x"],
        "xT": i["x"].reshape(NB * S, D).T,
        "id0": i["itok_B_0_8"][None, :],
        "id1": i["itok_B_0_6"][None, :],
        "l0_w1": i["L0_cond_W1"],
        "l0_b1": i["L0_cond_b1"],
        "l0_w2b2": _np.concatenate([i["L0_cond_W2"], i["L0_cond_b2"][:, None, :]], axis=1),
        "l0_gamma": i["L0_cond_gamma"],
        "l0_beta": i["L0_cond_beta"],
        "w1T": i["L0_ffn_w1"].T,
        "conv": conv.reshape(F // 128, 128, 4).transpose(1, 0, 2),
        "w2T": i["L0_ffn_w2"].T,
        "l1_down": i["L1_cond_down_w"],
        "l1_down_b": i["L1_cond_down_b"],
        "l1_up": i["L1_cond_up_w"],
        "l1_up_b": i["L1_cond_up_b"],
        "l1_gamma": i["L1_cond_ln_g"],
        "l1_beta": i["L1_cond_ln_b"],
        "routerT": i["L1_ffn_router_weight"].T,
        "router_bias": i["L1_ffn_router_bias"],
        "gate_upT": _np.concatenate([i["L1_ffn_w_gate"].transpose(0, 2, 1), i["L1_ffn_w_up"].transpose(0, 2, 1)], axis=2),
        "downT": i["L1_ffn_w_down"].transpose(2, 0, 1),
    }
    arrays = {f"in_{k}": _np.ascontiguousarray(v) for k, v in arrays.items()}
    nc = _bacc.Bacc("TRN2", target_bir_lowering=False, num_devices=1)
    f32 = _mybir.dt.float32
    args = [nc.dram_tensor(k, v.shape, _mybir.dt.from_np(v.dtype), kind="ExternalInput").ap() for k, v in arrays.items()]
    args.append(nc.dram_tensor("out_0", i["x"].shape, f32, kind="ExternalOutput").ap())
    args.append(nc.dram_tensor("sent", (E * (NB * S + 128) + 128, D + 2), f32, kind="Internal").ap())
    args.append(nc.dram_tensor("done", (4 * NB * S, D), f32, kind="Internal").ap())
    build(nc, *args)
    r = _run(nc, [arrays], core_ids=[0])
    return r.results[0]["out_0"]
```
